# Optimizing a Trainium2 kernel written in Bass

```python
import numpy as np
import jax
import jax.numpy as jnp

def _softmax(x, axis=-1):
    return jax.nn.softmax(x, axis=axis)

def _gelu(x):
    return jax.nn.gelu(x, approximate=True)

def _silu(x):
    return jax.nn.silu(x)

def _sigmoid(x):
    return jax.nn.sigmoid(x)

def _layernorm(x, axis=-1, eps=1e-05):
    m = jnp.mean(x, axis=axis, keepdims=True)
    v = jnp.var(x, axis=axis, keepdims=True)
    return (x - m) / jnp.sqrt(v + eps)

def _scatter_add(tgt, idx, src, axis=0):
    return tgt.at[idx].add(src)

def _segment_sum(src, seg, n):
    return jax.ops.segment_sum(src, seg, n)
kernel_name = 'mk_gps_d1_gnn_r8_d5b3b2'

def setup_inputs(seed: int=0):
    np.random.seed(seed)
    _w = jnp.asarray

    def _rec_inputs():
        import jax
        import jax.numpy as jnp
        _gk = jax.random.key(seed)
        x = -8.776e-05 + 1 * jax.random.normal(jax.random.fold_in(_gk, 1), (1250, 512), jnp.float32)
        _s = jax.random.randint(jax.random.fold_in(_gk, 2), (10000,), 0, 1250, jnp.int32)
        _d = jax.random.randint(jax.random.fold_in(_gk, 3), (10000,), 0, 1250, jnp.int32)
        _loop = jnp.arange(1250, dtype=jnp.int32)
        src = jnp.concatenate([_s, _d, _loop])
        dst = jnp.concatenate([_d, _s, _loop])
        _o = jnp.argsort(dst, stable=True)
        src = src[_o]
        dst = dst[_o]
        return (x, src, dst)
    x, src, dst = _rec_inputs()

    def _L0_gnn_setup():
        import jax, jax.numpy as jnp
        import numpy as np
        N_NODES = 1250
        N_EDGES = 20000
        D = 512
        key = jax.random.key(seed)
        k_h, k_e, k_w1, k_w2 = jax.random.split(key, 4)
        h = jax.random.normal(k_h, (N_NODES, D), dtype=jnp.float32)
        edge_index = jax.random.randint(k_e, (2, N_EDGES), 0, N_NODES, dtype=jnp.int64)
        scale = 1.0 / np.sqrt(D)
        W1 = jax.random.normal(k_w1, (D, D), dtype=jnp.float32) * scale
        b1 = jnp.zeros((D,), dtype=jnp.float32)
        W2 = jax.random.normal(k_w2, (D, D), dtype=jnp.float32) * scale
        b2 = jnp.zeros((D,), dtype=jnp.float32)
        return {'h': h, 'edge_index': edge_index, 'W1': W1, 'b1': b1, 'W2': W2, 'b2': b2}
    _L0_gnn_all = _L0_gnn_setup()
    _L0_gnn_in = {k: v for k, v in _L0_gnn_all.items() if k in ('W1', 'b1', 'W2', 'b2')}
    del _L0_gnn_all

    def _L0_mix_setup():
        import jax, jax.numpy as jnp
        import numpy as np
        BATCH, SEQ, D_MODEL = (16, 392, 512)
        M = 256

        def _ln(x, g, b, eps=1e-05):
            mu = jnp.mean(x, axis=-1, keepdims=True)
            var = jnp.mean(jnp.square(x - mu), axis=-1, keepdims=True)
            return (x - mu) / jnp.sqrt(var + eps) * g + b

        def _prm_exp(x, w):
            m = w.shape[0]
            xd = jnp.sum(x * x, axis=-1, keepdims=True) / 2.0
            wtd = jnp.einsum('btd,md->btm', x, w)
            return jnp.exp(wtd - xd) / np.sqrt(m).astype(np.float32)
        key = jax.random.key(seed)
        ks = jax.random.split(key, 8)
        d, m = (D_MODEL, M)
        x = jax.random.normal(ks[0], (BATCH, SEQ, d), dtype=jnp.float32)
        q_mat, _ = jnp.linalg.qr(jax.random.normal(ks[1], (d, m), dtype=jnp.float32))
        w = q_mat.T * np.sqrt(m).astype(np.float32)
        Wkqv = jax.random.normal(ks[2], (d, 3 * d), dtype=jnp.float32) * 0.02
        bkqv = jnp.zeros((3 * d,), jnp.float32)
        Wo = jax.random.normal(ks[3], (d, d), dtype=jnp.float32) * 0.02
        bo = jnp.zeros((d,), jnp.float32)
        W1 = jax.random.normal(ks[4], (d, d), dtype=jnp.float32) * 0.02
        b1 = jnp.zeros((d,), jnp.float32)
        W2 = jax.random.normal(ks[5], (d, d), dtype=jnp.float32) * 0.02
        b2 = jnp.zeros((d,), jnp.float32)
        g1 = jnp.ones((d,), jnp.float32)
        be1 = jnp.zeros((d,), jnp.float32)
        g2 = jnp.ones((d,), jnp.float32)
        be2 = jnp.zeros((d,), jnp.float32)
        return dict(x=x, w=w, Wkqv=Wkqv, bkqv=bkqv, Wo=Wo, bo=bo, W1=W1, b1=b1, W2=W2, b2=b2, g1=g1, be1=be1, g2=g2, be2=be2)
    _L0_mix_all = _L0_mix_setup()
    _L0_mix_in = {k: v for k, v in _L0_mix_all.items() if k in ('w', 'Wkqv', 'bkqv', 'Wo', 'bo', 'W1', 'b1', 'W2', 'b2', 'g1', 'be1', 'g2', 'be2')}
    del _L0_mix_all

    def _L0_ffn_setup():
        import jax, jax.numpy as jnp
        import numpy as np
        TOP_K = 2

        def quick_gelu(x):
            return x * jax.nn.sigmoid(1.702 * x)
        key = jax.random.key(seed)
        ks = jax.random.split(key, 6)
        B, S, H, I, E = (8, 512, 512, 1024, 8)
        s_h = 1.0 / np.sqrt(H).astype(np.float32)
        s_i = 1.0 / np.sqrt(I).astype(np.float32)
        return {'hidden_states': jax.random.normal(ks[0], (B, S, H), jnp.float32), 'router_w': jax.random.normal(ks[1], (H, E), jnp.float32) * s_h, 'router_b': jnp.zeros((E,), jnp.float32), 'gate_up_proj': jax.random.normal(ks[2], (E, H, 2 * I), jnp.float32) * s_h, 'gate_up_proj_bias': jnp.zeros((E, 2 * I), jnp.float32), 'down_proj': jax.random.normal(ks[3], (E, I, H), jnp.float32) * s_i, 'down_proj_bias': jnp.zeros((E, H), jnp.float32)}
    _L0_ffn_all = _L0_ffn_setup()
    _L0_ffn_in = {k: v for k, v in _L0_ffn_all.items() if k in ('router_w', 'router_b', 'gate_up_proj', 'gate_up_proj_bias', 'down_proj', 'down_proj_bias')}
    del _L0_ffn_all
    return {'x': x, 'src': src, 'dst': dst, 'L0_gnn_W1': _L0_gnn_in['W1'], 'L0_gnn_b1': _L0_gnn_in['b1'], 'L0_gnn_W2': _L0_gnn_in['W2'], 'L0_gnn_b2': _L0_gnn_in['b2'], 'L0_mix_w': _L0_mix_in['w'], 'L0_mix_Wkqv': _L0_mix_in['Wkqv'], 'L0_mix_bkqv': _L0_mix_in['bkqv'], 'L0_mix_Wo': _L0_mix_in['Wo'], 'L0_mix_bo': _L0_mix_in['bo'], 'L0_mix_W1': _L0_mix_in['W1'], 'L0_mix_b1': _L0_mix_in['b1'], 'L0_mix_W2': _L0_mix_in['W2'], 'L0_mix_b2': _L0_mix_in['b2'], 'L0_mix_g1': _L0_mix_in['g1'], 'L0_mix_be1': _L0_mix_in['be1'], 'L0_mix_g2': _L0_mix_in['g2'], 'L0_mix_be2': _L0_mix_in['be2'], 'L0_ffn_router_w': _L0_ffn_in['router_w'], 'L0_ffn_router_b': _L0_ffn_in['router_b'], 'L0_ffn_gate_up_proj': _L0_ffn_in['gate_up_proj'], 'L0_ffn_gate_up_proj_bias': _L0_ffn_in['gate_up_proj_bias'], 'L0_ffn_down_proj': _L0_ffn_in['down_proj'], 'L0_ffn_down_proj_bias': _L0_ffn_in['down_proj_bias']}

def reference(x, src, dst, L0_gnn_W1, L0_gnn_b1, L0_gnn_W2, L0_gnn_b2, L0_mix_w, L0_mix_Wkqv, L0_mix_bkqv, L0_mix_Wo, L0_mix_bo, L0_mix_W1, L0_mix_b1, L0_mix_W2, L0_mix_b2, L0_mix_g1, L0_mix_be1, L0_mix_g2, L0_mix_be2, L0_ffn_router_w, L0_ffn_router_b, L0_ffn_gate_up_proj, L0_ffn_gate_up_proj_bias, L0_ffn_down_proj, L0_ffn_down_proj_bias):
    import jax
    import jax.numpy as jnp

    def _L0_gnn_ref(h, edge_index, W1, b1, W2, b2):
        import jax, jax.numpy as jnp
        import numpy as np
        N_NODES = 1250
        N_EDGES = 20000
        D = 512
        send, rec = (edge_index[0], edge_index[1])
        agg = jax.ops.segment_sum(h[send], rec, num_segments=h.shape[0])
        x = h + agg
        x = jax.nn.relu(x @ W1 + b1)
        x = x @ W2 + b2
        return x

    def _L0_mix_ref(x, w, Wkqv, bkqv, Wo, bo, W1, b1, W2, b2, g1, be1, g2, be2):
        import jax, jax.numpy as jnp
        import numpy as np
        BATCH, SEQ, D_MODEL = (16, 392, 512)
        M = 256

        def _ln(x, g, b, eps=1e-05):
            mu = jnp.mean(x, axis=-1, keepdims=True)
            var = jnp.mean(jnp.square(x - mu), axis=-1, keepdims=True)
            return (x - mu) / jnp.sqrt(var + eps) * g + b

        def _prm_exp(x, w):
            m = w.shape[0]
            xd = jnp.sum(x * x, axis=-1, keepdims=True) / 2.0
            wtd = jnp.einsum('btd,md->btm', x, w)
            return jnp.exp(wtd - xd) / np.sqrt(m).astype(np.float32)
        eps = 1e-08
        xn = _ln(x, g1, be1)
        kqv = xn @ Wkqv + bkqv
        k, q, v = jnp.split(kqv, 3, axis=-1)
        kp = _prm_exp(k, w)
        qp = _prm_exp(q, w)
        D = jnp.einsum('btm,bm->bt', qp, jnp.sum(kp, axis=1))[..., None]
        kptv = jnp.einsum('btn,btm->bnm', v, kp)
        y = jnp.einsum('btm,bnm->btn', qp, kptv) / (D + eps)
        y = v + (y @ Wo + bo)
        h = _ln(y, g2, be2)
        h = jax.nn.gelu(h @ W1 + b1, approximate=False) @ W2 + b2
        return y + h

    def _L0_ffn_ref(hidden_states, router_w, router_b, gate_up_proj, gate_up_proj_bias, down_proj, down_proj_bias):
        import jax, jax.numpy as jnp
        import numpy as np
        TOP_K = 2

        def quick_gelu(x):
            return x * jax.nn.sigmoid(1.702 * x)
        B, S, H = hidden_states.shape
        E = router_b.shape[0]
        x = hidden_states.reshape(-1, H)
        T = x.shape[0]
        logits = x @ router_w + router_b
        top_w, sel = jax.lax.top_k(logits, TOP_K)
        top_w = jax.nn.softmax(top_w, axis=-1)
        tok_w = jnp.zeros((T, E), x.dtype).at[jnp.arange(T)[:, None], sel].add(top_w)

        def body(acc, params):
            Wgu, bgu, Wd, bd, w_e = params
            gu = x @ Wgu + bgu
            gate, up = jnp.split(gu, 2, axis=-1)
            act = (up + 1.0) * quick_gelu(gate)
            out = act @ Wd + bd
            return (acc + out * w_e[:, None], None)
        acc0 = jnp.zeros((T, H), x.dtype)
        acc, _ = jax.lax.scan(body, acc0, (gate_up_proj, gate_up_proj_bias, down_proj, down_proj_bias, tok_w.T))
        return acc.reshape(B, S, H)
    edge_index = jnp.stack([src, dst])
    xn = _layernorm(x, axis=-1)
    x = x + _L0_gnn_ref(xn, edge_index, L0_gnn_W1, L0_gnn_b1, L0_gnn_W2, L0_gnn_b2) + _L0_mix_ref(xn[None], L0_mix_w, L0_mix_Wkqv, L0_mix_bkqv, L0_mix_Wo, L0_mix_bo, L0_mix_W1, L0_mix_b1, L0_mix_W2, L0_mix_b2, L0_mix_g1, L0_mix_be1, L0_mix_g2, L0_mix_be2)[0]
    x = x + _L0_ffn_ref(_layernorm(x, axis=-1)[None], L0_ffn_router_w, L0_ffn_router_b, L0_ffn_gate_up_proj, L0_ffn_gate_up_proj_bias, L0_ffn_down_proj, L0_ffn_down_proj_bias)[0]
    return x

_drawn_inputs = setup_inputs


def setup_inputs(seed=0):
    import zlib

    import numpy as np

    out = dict(_drawn_inputs(seed))
    spreads = {'L0_gnn_b1': (0.0, 0.1),
     'L0_gnn_b2': (0.0, 0.1),
     'L0_mix_bkqv': (0.0, 0.1),
     'L0_mix_bo': (0.0, 0.1),
     'L0_mix_b1': (0.0, 0.463),
     'L0_mix_b2': (0.0, 0.1),
     'L0_mix_g1': (1.0, 0.2),
     'L0_mix_be1': (0.0, 0.349),
     'L0_mix_g2': (1.0, 0.6),
     'L0_mix_be2': (0.0, 0.574),
     'L0_ffn_router_b': (0.0, 0.1),
     'L0_ffn_gate_up_proj_bias': (0.0, 0.308),
     'L0_ffn_down_proj_bias': (0.0, 0.37)}
    factors = {}
    for name, (base, spread) in spreads.items():
        noise = np.random.default_rng([zlib.crc32(name.encode()), seed]).standard_normal(out[name].shape)
        drawn = base * np.exp(spread * noise) if base else spread * noise
        out[name] = jnp.asarray(drawn.astype(out[name].dtype))
    for name, factor in factors.items():
        out[name] = (out[name] * factor).astype(out[name].dtype)
    return out
```

```python
from contextlib import ExitStack

import concourse.bass as bass
from concourse import mybir

ALU = mybir.AluOpType
ACT = mybir.ActivationFunctionType
AX_X = mybir.AxisListType.X
F32 = mybir.dt.float32
BF16 = mybir.dt.bfloat16
I32 = mybir.dt.int32
U32 = mybir.dt.uint32
I16 = mybir.dt.int16
P = 128
BANK = 512
EPS = 1e-5
ATT_EPS = 1e-8


def bass_gps_gnn_performer_moe(nc, x, src, dst, gw1, gb1, gw2, gb2, w, wkqv, bkqv, wo, bo, w1, b1, w2, b2,
                               g1, be1, g2, be2, rw, rb, wgu, bgu, wd, bd, out):
    N, D = x.shape
    E = src.shape[0]
    M = w.shape[0]
    NX = rw.shape[1]
    I = wd.shape[1]
    TOP = 2
    NT = -(-N // P)
    KD = D // P
    KM = M // P
    KI = I // P
    LAST = N - (NT - 1) * P
    ET = -(-E // P)
    EFULL = E // P
    EREST = E - EFULL * P
    NOWHERE = 2047
    SLOTS = (TOP * N + NX * (P - 1)) // P
    RING = 4
    assert D == BANK and EREST and ET <= 2 * P and M % P == 0

    def rows(t):
        return P if t < NT - 1 else LAST

    COLS = [(a, min(BANK, N - a)) for a in range(0, N, BANK)]
    NC = len(COLS)
    TPC = BANK // P

    a_n = 0

    def a_stage(n):
        nonlocal a_n
        a_n += n
        return a_n - n
    A_VEC = a_stage(1)
    A_WT = a_stage(KM)
    A_XMT = a_stage(KD * NC)
    A_Z = a_stage(KD * NC)
    A_R = a_stage(KD * NC)
    A_KQ = a_stage(2 * KD * NC)
    A_KP = a_stage(NT)
    A_QP = a_stage(NT)
    A_QPT = a_stage(KM * NC)
    A_KPTV = a_stage(KM)
    A_ATT = a_stage(KD * NC)
    A_H = a_stage(KD * NC)
    A_G = a_stage(KD * NC)
    A_X2T = a_stage(NT)
    A_END = a_n
    D_EDGE, D_RANGE, D_XDK, D_V = 0, 1, 2, 3
    D_XDQ = D_V + NT
    D_KSUM = D_XDQ + 1
    D_DEN = D_KSUM + 1
    D_Y = D_DEN + 1
    d_last = D_Y + NT
    D_X1, D_LOG = {}, {}
    for t in range(NT + 2):
        if t < NT:
            D_X1[t] = d_last
            d_last += 1
        if t >= 2:
            D_LOG[t - 2] = d_last
            d_last += 1
    D_RANK = d_last
    D_SLOT = D_RANK + 1

    with ExitStack() as ctx:
        def sb(name, shape, dt=F32):
            return ctx.enter_context(nc.sbuf_tensor(name, shape, dt))

        def sem(name):
            return ctx.enter_context(nc.semaphore(name))

        xr = sb("x_rows", [P, NT, D])
        r1 = sb("r1", [P, NT * D])
        HALF = 2 * KD * N + NT * M
        EXW = KD * 2 * I + KI * D
        assert EXW <= HALF and NT * N <= HALF
        B2, B4 = HALF, HALF + KD * N
        B5 = B4 + 2 * NT * M
        arena = sb("arena", [P, B5 + NT * D])
        assert HALF + EXW <= B5 + NT * D
        wa = sb("weights", [P, 5 * KD * D + KD * M])

        def t3(ap, n):
            return ap.rearrange("p (a b) -> p a b", a=n)

        xn = t3(r1[:, :], NT)
        v = xn
        cT = t3(arena[:, 0:NT * N], NT)
        kT = t3(arena[:, 0:KD * N], KD)
        qT = t3(arena[:, KD * N:2 * KD * N], KD)
        kp = t3(arena[:, 2 * KD * N:HALF], NT)
        kptvT = t3(arena[:, 0:KM * D], KM)
        yhat = t3(arena[:, 0:NT * D], NT)
        w_raw = t3(arena[:, 0:KM * D], KM)
        o = KM * D
        e_int = arena[:, o:o + 4 * P].bitcast(I32).rearrange("p (a g c) -> p a g c", a=2, g=2)
        o += 4 * P
        e_f = arena[:, o:o + 4 * P].rearrange("p (a g c) -> p a g c", a=2, g=2)
        o += 4 * P
        e_diag = arena[:, o:o + 4 * P].rearrange("p (a g c) -> p a g c", a=2, g=2)
        xmT = t3(arena[:, B2:B2 + KD * N], KD)
        attT = xmT
        gT = xmT
        zT = t3(arena[:, B4:B4 + KD * N], KD)
        sq = zT
        hT = zT
        RW = NT * P + 2 * P
        ring = arena[:, B4:B4 + RING * RW // 2].bitcast(BF16)
        c_stage = arena[:, B4 + RING * RW // 2:B4 + RING * RW // 2 + N]
        assert RING * RW // 2 + N <= 2 * NT * M
        qp = t3(arena[:, B4:B4 + NT * M], NT)
        qpT = t3(arena[:, B4 + NT * M:B4 + NT * M + KM * N], KM)
        x2 = t3(arena[:, B4:B4 + 2 * D], 2)
        x2T = arena[:, B4 + 2 * D:B4 + 4 * D].rearrange("p (b k c) -> p b k c", b=2, k=KD)
        xm = t3(arena[:, B5:B5 + NT * D], NT)
        rT = t3(arena[:, B5:B5 + KD * N], KD)
        WSZ = KD * D
        gw1_s = t3(wa[:, 0:WSZ], KD)
        gw2_s = t3(wa[:, WSZ:2 * WSZ], KD)
        EW = N + (NT - 1) * P
        e_id = wa[:, WSZ:WSZ + EW // 2].bitcast(BF16)
        o = WSZ + EW // 2 + 1
        iota16 = wa[:, o:o + NT * P // 2].bitcast(I16)
        assert o + NT * P // 2 <= 2 * WSZ
        kqv_s = t3(wa[:, 2 * WSZ:5 * WSZ], KD)
        wo_s, w1_s, w2_s = (t3(wa[:, (2 + i) * WSZ:(3 + i) * WSZ], KD) for i in range(3))
        wT = t3(wa[:, 5 * WSZ:5 * WSZ + KD * M], KD)
        bgu_b, bd_b = t3(wa[:, 0:4 * I], 2), t3(wa[:, 4 * I:4 * I + 2 * D], 2)
        o = 4 * I + 2 * D
        g_s, u_s, sig_s, a_s, aT = (wa[:, o + i * I:o + (i + 1) * I] for i in range(5))
        o += 5 * I
        xs, xsT = wa[:, o:o + D], wa[:, o + D:o + 2 * D]
        assert o + 2 * D <= 5 * WSZ + KD * M
        ybuf = t3(r1[:, 0:2 * D], 2)

        ident = sb("ident", [P, P])
        ident_b = sb("ident_b", [P, P], BF16)
        ones = sb("ones", [P, P])
        ones_b = sb("ones_b", [P, P], BF16)
        tri_b = sb("tri_b", [P, P], BF16)
        vrow = sb("vrow", [8 * KD, P])
        vT = sb("vT", [P, 8 * KD])
        V_G1, V_BE1, V_G2, V_BE2, V_GB1, V_B1, V_BK, V_BQ = (KD * i for i in range(8))
        bv_b = sb("bv_b", [P, D])
        bo_b = sb("bo_b", [P, D])
        b2_b = sb("b2_b", [P, D])
        gb2_b = sb("gb2_b", [P, D])
        rb_b = sb("rb_b", [P, NX])
        rw_s = sb("rw_s", [P, KD, NX])
        srcT = sb("srcT", [P, 2 * P])
        dstT = sb("dstT", [P, 2 * P])
        st6 = sb("st6", [P, NT, 6])
        mv = sb("mv", [P, NT, 2])
        ve = sb("ve", [P, NT])
        sd = sb("sd", [P, NT])
        rstd = sb("rstd", [P, NT])
        mm2 = sb("minmax", [P, 4])
        xdn = sb("xdn", [P, 2 * NT])
        ksum = sb("ksum", [P, KM])
        den = sb("den", [P, NT])
        rden = sb("rden", [P, NT])
        piota = sb("piota", [P, 1])
        lo_j = sb("lo_j", [P, 1])
        hi_j = sb("hi_j", [P, 1])
        rng = sb("rng", [P, 4])
        rng_i = sb("rng_i", [P, 2], I32)
        etab = sb("etab", [P, SLOTS], I32)
        cend_i = sb("cend_i", [P, NX], I32)
        pos_i = sb("pos_i", [P, TOP, NT], I32)
        idx_i = sb("idx_i", [P, SLOTS], I32)
        wgt = sb("wgt", [P, TOP, NT])
        logit = sb("logit", [P, NT, NX])
        erow = t3(arena[:, B5:B5 + 5 * 2 * P], 5)
        o = 2 * D

        def r1_take(n):
            nonlocal o
            o += n
            assert o <= NT * D
            return r1[:, o - n:o]
        mx8 = t3(r1_take(NT * NX), NT)
        mi8 = t3(r1_take(NT * NX).bitcast(U32), NT)
        mif = t3(r1_take(NT * NX), NT)
        oh = r1_take(TOP * NT * NX).rearrange("p (k t e) -> p k t e", k=TOP, t=NT)
        prod = r1_take(TOP * NT * NX).rearrange("p (k t e) -> p k t e", k=TOP, t=NT)
        msk_b = r1_take(NT * NX // 2).bitcast(BF16)
        rank = t3(r1_take(NT * NX), NT)
        pre = t3(r1_take((NT + 1) * NX), NT + 1)
        cnt_i = r1_take(NX).bitcast(I32)
        cnt = r1_take(NX)
        cend = r1_take(NX)
        base = r1_take(NX)
        ex2 = t3(r1_take(2 * NT), 2)
        posf = t3(r1_take(TOP * NT), TOP)
        pa_i = t3(r1_take(TOP * NT).bitcast(I32), TOP)
        pb_i = t3(r1_take(TOP * NT).bitcast(I32), TOP)
        pa_f = t3(r1_take(TOP * NT), TOP)
        pb_f = t3(r1_take(TOP * NT), TOP)
        tok = r1_take(NT)
        iota8 = r1_take(NX)
        iota_s = r1_take(SLOTS)
        cmp_s = r1_take(SLOTS * NX).rearrange("p (s e) -> p s e", s=SLOTS)
        e_fl = r1_take(SLOTS)
        slot_b = wa[:, 0:TOP * NT * P].rearrange("p (k t c) -> p k t c", k=TOP, t=NT)
        slot_a = wa[:, TOP * NT * P:TOP * NT * (P + SLOTS)].rearrange("p (k t s) -> p k t s", k=TOP, t=NT)
        iota_c = wa[:, TOP * NT * (P + SLOTS):TOP * NT * (P + SLOTS) + P]
        CB = 4
        yg = arena[:, 0:CB * TOP * D].rearrange("p (b k c) -> p b k c", b=CB, k=TOP)
        ob = t3(arena[:, CB * TOP * D:CB * (TOP + 1) * D], CB)

        ps = ctx.enter_context(nc.psum_tensor("ps", [P, 8, BANK], F32))

        x2_d = nc.dram_tensor("x2_scratch", (N, D), F32, kind="Internal").ap()
        y_d = nc.dram_tensor("y_scratch", (SLOTS * P, D), F32, kind="Internal").ap()

        ld_x, ld_e, ld_w, ld_vec, ld_rows = (sem(f"ld_{n}") for n in ("x", "edges", "w", "vec", "rows"))
        ld_gw1, ld_gw2, ld_kqv, ld_ow1w2 = (sem(f"ld_{n}") for n in ("gw1", "gw2", "kqv", "wow1w2"))
        consts = sem("consts_ready")
        pads = sem("edge_pads")
        dch = sem("dve_chain")
        pch = sem("pool_chain")
        sq_in, sq_out = sem("sqrt_in"), sem("sqrt_out")
        a_in, a_out = sem("act_tile_full"), sem("act_tile_out")
        d_in, d_out = sem("dve_tile_full"), sem("dve_tile_out")
        range_ready = sem("edge_ranges_ready")
        oh_ready, oh_free = sem("onehots_ready"), sem("onehots_free")
        c_full, c_out = sem("counts_full"), sem("counts_out")
        ct_full, ct_out = sem("countsT_full"), sem("countsT_out")
        sq_ready = sem("squares_ready")
        xm_ready, yh_ready = sem("xm_ready"), sem("yhat_ready")
        xy_ready = sem("x_plus_y_ready")
        xn2_ready = sem("xn2_ready")
        st_x2 = [sem(f"x2_stored{i}") for i in range(2)]
        y_ready = sem("y_rows_ready")
        msk_ready, slot_ready, route_ready, exp_in, exp_out = (sem(n) for n in (
            "mask_ready", "slot_onehots_ready", "route_ready", "gate_exp_in", "gate_exp_out"))
        w_in = sem("expert_loaded")
        gath, xt_full, xt_out = sem("rows_gathered"), sem("xsT_full"), sem("xsT_out")
        gu_full, g_out, gu_out = sem("gate_up_full"), sem("gate_out"), sem("gate_up_out")
        sig_out, a_ready = sem("sigmoid_out"), sem("act_ready")
        at_full, at_out, dn_full, slot_done, y_st = (sem(n) for n in (
            "actT_full", "actT_out", "down_full", "slots_done", "y_stored"))
        cg = [sem(f"pair_gathered{i}") for i in range(CB)]
        o_ready = sem("out_ready")
        o_st = [sem(f"out_stored{i}") for i in range(CB)]

        block = ctx.enter_context(nc.Block())

        def tiled(ap):
            return ap.rearrange("(k p) n -> p k n", p=P)

        def one_row(ap):
            return ap.rearrange("(a n) -> a n", a=1)

        @block.sync
        def _(sp):
            sp.wait_ge(pads, 2)
            for i, e in enumerate((src, dst)):
                sp.dma_start(e_int[:, i, 0, :], e[0:P * P].rearrange("(c k) -> c k", k=P)).then_inc(ld_e, 16)
                sp.dma_start(e_int[0:EFULL - P, i, 1, :],
                             e[P * P:EFULL * P].rearrange("(c k) -> c k", k=P)).then_inc(ld_e, 16)
                sp.dma_start(e_int[EFULL - P:EFULL - P + 1, i, 1, 0:EREST],
                             one_row(e[EFULL * P:E])).then_inc(ld_e, 16)
            sp.dma_start(xr[:, 0:NT - 1, :], tiled(x[0:(NT - 1) * P, :])).then_inc(ld_x, 16)
            sp.dma_start(xr[0:LAST, NT - 1, :], x[(NT - 1) * P:N, :]).then_inc(ld_x, 16)
            sp.dma_start(w_raw, tiled(w)).then_inc(ld_w, 16)
            for at, vec in ((V_G1, g1), (V_BE1, be1), (V_G2, g2), (V_BE2, be2), (V_GB1, gb1), (V_B1, b1),
                            (V_BK, bkqv[0:2 * D])):
                n = vec.shape[0] // P
                sp.dma_start(vrow[at:at + n, :], vec.rearrange("(k p) -> k p", p=P)).then_inc(ld_vec, 16)
            sp.dma_start(gw1_s, tiled(gw1)).then_inc(ld_gw1, 16)
            sp.dma_start(kqv_s, tiled(wkqv)).then_inc(ld_kqv, 16)
            for to, row in ((bv_b, bkqv[2 * D:3 * D]), (bo_b, bo), (b2_b, b2), (gb2_b, gb2), (rb_b, rb)):
                sp.dma_start(to[:, :], row.partition_broadcast(P)).then_inc(ld_rows, 16)
            sp.dma_start(rw_s[:, :, :], tiled(rw)).then_inc(ld_rows, 16)
            sp.wait_ge(ct_out, NT * (NC + 1))
            sp.dma_start(gw2_s, tiled(gw2)).then_inc(ld_gw2, 16)
            sp.wait_ge(d_in, D_V + NT)
            for to, f in ((wo_s, wo), (w1_s, w1), (w2_s, w2)):
                sp.dma_start(to, tiled(f)).then_inc(ld_ow1w2, 16)

            def load_expert(e, part):
                half = (e % 2) * HALF
                if part == 0:
                    sp.dma_start(t3(arena[:, half:half + KD * 2 * I], KD), tiled(wgu[e])).then_inc(w_in, 16)
                    sp.dma_start(t3(arena[:, half + KD * 2 * I:half + EXW], KI), tiled(wd[e])).then_inc(w_in, 16)
                else:
                    sp.dma_start(bgu_b[:, e % 2, :], bgu[e].partition_broadcast(P)).then_inc(w_in, 16)
                    sp.dma_start(bd_b[:, e % 2, :], bd[e].partition_broadcast(P)).then_inc(w_in, 16)
            sp.wait_ge(a_in, A_H + KD * NC)
            load_expert(0, 0)
            for t in range(NT):
                sp.wait_ge(xn2_ready, t + 1)
                sp.dma_start(x2_d[t * P:t * P + rows(t), :], x2[0:rows(t), t % 2, :]).then_inc(st_x2[t % 2], 16)
            for i in range(2):
                sp.wait_ge(st_x2[i], 16 * (NT // 2))
            sp.wait_ge(d_in, D_SLOT + 1)
            load_expert(0, 1)
            sp.wait_ge(route_ready, 1)
            ends = [sp.snap(sp.value_load(cend_i[0:1, e:e + 1], min_val=0, max_val=SLOTS)) for e in range(NX - 2)]
            for e in range(1, NX):
                sp.wait_ge(w_in, 64 * e)
                if e >= 2:
                    sp.wait_ge(slot_done, ends[e - 2] + 1)
                load_expert(e, 0)
                load_expert(e, 1)
            for t in range(NT):
                sp.wait_ge(o_ready, t + 1)
                sp.dma_start(out[t * P:t * P + rows(t), :], ob[0:rows(t), t % CB, :]).then_inc(o_st[t % CB], 16)
            for i in range(CB):
                sp.wait_ge(o_st[i], 16 * len(range(i, NT, CB)))

        @block.gpsimd
        def _(pool):
            n_link = 0

            def link(ins):
                nonlocal n_link
                n_link += 1
                ins.then_inc(pch, 1)
                pool.wait_ge(pch, n_link)
            link(nc.gpsimd.memset(ident[:, :], 0.0))
            nc.gpsimd.affine_select(out=ident[:, :], in_=ident[:, :], compare_op=ALU.not_equal, fill=1.0, base=0,
                                    pattern=[[-1, P]], channel_multiplier=1).then_inc(consts, 1)
            link(nc.gpsimd.memset(ones[:, :], 1.0))
            link(nc.gpsimd.memset(ident_b[:, :], 0.0))
            link(nc.gpsimd.affine_select(out=ident_b[:, :], in_=ident_b[:, :], compare_op=ALU.not_equal, fill=1.0,
                                         base=0, pattern=[[-1, P]], channel_multiplier=1))
            link(nc.gpsimd.iota(piota[:, :], pattern=[[0, 1]], base=0, channel_multiplier=1,
                                allow_small_or_imprecise_dtypes=True))
            nc.gpsimd.iota(iota16[:, :], pattern=[[1, NT * P]], base=0, channel_multiplier=0,
                           allow_small_or_imprecise_dtypes=True).then_inc(consts, 1)
            nc.gpsimd.iota(erow[:, 4, 0:ET], pattern=[[1, ET]], base=0, channel_multiplier=0,
                           allow_small_or_imprecise_dtypes=True).then_inc(consts, 1)
            link(nc.gpsimd.memset(e_id[:, :], 0.0))
            nc.gpsimd.affine_select(out=e_id[:, (NT - 1) * P:NT * P], in_=e_id[:, (NT - 1) * P:NT * P],
                                    compare_op=ALU.not_equal, fill=1.0, base=0, pattern=[[-1, P]],
                                    channel_multiplier=1).then_inc(consts, 1)
            link(nc.gpsimd.memset(ones_b[:, :], 1.0))
            nc.gpsimd.affine_select(out=tri_b[:, :], in_=ones_b[:, :], compare_op=ALU.is_gt, fill=0.0, base=0,
                                    pattern=[[1, P]], channel_multiplier=-1).then_inc(consts, 1)
            pool.wait_ge(ld_rows, 6 * 16)
            link(nc.gpsimd.tensor_tensor(b2_b[:, :], b2_b[:, :], gb2_b[:, :], ALU.add))
            for t in range(NT):
                pool.wait_ge(y_ready, t + 1)
                r = rows(t)
                link(nc.gpsimd.tensor_tensor(xr[0:r, t, :], xr[0:r, t, :], v[0:r, t, :], ALU.add))
                nc.gpsimd.tensor_tensor(xr[0:r, t, :], xr[0:r, t, :], b2_b[0:r, :], ALU.add).then_inc(xy_ready, 1)
            pool.wait_ge(xy_ready, NT)
            pool.wait_ge(d_out, D_X1[NT - 1] + 1)
            nc.gpsimd.iota(iota8[:, :], pattern=[[1, NX]], base=0, channel_multiplier=0,
                           allow_small_or_imprecise_dtypes=True).then_inc(consts, 1)
            nc.gpsimd.iota(iota_s[:, :], pattern=[[1, SLOTS]], base=0, channel_multiplier=0,
                           allow_small_or_imprecise_dtypes=True).then_inc(consts, 1)
            nc.gpsimd.iota(tok[:, :], pattern=[[P, NT]], base=0, channel_multiplier=1,
                           allow_small_or_imprecise_dtypes=True).then_inc(consts, 1)
            nc.gpsimd.iota(iota_c[:, :], pattern=[[1, P]], base=0, channel_multiplier=0,
                           allow_small_or_imprecise_dtypes=True).then_inc(consts, 1)
            pool.wait_ge(route_ready, 1)
            for i in range(2):
                pool.wait_ge(st_x2[i], 16 * (NT // 2))
            for s in range(SLOTS):
                if s:
                    pool.wait_ge(xt_full, s)
                nc.gpsimd.indirect_dma_start(xs, None, x2_d, bass.IndirectOffsetOnAxis(ap=idx_i[:, s:s + 1], axis=0),
                                             bounds_check=N - 1).then_inc(gath, 16)
            pool.wait_ge(y_st, 16 * (SLOTS + 2))
            for t in range(NT):
                r = rows(t)
                if t >= CB:
                    pool.wait_ge(o_ready, t - CB + 1)
                for k in range(TOP):
                    nc.gpsimd.indirect_dma_start(yg[0:r, t % CB, k, :], None, y_d,
                                                 bass.IndirectOffsetOnAxis(ap=pos_i[0:r, k, t:t + 1], axis=0),
                                                 bounds_check=SLOTS * P - 1).then_inc(cg[t % CB], 16)

        @block.scalar
        def _(act):
            n_sqrt = 0

            def sqrt(a, b):
                nonlocal n_sqrt
                n_sqrt += 1
                act.wait_ge(sq_in, n_sqrt)
                nc.scalar.activation(sd[:, a:b], ve[:, a:b], ACT.Sqrt).then_inc(sq_out, 1)

            def full(n):
                act.wait_ge(a_in, n + 1)
                return ps[:, n % 4, :]

            def linear(to, n0, cols, fn, bias):
                for b in range(KD):
                    for c, (a, m) in enumerate(cols):
                        bank = full(n0 + b * NC + c)
                        nc.scalar.activation(to[:, b, a:a + m], bank[:, 0:m], fn,
                                             bias=vT[:, bias + b:bias + b + 1]).then_inc(a_out, 1)
            sqrt(0, NT)
            sqrt(0, NT)
            nc.scalar.copy(vT[:, :], full(A_VEC)[:, 0:8 * KD]).then_inc(a_out, 1)
            for m in range(KM):
                nc.scalar.copy(wT[:, :, m * P:(m + 1) * P],
                               full(A_WT + m)[:, :].rearrange("p (k c) -> p k c", k=KD)).then_inc(a_out, 1)
            act.wait_ge(a_out, A_VEC + 1)

            def affine(to, n0, scale, bias):
                for b in range(KD):
                    for c, (a, m) in enumerate(COLS):
                        bank = full(n0 + b * NC + c)
                        nc.scalar.activation(to[:, b, a:a + m], bank[:, 0:m], ACT.Identity,
                                             scale=vT[:, scale + b:scale + b + 1],
                                             bias=vT[:, bias + b:bias + b + 1]).then_inc(a_out, 1)
            affine(xmT, A_XMT, V_G1, V_BE1)
            for j in range(NT + 1):
                if j < NT:
                    act.wait_ge(c_full, j + 1)
                    if j:
                        act.wait_ge(ct_full, NC * j)
                    for c, (a, m) in enumerate(COLS):
                        nc.scalar.copy(c_stage[:, a:a + m], ps[:, 3 * (j % 2) + c, 0:m]).then_inc(c_out, 1)
                if j < NT:
                    for g in range(NC):
                        n = NC * j + g
                        act.wait_ge(ct_full, n + 1)
                        bank = ps[:, 6 + n % 2, :].rearrange("p (k c) -> p k c", k=TPC)
                        r = rows(j)
                        whole = min(TPC, NT - 1 - TPC * g)
                        nc.scalar.copy(cT[:, TPC * g:TPC * g + whole, j * P:j * P + r], bank[:, 0:whole, 0:r])\
                            .then_inc(ct_out, 1)
                        if whole < TPC:
                            nc.scalar.copy(cT[0:LAST, NT - 1, j * P:j * P + r], bank[0:LAST, whole, 0:r])\
                                .then_inc(ct_out, 1)
            for b in range(KD):
                for c, (a, m) in enumerate(COLS):
                    nc.scalar.copy(zT[:, b, a:a + m], full(A_Z + b * NC + c)[:, 0:m]).then_inc(a_out, 1)
            linear(rT, A_R, COLS, ACT.Relu, V_GB1)
            linear(kT, A_KQ, COLS, ACT.Identity, V_BK)
            linear(qT, A_KQ + KD * NC, COLS, ACT.Identity, V_BQ)
            for i, (to, n0, d0) in enumerate(((kp, A_KP, D_XDK), (qp, A_QP, D_XDQ))):
                act.wait_ge(d_out, d0 + 1)
                for t in range(NT):
                    r = rows(t)
                    nc.scalar.activation(to[0:r, t, :], full(n0 + t)[0:r, 0:M], ACT.Exp,
                                         bias=xdn[0:r, i * NT + t:i * NT + t + 1]).then_inc(a_out, 1)
            for b in range(KM):
                for c, (a, m) in enumerate(COLS):
                    nc.scalar.copy(qpT[:, b, a:a + m], full(A_QPT + b * NC + c)[:, 0:m]).then_inc(a_out, 1)
            for b in range(KM):
                nc.scalar.copy(kptvT[:, b, :], full(A_KPTV + b)).then_inc(a_out, 1)
            for b in range(KD):
                for c, (a, m) in enumerate(COLS):
                    nc.scalar.copy(attT[:, b, a:a + m], full(A_ATT + b * NC + c)[:, 0:m]).then_inc(a_out, 1)
            for c in range(NC):
                sqrt(TPC * c, min(TPC * c + TPC, NT))
            affine(hT, A_H, V_G2, V_BE2)
            linear(gT, A_G, COLS, ACT.Gelu, V_B1)
            for t in range(NT + 1):
                if t < NT:
                    sqrt(t, t + 1)
                if t >= 1:
                    r = rows(t - 1)
                    nc.scalar.copy(x2T[:, (t - 1) % 2, :, 0:r],
                                   full(A_X2T + t - 1)[:, :].rearrange("p (k c) -> p k c", k=KD)[:, :, 0:r])\
                        .then_inc(a_out, 1)
            act.wait_ge(exp_in, 1)
            nc.scalar.activation(ex2[:, 1, :], ex2[:, 0, :], ACT.Exp).then_inc(exp_out, 1)

            def xsT_out(n):
                act.wait_ge(xt_full, n)
                nc.scalar.copy(xsT, ps[:, 7, :]).then_inc(xt_out, 1)

            def slot(s, prev, nxt):
                act.wait_ge(g_out, s + 1)
                nc.scalar.activation(sig_s, g_s, ACT.Sigmoid, scale=1.702).then_inc(sig_out, 1)
                if prev:
                    aT_out(s)
                if nxt:
                    xsT_out(s + 2)
                if prev:
                    store(s)

            def aT_out(n):
                for h in range(2):
                    act.wait_ge(at_full, 2 * n - 1 + h)
                    nc.scalar.copy(aT[:, h * BANK:(h + 1) * BANK], ps[:, 4 + h, :]).then_inc(at_out, 1)

            def store(n):
                act.wait_ge(slot_done, n + 1)
                act.wait_ge(y_st, 16 * (n + 1))
                act.dma_start(y_d[bass.ds((n - 1) * P, P), :], ybuf[:, (n - 1) % 2, :]).then_inc(y_st, 16)
            act.sem_inc(y_st, 32)
            xsT_out(1)
            slot(0, False, True)
            with act.Fori(1, SLOTS - 1) as s:
                slot(s, True, True)
            slot(SLOTS - 1, True, False)
            aT_out(SLOTS)
            store(SLOTS)

        @block.vector
        def _(dve):
            n_link = 0

            def link(ins):
                nonlocal n_link
                n_link += 1
                ins.then_inc(dch, 1)
                dve.wait_ge(dch, n_link)

            def full(n):
                dve.wait_ge(d_in, n + 1)
                return ps[:, 4 + n % 4, :]

            n_sqrt = 0

            def stats(t, rows_of):
                r = rows(t)
                link(nc.vector.bn_stats(st6[0:r, t, :], rows_of[0:r, t, :]))
                link(nc.vector.bn_aggr(mv[0:r, t, :], st6[0:r, t, :]))

            def rstds(a, b):
                nonlocal n_sqrt
                n_sqrt += 1
                nc.vector.tensor_scalar(ve[:, a:b], mv[:, a:b, 1], EPS, None, ALU.add).then_inc(sq_in, 1)
                dve.wait_ge(sq_out, n_sqrt)
                link(nc.vector.reciprocal(rstd[:, a:b], sd[:, a:b]))

            def normed(to, rows_of, t):
                r = rows(t)
                return nc.vector.tensor_scalar(to, rows_of[0:r, t, :], mv[0:r, t, 0:1], rstd[0:r, t:t + 1],
                                               ALU.subtract, ALU.mult)
            nc.vector.memset(e_int[:, 0, 1, :], 0).then_inc(pads, 1)
            nc.vector.memset(e_int[:, 1, 1, :], NOWHERE).then_inc(pads, 1)
            nc.vector.memset(mv[:, :, :], 1.0).then_inc(dch, 1)
            n_link += 1
            dve.wait_ge(ld_e, 6 * 16)
            link(nc.vector.tensor_copy(e_f[:, :, :, :], e_int[:, :, :, :]))
            for g in range(2):
                link(nc.vector.tensor_reduce(mm2[:, g:g + 1], e_f[:, 1, g, :], AX_X, ALU.min))
                link(nc.vector.tensor_reduce(mm2[:, 2 + g:3 + g], e_f[:, 1, g, :], AX_X, ALU.max))
            dve.wait_ge(consts, 1)
            for i in range(4):
                link(nc.vector.tensor_scalar(e_diag[:, i // 2, i % 2, :], ident[:, :], mm2[:, i:i + 1], None, ALU.mult))
            bank = full(D_EDGE)
            nc.vector.tensor_copy(srcT[:, :], bank[:, 0:2 * P])
            link(nc.vector.tensor_copy(dstT[:, :], bank[:, 2 * P:4 * P]))
            dve.wait_ge(consts, 5)
            link(nc.vector.tensor_scalar(lo_j[:, :], piota[:, :], float(P), None, ALU.mult))
            link(nc.vector.tensor_scalar(hi_j[:, :], piota[:, :], float(P), float(P), ALU.mult, ALU.add))
            bank = full(D_RANGE)
            link(nc.vector.tensor_scalar(erow[0:NT, 0, 0:ET], bank[0:NT, 2 * P:2 * P + ET], lo_j[0:NT, :], None, ALU.is_ge))
            link(nc.vector.scalar_tensor_tensor(out=erow[0:NT, 1, 0:ET], in0=bank[0:NT, 0:ET], scalar=hi_j[0:NT, :],
                                                in1=erow[0:NT, 0, 0:ET], op0=ALU.is_lt, op1=ALU.mult))
            link(nc.vector.scalar_tensor_tensor(out=erow[0:NT, 2, 0:ET], in0=erow[0:NT, 4, 0:ET], scalar=1.0,
                                                in1=erow[0:NT, 1, 0:ET], op0=ALU.add, op1=ALU.mult))
            link(nc.vector.tensor_scalar(erow[0:NT, 3, 0:ET], erow[0:NT, 4, 0:ET], -1.0, float(ET), ALU.mult, ALU.add))
            link(nc.vector.tensor_tensor(erow[0:NT, 3, 0:ET], erow[0:NT, 3, 0:ET], erow[0:NT, 1, 0:ET], ALU.mult))
            link(nc.vector.tensor_reduce(rng[0:NT, 0:1], erow[0:NT, 3, 0:ET], AX_X, ALU.max))
            link(nc.vector.tensor_reduce(rng[0:NT, 1:2], erow[0:NT, 2, 0:ET], AX_X, ALU.max))
            link(nc.vector.tensor_scalar(rng[0:NT, 2:3], rng[0:NT, 0:1], -1.0, float(ET), ALU.mult, ALU.add))
            link(nc.vector.tensor_scalar(rng[0:NT, 2:3], rng[0:NT, 2:3], float(ET - 1), None, ALU.min))
            link(nc.vector.scalar_tensor_tensor(out=rng[0:NT, 3:4], in0=rng[0:NT, 2:3], scalar=1.0,
                                                in1=rng[0:NT, 1:2], op0=ALU.add, op1=ALU.max))
            link(nc.vector.tensor_copy(rng_i[0:NT, :], rng[0:NT, 2:4]))
            dve.sem_inc(range_ready, 1)
            dve.sem_inc(d_out, 2)
            dve.wait_ge(ld_x, 32)
            for t in range(NT):
                stats(t, xr)
            rstds(0, NT)
            for t in range(NT):
                link(normed(xn[0:rows(t), t, :], xr, t))
            for t in range(NT):
                stats(t, xn)
            rstds(0, NT)
            for t in range(NT):
                normed(xm[0:rows(t), t, :], xn, t).then_inc(xm_ready, 1)
            made = nc.vector.alloc_register("onehots_made")
            nc.vector.reg_mov(made, 0)
            for j in range(NT):
                first = nc.vector.value_load(rng_i[j:j + 1, 0:1], min_val=0, max_val=ET - 1)
                end = nc.vector.value_load(rng_i[j:j + 1, 1:2], min_val=1, max_val=ET)
                with dve.Fori(first, end) as i:
                    k = nc.vector.snap(made, min_val=0, max_val=NT * ET)
                    dve.wait_ge(oh_free, k + 1)
                    at = nc.vector.snap((k % RING) * RW)
                    nc.vector.tensor_scalar(ring[:, bass.ds(at, N)], iota16[:, 0:N], srcT[:, bass.ds(i, 1)], None,
                                            ALU.is_equal)
                    nc.vector.tensor_scalar(ring[:, bass.ds(at + NT * P, P)], iota16[:, j * P:(j + 1) * P],
                                            dstT[:, bass.ds(i, 1)], None, ALU.is_equal).then_inc(oh_ready, 1)
                    nc.vector.reg_add(made, made, 1)
            dve.wait_ge(a_out, A_KQ + KD * NC)
            for b in range(KD):
                nc.vector.tensor_tensor(sq[:, b, :], kT[:, b, :], kT[:, b, :], ALU.mult).then_inc(sq_ready, 1)
            nc.vector.tensor_scalar(xdn[:, 0:NT], full(D_XDK)[:, 0:NT], -0.5, None, ALU.mult).then_inc(d_out, 1)
            dve.wait_ge(a_out, A_KQ + 2 * KD * NC)
            for b in range(KD):
                nc.vector.tensor_tensor(sq[:, b, :], qT[:, b, :], qT[:, b, :], ALU.mult).then_inc(sq_ready, 1)
            dve.wait_ge(ld_rows, 6 * 16)
            for t in range(NT):
                r = rows(t)
                nc.vector.tensor_tensor(v[0:r, t, :], full(D_V + t)[0:r, :], bv_b[0:r, :], ALU.add).then_inc(d_out, 1)
            nc.vector.tensor_scalar(xdn[:, NT:2 * NT], full(D_XDQ)[:, 0:NT], -0.5, None, ALU.mult).then_inc(d_out, 1)
            nc.vector.tensor_copy(ksum[:, :], full(D_KSUM)[:, 0:KM]).then_inc(d_out, 1)
            nc.vector.tensor_scalar(den[:, :], full(D_DEN)[:, 0:NT], float(M) * ATT_EPS, None, ALU.add).then_inc(d_out, 1)
            dve.wait_ge(d_out, D_DEN + 1)
            link(nc.vector.reciprocal(rden[:, :], den[:, :]))
            for t in range(NT):
                r = rows(t)
                link(nc.vector.scalar_tensor_tensor(out=v[0:r, t, :], in0=full(D_Y + t)[0:r, :], scalar=rden[0:r, t:t + 1],
                                                    in1=v[0:r, t, :], op0=ALU.mult, op1=ALU.add))
                dve.sem_inc(d_out, 1)
                nc.vector.tensor_tensor(v[0:r, t, :], v[0:r, t, :], bo_b[0:r, :], ALU.add).then_inc(y_ready, 1)
                dve.wait_ge(y_ready, t + 1)
                stats(t, v)
                if t % TPC == TPC - 1 or t == NT - 1:
                    a = t - t % TPC
                    rstds(a, t + 1)
                    for u in range(a, t + 1):
                        normed(yhat[0:rows(u), u, :], v, u).then_inc(yh_ready, 1)
            link(nc.vector.memset(logit[:, :, :], 0.0))
            for t in range(NT + 2):
                if t < NT:
                    r = rows(t)
                    bank = full(D_X1[t])
                    dve.wait_ge(xy_ready, t + 1)
                    nc.vector.tensor_tensor(xr[0:r, t, :], bank[0:r, :], xr[0:r, t, :], ALU.add).then_inc(d_out, 1)
                    dve.wait_ge(d_out, D_X1[t] + 1)
                    stats(t, xr)
                    rstds(t, t + 1)
                    if t >= 2:
                        dve.wait_ge(a_in, A_X2T + t - 1)
                        dve.wait_ge(st_x2[t % 2], 16 * (t // 2))
                    normed(x2[0:r, t % 2, :], xr, t).then_inc(xn2_ready, 1)
                if t >= 2:
                    r = rows(t - 2)
                    nc.vector.tensor_tensor(logit[0:r, t - 2, :], full(D_LOG[t - 2])[0:r, 0:NX], rb_b[0:r, :],
                                            ALU.add).then_inc(d_out, 1)
            dve.wait_ge(d_out, D_LOG[NT - 1] + 1)
            dve.wait_ge(consts, 9)
            for t in range(NT):
                link(nc.vector.max(mx8[:, t, :], logit[:, t, :]))
                link(nc.vector.max_index(mi8[:, t, :], mx8[:, t, :], logit[:, t, :]))
            nc.vector.tensor_tensor(ex2[:, 0, :], mx8[:, :, 1], mx8[:, :, 0], ALU.subtract).then_inc(exp_in, 1)
            link(nc.vector.tensor_copy(mif[:, :, :], mi8[:, :, :]))
            link(nc.vector.tensor_scalar(lo_j[:, :], piota[:, :], float(LAST), None, ALU.is_lt))
            for k in range(TOP):
                for t in range(NT):
                    link(nc.vector.tensor_scalar(oh[:, k, t, :], iota8[:, :], mif[:, t, k:k + 1], None, ALU.is_equal))
                link(nc.vector.tensor_scalar(oh[:, k, NT - 1, :], oh[:, k, NT - 1, :], lo_j[:, 0:1], None, ALU.mult))
            nc.vector.tensor_tensor(msk_b.rearrange("p (t e) -> p t e", t=NT), oh[:, 0, :, :], oh[:, 1, :, :],
                                    ALU.add).then_inc(msk_ready, 1)
            dve.wait_ge(exp_out, 1)
            link(nc.vector.tensor_scalar(den[:, :], ex2[:, 1, :], 1.0, None, ALU.add))
            link(nc.vector.reciprocal(wgt[:, 0, :], den[:, :]))
            link(nc.vector.tensor_tensor(wgt[:, 1, :], wgt[:, 0, :], ex2[:, 1, :], ALU.mult))
            bank = full(D_RANK)
            tot = t3(bank[:, NT * NX:2 * NT * NX], NT)
            link(nc.vector.memset(pre[:, 0, :], 0.0))
            for t in range(NT):
                link(nc.vector.tensor_tensor(pre[:, t + 1, :], tot[:, t, :], pre[:, t, :], ALU.add))
            link(nc.vector.tensor_scalar(cnt[:, :], pre[:, NT, :], float(P - 1), None, ALU.add))
            link(nc.vector.tensor_copy(cnt_i[:, :], cnt[:, :]))
            link(nc.vector.tensor_scalar(cnt_i[:, :], cnt_i[:, :], 7, None, ALU.arith_shift_right))
            link(nc.vector.tensor_copy(cnt[:, :], cnt_i[:, :]))
            link(nc.vector.tensor_copy(cend[:, 0:1], cnt[:, 0:1]))
            for e in range(1, NX):
                link(nc.vector.tensor_tensor(cend[:, e:e + 1], cend[:, e - 1:e], cnt[:, e:e + 1], ALU.add))
            link(nc.vector.tensor_copy(cend_i[:, :], cend[:, :]))
            link(nc.vector.tensor_tensor(base[:, :], cend[:, :], cnt[:, :], ALU.subtract))
            link(nc.vector.tensor_scalar(base[:, :], base[:, :], float(P), None, ALU.mult))
            link(nc.vector.tensor_tensor(rank, t3(bank[:, 0:NT * NX], NT), pre[:, 0:NT, :], ALU.add))
            for t in range(NT):
                link(nc.vector.tensor_tensor(rank[:, t, :], rank[:, t, :], base[:, :], ALU.add))
            for k in range(TOP):
                link(nc.vector.tensor_tensor(prod[:, k, :, :], oh[:, k, :, :], rank, ALU.mult))
                link(nc.vector.tensor_reduce(posf[:, k, :], prod[:, k, :, :], AX_X, ALU.add))
            link(nc.vector.tensor_copy(pos_i[:, :, :], posf))
            link(nc.vector.tensor_scalar(pa_i, pos_i[:, :, :], 7, None, ALU.arith_shift_right))
            link(nc.vector.tensor_scalar(pb_i, pos_i[:, :, :], P - 1, None, ALU.bitwise_and))
            link(nc.vector.tensor_copy(pa_f, pa_i))
            link(nc.vector.tensor_copy(pb_f, pb_i))
            link(nc.vector.tensor_tensor(tok[:, NT - 1:NT], tok[:, NT - 1:NT], lo_j[:, 0:1], ALU.mult))
            for k in range(TOP):
                for t in range(NT):
                    nc.vector.tensor_scalar(slot_b[:, k, t, :], iota_c[:, :], pb_f[:, k, t:t + 1], None, ALU.is_equal)
                    nc.vector.tensor_scalar(slot_a[:, k, t, :], iota_s[:, :], pa_f[:, k, t:t + 1], tok[:, t:t + 1],
                                            ALU.is_equal, ALU.mult).then_inc(slot_ready, 1)
            for s in range(NX):
                link(nc.vector.tensor_scalar(cmp_s[:, :, s], iota_s[:, :], cend[:, s:s + 1], None, ALU.is_ge))
            link(nc.vector.tensor_reduce(e_fl[:, :], cmp_s[:, :, :], AX_X, ALU.add))
            link(nc.vector.tensor_scalar(e_fl[:, :], e_fl[:, :], float(NX - 1), None, ALU.min))
            link(nc.vector.tensor_copy(etab[:, :], e_fl[:, :]))
            link(nc.vector.tensor_copy(idx_i[:, :], full(D_SLOT)[:, 0:SLOTS]))
            dve.sem_inc(route_ready, 1)

            gate = ps[:, 0:2, :].rearrange("p a b -> p (a b)")
            up = ps[:, 2:4, :].rearrange("p a b -> p (a b)")

            def expert_of(s):
                e = nc.vector.value_load(etab[0:1, bass.ds(s, 1)], min_val=0, max_val=NX - 1)
                return nc.vector.snap(e % 2)

            def activate(s, first=False):
                h = expert_of(s)
                bias = bgu_b.rearrange("p a b -> p (a b)")
                dve.wait_ge(gu_full, 4 * s + 2)
                nc.vector.tensor_tensor(g_s, gate, bias[:, bass.ds(h * (2 * I), I)], ALU.add).then_inc(g_out, 1)
                dve.wait_ge(gu_full, 4 * s + 4)
                if not first:
                    dve.wait_ge(a_ready, s)
                nc.vector.scalar_tensor_tensor(out=u_s, in0=up, scalar=1.0, in1=bias[:, bass.ds(h * (2 * I) + I, I)],
                                               op0=ALU.add, op1=ALU.add).then_inc(gu_out, 1)
                dve.wait_ge(sig_out, s + 1)
                nc.vector.tensor_tensor(sig_s, g_s, sig_s, ALU.mult).then_inc(gu_out, 1)
                dve.wait_ge(gu_out, 2 * s + 2)
                if not first:
                    dve.wait_ge(at_full, 2 * s)
                nc.vector.tensor_tensor(a_s, u_s, sig_s, ALU.mult).then_inc(a_ready, 1)

            def finish(n):
                h = expert_of(n - 1)
                dve.wait_ge(dn_full, n)
                dve.wait_ge(y_st, 16 * n)
                nc.vector.tensor_tensor(ybuf.rearrange("p a b -> p (a b)")[:, bass.ds(((n - 1) % 2) * D, D)], ps[:, 6, :],
                                        bd_b.rearrange("p a b -> p (a b)")[:, bass.ds(h * D, D)],
                                        ALU.add).then_inc(slot_done, 1)
            dve.sem_inc(slot_done, 1)
            activate(0, True)
            with dve.Fori(1, SLOTS) as s:
                activate(s)
                finish(s)
            finish(SLOTS)

            for t in range(NT):
                r, c = rows(t), t % CB
                dve.wait_ge(cg[c], 32 * (t // CB + 1))
                if t >= CB:
                    dve.wait_ge(o_st[c], 16 * (t // CB))
                link(nc.vector.scalar_tensor_tensor(out=xr[0:r, t, :], in0=yg[0:r, c, 0, :], scalar=wgt[0:r, 0, t:t + 1],
                                                    in1=xr[0:r, t, :], op0=ALU.mult, op1=ALU.add))
                nc.vector.scalar_tensor_tensor(out=ob[0:r, c, :], in0=yg[0:r, c, 1, :], scalar=wgt[0:r, 1, t:t + 1],
                                               in1=xr[0:r, t, :], op0=ALU.mult, op1=ALU.add).then_inc(o_ready, 1)

        @block.tensor
        def _(pe):
            mm, tr = nc.tensor.matmul, nc.tensor.transpose

            def a_tile(n):
                if n >= 4:
                    pe.wait_ge(a_out, n - 3)
                return ps[:, n % 4, :]

            def d_tile(n):
                if n >= 4:
                    pe.wait_ge(d_out, n - 3)
                return ps[:, 4 + n % 4, :]

            def to_cols(n0, rows_of, ready, nb):
                for b in range(nb):
                    for c, (a, m) in enumerate(COLS):
                        bank = a_tile(n0 + b * NC + c)
                        for t in range(TPC * c, min(TPC * c + TPC, NT)):
                            ready(t)
                            r = rows(t)
                            q = tr(bank[:, (t - TPC * c) * P:(t - TPC * c) * P + r], rows_of[0:r, t, b * P:(b + 1) * P],
                                   ident[0:r, 0:r])
                        q.then_inc(a_in, 1)

            def layer(n0, wt, xT, nk, col0=0):
                for b in range(KD):
                    for c, (a, m) in enumerate(COLS):
                        bank = a_tile(n0 + b * NC + c)
                        for k in range(nk):
                            q = mm(bank[:, 0:m], wt[:, k, col0 + b * P:col0 + (b + 1) * P], xT[:, k, a:a + m],
                                   start=(k == 0), stop=(k == nk - 1))
                        q.then_inc(a_in, 1)
            pe.wait_ge(consts, 1)
            pe.wait_ge(dch, 2)
            bank = d_tile(D_EDGE)
            for i in range(4):
                q = tr(bank[:, i * P:(i + 1) * P], e_f[:, i // 2, i % 2, :], ident[:, :])
            q.then_inc(d_in, 1)
            pe.wait_ge(dch, 10)
            pe.wait_ge(consts, 2)
            bank = d_tile(D_RANGE)
            for i in range(4):
                q = mm(bank[0:NT, i * P:(i + 1) * P], ones[:, 0:NT], e_diag[:, i // 2, i % 2, :], start=True, stop=True)
            q.then_inc(d_in, 1)
            pe.wait_ge(ld_vec, 7 * 16)
            tr(a_tile(A_VEC)[:, 0:8 * KD], vrow[:, :], ident[0:8 * KD, 0:8 * KD]).then_inc(a_in, 1)
            pe.wait_ge(ld_w, 16)
            for m in range(KM):
                bank = a_tile(A_WT + m)
                for k in range(KD):
                    q = tr(bank[:, k * P:(k + 1) * P], w_raw[:, m, k * P:(k + 1) * P], ident[:, :])
                q.then_inc(a_in, 1)
            to_cols(A_XMT, xm, lambda t: pe.wait_ge(xm_ready, t + 1), KD)

            pe.wait_ge(consts, 5)
            pe.wait_ge(range_ready, 1)
            pe.wait_ge(a_out, A_XMT + KD * NC)
            pe.wait_ge(d_out, D_RANGE + 1)
            pe.sem_inc(oh_free, RING)
            used = nc.tensor.alloc_register("onehots_used")
            nc.tensor.reg_mov(used, 0)

            def turn_counts(j):
                for g in range(NC):
                    n = NC * j + g
                    pe.wait_ge(c_out, NC * j + g + 1)
                    if n >= 2:
                        before = n - 2
                        pe.wait_ge(ct_out, (NC + 1) * (before // NC) + (before % NC + 1 if before % NC < NC - 1 else NC + 1))
                    bank = ps[:, 6 + n % 2, :]
                    for i in range(TPC * g, min(TPC * g + TPC, NT)):
                        r = rows(i)
                        q = tr(bank[0:r, (i - TPC * g) * P:(i - TPC * g + 1) * P], c_stage[:, i * P:i * P + r], ident[:, :])
                    q.then_inc(ct_full, 1)
            for j in range(NT):
                first = nc.tensor.value_load(rng_i[j:j + 1, 0:1], min_val=0, max_val=ET - 1)
                end = nc.tensor.value_load(rng_i[j:j + 1, 1:2], min_val=1, max_val=ET)
                if j >= 2:
                    pe.wait_ge(c_out, NC * (j - 1))
                banks = [ps[:, 3 * (j % 2) + c, 0:m] for c, (a, m) in enumerate(COLS)]
                for c, (a, m) in enumerate(COLS):
                    o = (NT - 1 - j) * P + a
                    mm(banks[c], ident_b[:, :], e_id[:, o:o + m], start=True, stop=False, skip_group_check=True)
                with pe.Fori(first, end) as i:
                    k = nc.tensor.snap(used, min_val=0, max_val=NT * ET)
                    pe.wait_ge(oh_ready, k + 1)
                    at = nc.tensor.snap((k % RING) * RW)
                    for c, (a, m) in enumerate(COLS):
                        q = mm(banks[c], ring[:, bass.ds(at + NT * P, P)], ring[:, bass.ds(at + a, m)],
                               start=False, stop=True, skip_group_check=True)
                    q.then_inc(oh_free, 1)
                    nc.tensor.reg_add(used, used, 1)
                pe.wait_ge(oh_free, nc.tensor.snap(used, min_val=1, max_val=NT * ET) + RING)
                pe.sem_inc(c_full, 1)
                if j >= 1:
                    turn_counts(j - 1)
            turn_counts(NT - 1)

            pe.wait_ge(ct_out, (NC + 1) * NT)
            for b in range(KD):
                for c, (a, m) in enumerate(COLS):
                    bank = a_tile(A_Z + b * NC + c)
                    for i in range(NT):
                        r = rows(i)
                        q = mm(bank[:, 0:m], xn[0:r, i, b * P:(b + 1) * P], cT[0:r, i, a:a + m],
                               start=(i == 0), stop=(i == NT - 1))
                    q.then_inc(a_in, 1)
            pe.wait_ge(a_out, A_Z + KD * NC)
            pe.wait_ge(ld_gw1, 16)
            layer(A_R, gw1_s, zT, KD)
            pe.wait_ge(ld_kqv, 16)
            layer(A_KQ, kqv_s, xmT, KD)
            layer(A_KQ + KD * NC, kqv_s, xmT, KD, D)

            def squares(n, count):
                pe.wait_ge(sq_ready, count)
                bank = d_tile(n)
                for t in range(NT):
                    r = rows(t)
                    for k in range(KD):
                        q = mm(bank[0:r, t:t + 1], sq[:, k, t * P:t * P + r], ones[:, 0:1],
                               start=(k == 0), stop=(k == KD - 1))
                q.then_inc(d_in, 1)
            squares(D_XDK, KD)
            for t in range(NT):
                r = rows(t)
                bank = d_tile(D_V + t)
                for k in range(KD):
                    q = mm(bank[0:r, :], xmT[:, k, t * P:t * P + r], kqv_s[:, k, 2 * D:3 * D],
                           start=(k == 0), stop=(k == KD - 1))
                q.then_inc(d_in, 1)
            squares(D_XDQ, 2 * KD)
            for n0, xT in ((A_KP, kT), (A_QP, qT)):
                for t in range(NT):
                    r = rows(t)
                    bank = a_tile(n0 + t)
                    for k in range(KD):
                        q = mm(bank[0:r, 0:M], xT[:, k, t * P:t * P + r], wT[:, k, :], start=(k == 0), stop=(k == KD - 1))
                    q.then_inc(a_in, 1)
            pe.wait_ge(a_out, A_KP + NT)
            bank = d_tile(D_KSUM)
            for b in range(KM):
                for t in range(NT):
                    r = rows(t)
                    q = mm(bank[:, b:b + 1], kp[0:r, t, b * P:(b + 1) * P], ones[0:r, 0:1],
                           start=(t == 0), stop=(t == NT - 1))
            q.then_inc(d_in, 1)
            to_cols(A_QPT, qp, lambda t: pe.wait_ge(a_out, A_QP + t + 1), KM)
            pe.wait_ge(d_out, D_V + NT)
            for b in range(KM):
                bank = a_tile(A_KPTV + b)
                for t in range(NT):
                    r = rows(t)
                    q = mm(bank, kp[0:r, t, b * P:(b + 1) * P], v[0:r, t, :], start=(t == 0), stop=(t == NT - 1))
                q.then_inc(a_in, 1)
            pe.wait_ge(a_out, A_QPT + KM * NC)
            pe.wait_ge(d_out, D_KSUM + 1)
            bank = d_tile(D_DEN)
            for t in range(NT):
                r = rows(t)
                for b in range(KM):
                    q = mm(bank[0:r, t:t + 1], qpT[:, b, t * P:t * P + r], ksum[:, b:b + 1],
                           start=(b == 0), stop=(b == KM - 1))
            q.then_inc(d_in, 1)
            pe.wait_ge(a_out, A_KPTV + KM)
            layer(A_ATT, kptvT, qpT, KM)
            pe.wait_ge(ld_ow1w2, 3 * 16)
            pe.wait_ge(a_out, A_ATT + KD * NC)
            for t in range(NT):
                r = rows(t)
                bank = d_tile(D_Y + t)
                for k in range(KD):
                    q = mm(bank[0:r, :], attT[:, k, t * P:t * P + r], wo_s[:, k, :], start=(k == 0), stop=(k == KD - 1))
                q.then_inc(d_in, 1)
            to_cols(A_H, yhat, lambda t: pe.wait_ge(yh_ready, t + 1), KD)
            pe.wait_ge(a_out, A_H + KD * NC)
            layer(A_G, w1_s, hT, KD)
            pe.wait_ge(a_out, A_G + KD * NC)
            pe.wait_ge(ld_gw2, 16)
            for t in range(NT + 2):
                if t < NT:
                    r = rows(t)
                    bank = d_tile(D_X1[t])
                    for k in range(KD):
                        mm(bank[0:r, :], gT[:, k, t * P:t * P + r], w2_s[:, k, :], start=(k == 0), stop=False)
                    for k in range(KD):
                        q = mm(bank[0:r, :], rT[:, k, t * P:t * P + r], gw2_s[:, k, :], start=False, stop=(k == KD - 1))
                    q.then_inc(d_in, 1)
                if 1 <= t <= NT:
                    u = t - 1
                    r = rows(u)
                    pe.wait_ge(xn2_ready, u + 1)
                    bank = a_tile(A_X2T + u)
                    for k in range(KD):
                        q = tr(bank[:, k * P:k * P + r], x2[0:r, u % 2, k * P:(k + 1) * P], ident[0:r, 0:r])
                    q.then_inc(a_in, 1)
                if t >= 2:
                    u = t - 2
                    r = rows(u)
                    pe.wait_ge(a_out, A_X2T + u + 1)
                    bank = d_tile(D_LOG[u])
                    for k in range(KD):
                        q = mm(bank[0:r, 0:NX], x2T[:, u % 2, k, 0:r], rw_s[:, k, :], start=(k == 0), stop=(k == KD - 1))
                    q.then_inc(d_in, 1)
            pe.wait_ge(msk_ready, 1)
            bank = d_tile(D_RANK)
            mm(bank[:, 0:NT * NX], tri_b[:, :], msk_b, start=True, stop=True)
            mm(bank[:, NT * NX:2 * NT * NX], ones_b[:, :], msk_b, start=True, stop=True).then_inc(d_in, 1)
            bank = d_tile(D_SLOT)
            for n in range(TOP * NT):
                pe.wait_ge(slot_ready, n + 1)
                q = mm(bank[:, 0:SLOTS], slot_b[:, n // NT, n % NT, :], slot_a[:, n // NT, n % NT, :],
                       start=(n == 0), stop=(n == TOP * NT - 1))
            q.then_inc(d_in, 1)

            pe.wait_ge(route_ready, 1)

            def expert_of(s):
                return nc.tensor.value_load(etab[0:1, bass.ds(s, 1)], min_val=0, max_val=NX - 1)

            def turn_xs(n):
                pe.wait_ge(gath, 16 * n)
                for k in range(KD):
                    q = tr(ps[:, 7, k * P:(k + 1) * P], xs[:, k * P:(k + 1) * P], ident[:, :])
                q.then_inc(xt_full, 1)

            def gate_up(s, first):
                e = expert_of(s)
                half = nc.tensor.snap((e % 2) * HALF)
                pe.wait_ge(w_in, (e + 1) * 64)
                pe.wait_ge(xt_out, s + 1)
                for c in range(4):
                    if c % 2 == 0 and not first:
                        pe.wait_ge(*((g_out, s) if c == 0 else (gu_out, 2 * s - 1)))
                    for k in range(KD):
                        q = mm(ps[:, c, :], xsT[:, k * P:(k + 1) * P],
                               arena[:, bass.ds(half + (k * 2 * I + c * BANK), BANK)],
                               start=(k == 0), stop=(k == KD - 1))
                    q.then_inc(gu_full, 1)

            def turn_act(n):
                pe.wait_ge(a_ready, n)
                for h in range(2):
                    for k in range(4):
                        i = 4 * h + k
                        q = tr(ps[:, 4 + h, k * P:(k + 1) * P], a_s[:, i * P:(i + 1) * P], ident[:, :])
                    q.then_inc(at_full, 1)

            def down(n):
                e = expert_of(n - 1)
                half = nc.tensor.snap((e % 2) * HALF + KD * 2 * I)
                pe.wait_ge(slot_done, n)
                for k in range(KI):
                    if k % 4 == 0:
                        pe.wait_ge(at_out, 2 * n - 1 + k // 4)
                    q = mm(ps[:, 6, :], aT[:, k * P:(k + 1) * P], arena[:, bass.ds(half + k * D, D)],
                           start=(k == 0), stop=(k == KI - 1))
                q.then_inc(dn_full, 1)
            turn_xs(1)
            gate_up(0, True)
            turn_xs(2)
            with pe.Fori(1, SLOTS - 1) as s:
                gate_up(s, False)
                turn_act(s)
                turn_xs(s + 2)
                down(s)
            gate_up(SLOTS - 1, False)
            turn_act(SLOTS - 1)
            down(SLOTS - 1)
            turn_act(SLOTS)
            down(SLOTS)


_INS = ['x', 'src', 'dst', 'L0_gnn_W1', 'L0_gnn_b1', 'L0_gnn_W2', 'L0_gnn_b2', 'L0_mix_w', 'L0_mix_Wkqv',
        'L0_mix_bkqv', 'L0_mix_Wo', 'L0_mix_bo', 'L0_mix_W1', 'L0_mix_b1', 'L0_mix_W2', 'L0_mix_b2', 'L0_mix_g1',
        'L0_mix_be1', 'L0_mix_g2', 'L0_mix_be2', 'L0_ffn_router_w', 'L0_ffn_router_b', 'L0_ffn_gate_up_proj',
        'L0_ffn_gate_up_proj_bias', 'L0_ffn_down_proj', 'L0_ffn_down_proj_bias']
_OUTS = [((1250, 512), 'float32')]


def kernel(**inputs):
    import numpy as _np
    import concourse.bacc as _bacc
    from concourse import mybir as _mybir
    from concourse.bass_utils import run_bass_kernel_spmd as _run

    nc = _bacc.Bacc("TRN2", target_bir_lowering=False, num_devices=1)
    arrays, args = {}, []
    for name in _INS:
        a = _np.ascontiguousarray(inputs[name])
        arrays[f"in_{name}_dram"] = a
        args.append(nc.dram_tensor(f"in_{name}_dram", a.shape, _mybir.dt.from_np(a.dtype), kind="ExternalInput").ap())
    for i, (shape, dtype) in enumerate(_OUTS):
        dt = _mybir.dt.from_np(_np.dtype(dtype))
        args.append(nc.dram_tensor(f"out_{i}_dram", shape, dt, kind="ExternalOutput").ap())
    bass_gps_gnn_performer_moe(nc, *args)
    r = _run(nc, [arrays], core_ids=[0])
    got = tuple(r.results[0][f"out_{i}_dram"] for i in range(len(_OUTS)))
    return got[0]
```

```python
from contextlib import ExitStack

import concourse.bass as bass
from concourse import mybir

ALU = mybir.AluOpType
ACT = mybir.ActivationFunctionType
AX_X = mybir.AxisListType.X
F32 = mybir.dt.float32
F32R = mybir.dt.float32r
BF16 = mybir.dt.bfloat16
I32 = mybir.dt.int32
U32 = mybir.dt.uint32
I16 = mybir.dt.int16
P = 128
BANK = 512
EPS = 1e-5
ATT_EPS = 1e-8


def bass_gps_gnn_performer_moe(nc, x, src, dst, gw1, gb1, gw2, gb2, w, wkqv, bkqv, wo, bo, w1, b1, w2, b2,
                               g1, be1, g2, be2, rw, rb, wgu, bgu, wd, bd, out):
    N, D = x.shape
    E = src.shape[0]
    M = w.shape[0]
    NX = rw.shape[1]
    I = wd.shape[1]
    TOP = 2
    NT = -(-N // P)
    KD = D // P
    KM = M // P
    KI = I // P
    LAST = N - (NT - 1) * P
    ET = -(-E // P)
    EFULL = E // P
    EREST = E - EFULL * P
    LONG_SHIFT = 5
    assert (P << LONG_SHIFT) <= 1 << 12
    NOWHERE = 2047
    SLOTS = (TOP * N + NX * (P - 1)) // P
    SLOTS_MIN = -(-TOP * N // P)
    RING = 4
    assert D == BANK and EREST and ET + RING - 1 <= 2 * P and M % P == 0

    def rows(t):
        return P if t < NT - 1 else LAST

    COLS = [(a, min(BANK, N - a)) for a in range(0, N, BANK)]
    NC = len(COLS)
    TPC = BANK // P

    a_n = 0

    def a_stage(n):
        nonlocal a_n
        a_n += n
        return a_n - n
    A_VEC = a_stage(1)
    A_WT = a_stage(KM)
    A_Z = a_stage(KD * NC)
    A_XMT = a_stage(KD * NC)
    A_R = a_stage(KD * NC)
    A_KQ = a_stage(2 * KD * NC)
    A_KP = a_stage(NT)
    A_QP = a_stage(NT)
    A_QPT = a_stage(KM * NC)
    A_KPTV = a_stage(KM)
    A_ATT = a_stage(KD * NC)
    A_H = a_stage(KD * NC)
    A_G = a_stage(KD * NC)
    A_X2T = a_stage(NT)
    A_END = a_n
    D_EDGE, D_RANGE, D_XDK, D_V = 0, 1, 2, 3
    D_XDQ = D_V + NT
    D_KSUM = D_XDQ + 1
    D_Y = D_KSUM + 1
    d_last = D_Y + NT
    D_X1, D_LOG = {}, {}
    for t in range(NT + 2):
        if t < NT:
            D_X1[t] = d_last
            d_last += 1
        if t >= 2:
            D_LOG[t - 2] = d_last
            d_last += 1
    D_RANK = d_last
    D_SLOT = D_RANK + 1

    with ExitStack() as ctx:
        def sb(name, shape, dt=F32):
            return ctx.enter_context(nc.sbuf_tensor(name, shape, dt))

        def sem(name):
            return ctx.enter_context(nc.semaphore(name))

        xr = sb("x_rows", [P, NT, D])
        r1_at = nc.sbuf_base
        r1 = sb("r1", [P, NT * D])
        HALF = 2 * KD * N + NT * M
        assert NT * N <= HALF
        XL = -(-NT * N // 8) * 8
        B2, B4 = HALF, max(HALF + KD * N, XL + NT * D)
        B5 = B4 + 2 * NT * M
        arena_at = nc.sbuf_base
        arena = sb("arena", [P, B5 + NT * D])
        CW = KD * BANK
        GC, DC = 2 * I // BANK, KI // KD
        assert D == BANK and KD * BANK == CW and 2 * (GC + DC) * CW + 2 * I + 2 * D <= B5 + NT * D
        w_sp = nc.alloc_sbuf_tensor_at("weights_split", [P, GC + DC, 2, CW], F32R, offset=arena_at)
        aT_sp = nc.alloc_sbuf_tensor_at("act_split", [P, 2, I], F32R, offset=arena_at + 8 * (GC + DC) * CW)
        xT_sp = nc.alloc_sbuf_tensor_at("rows_split", [P, 2, D], F32R, offset=arena_at + 8 * (GC + DC) * CW + 8 * I)
        wa = sb("weights", [P, 5 * KD * D + KD * M + 3 * D + 4 * P])

        def t3(ap, n):
            return ap.rearrange("p (a b) -> p a b", a=n)

        v = t3(r1[:, :], NT)
        cT = t3(arena[:, 0:NT * N], NT)
        cT_r = nc.alloc_sbuf_tensor_at("countsT_short", [P, NT, N], F32R, offset=arena_at)
        xh = nc.alloc_sbuf_tensor_at("xn_leading", [P, NT, D], F32R, offset=r1_at)
        xl = nc.alloc_sbuf_tensor_at("xn_rest", [P, NT, D], F32R, offset=arena_at + 4 * XL)
        kT = t3(arena[:, 0:KD * N], KD)
        qT = t3(arena[:, KD * N:2 * KD * N], KD)
        kp = t3(arena[:, 2 * KD * N:HALF], NT)
        kptvT = t3(arena[:, 0:KM * D], KM)
        yhat = t3(arena[:, 0:NT * D], NT)
        w_raw = t3(arena[:, 0:KM * D], KM)
        o = KM * D
        e_int = arena[:, o:o + 4 * P].bitcast(I32).rearrange("p (a g c) -> p a g c", a=2, g=2)
        o += 4 * P
        e_f = arena[:, o:o + 4 * P].rearrange("p (a g c) -> p a g c", a=2, g=2)
        o += 4 * P
        e_diag = arena[:, o:o + 4 * P].rearrange("p (a g c) -> p a g c", a=2, g=2)
        xmT = t3(arena[:, B2:B2 + KD * N], KD)
        attT = xmT
        zero = arena[:, B2:B2 + D]
        gT = xmT
        zT = t3(arena[:, B4:B4 + KD * N], KD)
        sq = zT
        hT = zT
        RW = NT * P + P
        ring = t3(arena[:, B4:B4 + RING * RW // 2].bitcast(BF16), RING)
        c_stage = arena[:, B4 + RING * RW // 2:B4 + RING * RW // 2 + N]
        assert RING * RW // 2 + N <= 2 * NT * M
        qp = t3(arena[:, B4:B4 + NT * M], NT)
        qpT = t3(arena[:, B4 + NT * M:B4 + NT * M + KM * N], KM)
        x2 = t3(arena[:, B4:B4 + 2 * D], 2)
        x2T = arena[:, B4 + 2 * D:B4 + 4 * D].rearrange("p (b k c) -> p b k c", b=2, k=KD)
        xn = t3(arena[:, B5:B5 + NT * D], NT)
        xm = xn
        rT = t3(arena[:, B5:B5 + KD * N], KD)
        WSZ = KD * D
        gw1_s = t3(wa[:, 0:WSZ], KD)
        ksum, kpsum, qk = (wa[:, i * M:(i + 1) * M] for i in range(3))
        gw2_s = t3(wa[:, WSZ:2 * WSZ], KD)
        EW = N + (NT - 1) * P
        e_id = wa[:, WSZ:WSZ + EW // 2].bitcast(BF16)
        o = WSZ + EW // 2 + 1
        iota16 = wa[:, o:o + NT * P // 2].bitcast(I16)
        assert o + NT * P // 2 <= 2 * WSZ
        kqv_s = t3(wa[:, 2 * WSZ:5 * WSZ], KD)
        wo_s, w1_s, w2_s = (t3(wa[:, (2 + i) * WSZ:(3 + i) * WSZ], KD) for i in range(3))
        wT = t3(wa[:, 5 * WSZ:5 * WSZ + KD * M], KD)
        raw_gu, raw_d = ([wa[:, i * WSZ:(i + 1) * WSZ] for i in at] for at in ((0, 2), (3, 1)))
        BIAS0 = 4 * WSZ
        BIAS_STEP = WSZ + KD * M
        bd_b = wa[:, 5 * WSZ:5 * WSZ + 2 * D]
        assert CW == WSZ and 2 * I <= WSZ and 2 * D <= KD * M and BIAS0 + BIAS_STEP + 2 * I <= wa.shape[1]
        g_s, u_s, sig_s, a_s = (r1[:, 2 * D + i * I:2 * D + (i + 1) * I] for i in range(4))
        assert 2 * D + 4 * I <= NT * D
        ybuf = t3(r1[:, 0:2 * D], 2)

        ident = sb("ident", [P, P])
        ident_b = sb("ident_b", [P, P], BF16)
        ones = sb("ones", [P, P])
        ones_b = sb("ones_b", [P, P], BF16)
        tri_b = sb("tri_b", [P, P], BF16)
        vrow = sb("vrow", [8 * KD, P])
        vT = sb("vT", [P, 8 * KD])
        V_G1, V_BE1, V_G2, V_BE2, V_GB1, V_B1, V_BK, V_BQ = (KD * i for i in range(8))
        o = 5 * WSZ + KD * M
        bv_b, bo_b, b2_b = (wa[:, o + i * D:o + (i + 1) * D] for i in range(3))
        o += 3 * D
        srcT, dstT = wa[:, o:o + 2 * P], wa[:, o + 2 * P:o + 4 * P]
        gb2_b = sb("gb2_b", [P, D])
        xs = gb2_b[:, :]
        rb_b = sb("rb_b", [P, NX])
        rw_s = sb("rw_s", [P, KD, NX])
        st6 = sb("st6", [P, NT, 6])
        mv = sb("mv", [P, NT, 2])
        ve = sb("ve", [P, NT])
        sd = sb("sd", [P, NT])
        rstd = sb("rstd", [P, NT])
        rstd2 = sb("rstd2", [P, NT])
        nmr = sb("nmr", [P, NT])
        mm2 = sb("minmax", [P, 4])
        xdn = sb("xdn", [P, 2 * NT])
        den = sb("den", [P, NT])
        rden = sb("rden", [P, NT])
        piota = sb("piota", [P, 1])
        lo_j = sb("lo_j", [P, 1])
        hi_j = sb("hi_j", [P, 1])
        rng = sb("rng", [P, 4])
        rng_i = sb("rng_i", [P, 4], I32)
        place_i = sb("place_i", [P, SLOTS], I32)
        used_i = sb("used_i", [P, NX], I32)
        used_end_i = sb("used_end_i", [P, NX + 1], I32)
        last_i = sb("last_i", [P, 2], I32)
        change_i = sb("change_i", [P, SLOTS], I32)
        pos_i = sb("pos_i", [P, TOP, NT], I32)
        idx_i = sb("idx_i", [P, SLOTS], I32)
        idx_s = sb("idx_s", [P, 1], I32)
        wgt = sb("wgt", [P, TOP, NT])
        logit = sb("logit", [P, NT, NX])
        erow = t3(arena[:, B5:B5 + 5 * 2 * P], 5)
        o = 2 * D

        def r1_take(n):
            nonlocal o
            o += n
            assert o <= NT * D
            return r1[:, o - n:o]
        mx8 = t3(r1_take(NT * NX), NT)
        mi8 = t3(r1_take(NT * NX).bitcast(U32), NT)
        mif = t3(r1_take(NT * NX), NT)
        KT = TOP * NT
        oh = r1_take(KT * NX).rearrange("p (k t e) -> p k t e", k=TOP, t=NT)
        msk_b = r1_take(NT * NX // 2).bitcast(BF16)
        rank = t3(r1_take(NT * NX), NT)
        cnt_i = r1_take(NX).bitcast(I32)
        cnt = r1_take(NX)
        has = r1_take(NX)
        ends = t3(r1_take(2 * NX), 2)
        base = r1_take(NX)
        ex2 = t3(r1_take(2 * NT), 2)
        posf = r1_take(KT)
        pa_i, pb_i = (r1_take(KT).bitcast(I32) for _ in range(2))
        pa_f, pb_f = (r1_take(KT) for _ in range(2))
        behind = r1_take(1)
        tile_no = r1_take(KT)
        iota1 = r1_take(NX)
        iota_s = r1_take(SLOTS)
        iota_c = r1_take(P)
        cmp_s = t3(r1_take(SLOTS * NX), SLOTS)
        cmp_u = t3(r1_take(NX * NX), NX)
        num_end = t3(r1_take(2 * NX), 2)
        num_end_of = r1_take(2 * NX * NX).rearrange("p (w i e) -> p w i e", w=2, i=NX)
        used_f = t3(r1_take(2 * NX), 2)
        place_f = r1_take(SLOTS)
        last_f = r1_take(2)
        row_f = r1_take(SLOTS)
        slot_b = r1_take(KT * P // 2).bitcast(BF16).rearrange("p (n c) -> p n c", n=KT)
        slot_1 = r1_take(KT * SLOTS // 2).bitcast(BF16).rearrange("p (n s) -> p n s", n=KT)
        slot_a = r1_take(KT * SLOTS).bitcast(BF16).rearrange("p (n w s) -> p n w s", n=KT, w=2)
        CB = 4
        yg = arena[:, 0:CB * TOP * D].rearrange("p (b k c) -> p b k c", b=CB, k=TOP)
        ob = t3(arena[:, CB * TOP * D:CB * (TOP + 1) * D], CB)

        ps = ctx.enter_context(nc.psum_tensor("ps", [P, 8, BANK], F32))

        x2_d = nc.dram_tensor("x2_scratch", (N, D), F32, kind="Internal").ap()
        y_d = nc.dram_tensor("y_scratch", (SLOTS * P, D), F32, kind="Internal").ap()

        ld_x, ld_e, ld_w, ld_vec, ld_rows = (sem(f"ld_{n}") for n in ("x", "edges", "w", "vec", "rows"))
        ld_gw1, ld_gw2, ld_kqv, ld_ow1w2 = (sem(f"ld_{n}") for n in ("gw1", "gw2", "kqv", "wow1w2"))
        consts = sem("consts_ready")
        pads = sem("edge_pads")
        dch = sem("dve_chain")
        pch = sem("pool_chain")
        sq_in, sq_out = sem("sqrt_in"), sem("sqrt_out")
        a_in, a_out = sem("act_tile_full"), sem("act_tile_out")
        d_in, d_out = sem("dve_tile_full"), sem("dve_tile_out")
        range_ready = sem("edge_ranges_ready")
        oh_ready, oh_free = sem("onehots_ready"), sem("onehots_free")
        c_full, c_out = sem("counts_full"), sem("counts_out")
        ct_full, ct_out = sem("countsT_full"), sem("countsT_out")
        sq_ready, ks_ready = sem("squares_ready"), sem("keys_sum_ready")
        nmr_ready, xn_ready = sem("nmr_ready"), sem("xn_ready")
        xh_ready, xl_ready = sem("xn_leading_ready"), sem("xn_rest_ready")
        xm_ready, yh_ready = sem("xm_ready"), sem("yhat_ready")
        xy_ready = sem("x_plus_y_ready")
        xn2_ready = sem("xn2_ready")
        st_x2 = [sem(f"x2_stored{i}") for i in range(2)]
        y_ready = sem("y_rows_ready")
        msk_ready, slot_ready, route_ready, exp_in, exp_out = (sem(n) for n in (
            "mask_ready", "slot_onehots_ready", "route_ready", "gate_exp_in", "gate_exp_out"))
        zero_ready, st_zero = sem("zeros_ready"), sem("zeros_stored")
        gu_raw = [sem(f"gate_up_chunk_loaded{i}") for i in range(2)]
        d_raw = [sem(f"down_chunk_loaded{i}") for i in range(DC)]
        b_ld = sem("biases_loaded")
        gu_hi, gu_split, d_hi, d_split = (sem(n) for n in (
            "gate_up_leading", "gate_up_split", "down_leading", "down_split"))
        xt_hi, at_hi = sem("xsT_leading"), sem("actT_leading")
        idx_ready, pool_passed, sp_passed = sem("slot_index_ready"), sem("pool_passed"), sem("sp_passed")
        gath, xt_full, xt_out = sem("rows_gathered"), sem("xsT_full"), sem("xsT_out")
        gu_full, g_out, gu_out = sem("gate_up_full"), sem("gate_out"), sem("gate_up_out")
        sig_out, a_ready = sem("sigmoid_out"), sem("act_ready")
        at_full, at_out, dn_full, slot_done, y_st = (sem(n) for n in (
            "actT_full", "actT_out", "down_full", "slots_done", "y_stored"))
        cg = [sem(f"pair_gathered{i}") for i in range(CB)]
        o_ready = sem("out_ready")
        o_st = [sem(f"out_stored{i}") for i in range(CB)]

        block = ctx.enter_context(nc.Block())

        def tiled(ap):
            return ap.rearrange("(k p) n -> p k n", p=P)

        def one_row(ap):
            return ap.rearrange("(a n) -> a n", a=1)

        @block.sync
        def _(sp):
            sp.wait_ge(pads, 2)
            for i, e in enumerate((src, dst)):
                sp.dma_start(e_int[:, i, 0, :], e[0:P * P].rearrange("(c k) -> c k", k=P)).then_inc(ld_e, 16)
                sp.dma_start(e_int[0:EFULL - P, i, 1, :],
                             e[P * P:EFULL * P].rearrange("(c k) -> c k", k=P)).then_inc(ld_e, 16)
                sp.dma_start(e_int[EFULL - P:EFULL - P + 1, i, 1, 0:EREST],
                             one_row(e[EFULL * P:E])).then_inc(ld_e, 16)
            sp.dma_start(xr[:, 0:NT - 1, :], tiled(x[0:(NT - 1) * P, :])).then_inc(ld_x, 16)
            sp.dma_start(xr[0:LAST, NT - 1, :], x[(NT - 1) * P:N, :]).then_inc(ld_x, 16)
            sp.dma_start(w_raw, tiled(w)).then_inc(ld_w, 16)
            sp.wait_ge(zero_ready, 1)
            for s in range(SLOTS_MIN, SLOTS):
                sp.dma_start(y_d[s * P:(s + 1) * P, :], zero).then_inc(st_zero, 16)
            for at, vec in ((V_G1, g1), (V_BE1, be1), (V_G2, g2), (V_BE2, be2), (V_GB1, gb1), (V_B1, b1),
                            (V_BK, bkqv[0:2 * D])):
                n = vec.shape[0] // P
                sp.dma_start(vrow[at:at + n, :], vec.rearrange("(k p) -> k p", p=P)).then_inc(ld_vec, 16)
            sp.dma_start(gw1_s, tiled(gw1)).then_inc(ld_gw1, 16)
            sp.dma_start(kqv_s, tiled(wkqv)).then_inc(ld_kqv, 16)
            for to, row in ((bv_b, bkqv[2 * D:3 * D]), (bo_b, bo), (b2_b, b2), (gb2_b, gb2), (rb_b, rb)):
                sp.dma_start(to[:, :], row.partition_broadcast(P)).then_inc(ld_rows, 16)
            sp.dma_start(rw_s[:, :, :], tiled(rw)).then_inc(ld_rows, 16)
            sp.wait_ge(ct_out, NT * (NC + 1))
            sp.dma_start(gw2_s, tiled(gw2)).then_inc(ld_gw2, 16)
            sp.wait_ge(d_in, D_V + NT)
            for to, f in ((wo_s, wo), (w1_s, w1), (w2_s, w2)):
                sp.dma_start(to, tiled(f)).then_inc(ld_ow1w2, 16)

            def load_gate_up(e, c):
                w_e = wgu[bass.ds(e, 1), :, c * BANK:(c + 1) * BANK] if not isinstance(e, int) else \
                    wgu[e:e + 1, :, c * BANK:(c + 1) * BANK]
                sp.dma_start(t3(raw_gu[c % 2], KD), w_e.rearrange("a (k p) n -> p (a k) n", p=P))\
                    .then_inc(gu_raw[c % 2], 16)

            def load_down(e, h):
                w_e = wd[bass.ds(e, 1), h * CW // KD:(h + 1) * CW // KD, :] if not isinstance(e, int) else \
                    wd[e:e + 1, h * CW // KD:(h + 1) * CW // KD, :]
                sp.dma_start(t3(raw_d[h], KD), w_e.rearrange("a (k p) n -> p (a k) n", p=P)).then_inc(d_raw[h], 16)
            sp.wait_ge(d_out, D_Y + 1)
            load_gate_up(0, 0)
            sp.wait_ge(d_in, D_Y + NT)
            load_gate_up(0, 1)
            sp.wait_ge(a_in, A_G + KD * NC)
            load_down(0, 0)
            for t in range(NT):
                if t in (1, 3):
                    c = 2 + t // 2
                    sp.wait_ge(gu_split, c)
                    load_gate_up(0, c)
                sp.wait_ge(xn2_ready, t + 1)
                sp.dma_start(x2_d[t * P:t * P + rows(t), :], x2[0:rows(t), t % 2, :]).then_inc(st_x2[t % 2], 16)
            for i in range(2):
                sp.wait_ge(st_x2[i], 16 * (NT // 2))
            sp.wait_ge(d_in, D_X1[NT - 1] + 1)
            load_down(0, 1)
            sp.dma_start(wa[:, BIAS0:BIAS0 + 2 * I], bgu[0].partition_broadcast(P)).then_inc(b_ld, 16)
            sp.dma_start(bd_b[:, 0:D], bd[0].partition_broadcast(P)).then_inc(b_ld, 16)
            sp.wait_ge(route_ready, 1)
            sp.wait_ge(gu_split, GC + 1)
            sp.wait_ge(d_split, 2 * DC)
            used_last = sp.value_load(last_i[0:1, 0:1], min_val=1, max_val=NX - 1)

            with sp.Fori(1, used_last + 1) as i:
                e = sp.snap(sp.value_load(used_i[0:1, bass.ds(i, 1)], min_val=0, max_val=NX - 1))
                end2 = sp.snap(sp.value_load(used_end_i[0:1, bass.ds(i - 1, 1)], min_val=0, max_val=SLOTS))
                half = sp.snap(i % 2)
                for c in range(GC):
                    sp.wait_ge(gu_split, i * GC + c)
                    sp.sem_inc(sp_passed, 1)
                    load_gate_up(e, c)
                sp.wait_ge(slot_done, end2 + 1)
                sp.sem_inc(sp_passed, 1)
                sp.wait_ge(b_ld, i * 32)
                sp.sem_inc(sp_passed, 1)
                sp.dma_start(wa[:, bass.ds(half * BIAS_STEP + BIAS0, 2 * I)],
                             bgu[bass.ds(e, 1), :].rearrange("a n -> (a n)").partition_broadcast(P)).then_inc(b_ld, 16)
                sp.dma_start(bd_b[:, bass.ds(half * D, D)],
                             bd[bass.ds(e, 1), :].rearrange("a n -> (a n)").partition_broadcast(P)).then_inc(b_ld, 16)
                for h in range(DC):
                    sp.wait_ge(d_split, i * DC + (h + 1))
                    sp.sem_inc(sp_passed, 1)
                    load_down(e, h)
            for t in range(NT):
                sp.wait_ge(o_ready, t + 1)
                sp.dma_start(out[t * P:t * P + rows(t), :], ob[0:rows(t), t % CB, :]).then_inc(o_st[t % CB], 16)
            for i in range(CB):
                sp.wait_ge(o_st[i], 16 * len(range(i, NT, CB)))

        @block.gpsimd
        def _(pool):
            n_link = 0

            def link(ins):
                nonlocal n_link
                n_link += 1
                ins.then_inc(pch, 1)
                pool.wait_ge(pch, n_link)
            link(nc.gpsimd.memset(ident[:, :], 0.0))
            nc.gpsimd.affine_select(out=ident[:, :], in_=ident[:, :], compare_op=ALU.not_equal, fill=1.0, base=0,
                                    pattern=[[-1, P]], channel_multiplier=1).then_inc(consts, 1)
            link(nc.gpsimd.memset(ones[:, :], 1.0))
            nc.gpsimd.memset(zero, 0.0).then_inc(zero_ready, 1)
            link(nc.gpsimd.memset(ident_b[:, :], 0.0))
            link(nc.gpsimd.affine_select(out=ident_b[:, :], in_=ident_b[:, :], compare_op=ALU.not_equal, fill=1.0,
                                         base=0, pattern=[[-1, P]], channel_multiplier=1))
            link(nc.gpsimd.iota(piota[:, :], pattern=[[0, 1]], base=0, channel_multiplier=1,
                                allow_small_or_imprecise_dtypes=True))
            nc.gpsimd.iota(iota16[:, :], pattern=[[1, NT * P]], base=0, channel_multiplier=0,
                           allow_small_or_imprecise_dtypes=True).then_inc(consts, 1)
            nc.gpsimd.iota(erow[:, 4, 0:ET], pattern=[[1, ET]], base=0, channel_multiplier=0,
                           allow_small_or_imprecise_dtypes=True).then_inc(consts, 1)
            link(nc.gpsimd.memset(e_id[:, :], 0.0))
            nc.gpsimd.affine_select(out=e_id[:, (NT - 1) * P:NT * P], in_=e_id[:, (NT - 1) * P:NT * P],
                                    compare_op=ALU.not_equal, fill=1.0, base=0, pattern=[[-1, P]],
                                    channel_multiplier=1).then_inc(consts, 1)
            link(nc.gpsimd.memset(ones_b[:, :], 1.0))
            nc.gpsimd.affine_select(out=tri_b[:, :], in_=ones_b[:, :], compare_op=ALU.is_gt, fill=0.0, base=0,
                                    pattern=[[1, P]], channel_multiplier=-1).then_inc(consts, 1)
            pool.wait_ge(st_zero, 16 * (SLOTS - SLOTS_MIN))
            for t in range(NT):
                r = rows(t)
                pool.wait_ge(xh_ready, t + 1)
                nc.gpsimd.tensor_tensor(xl[0:r, t, :], xn[0:r, t, :], xh[0:r, t, :].bitcast(F32), ALU.subtract)\
                    .then_inc(xl_ready, 1)
            pool.wait_ge(ld_rows, 6 * 16)
            link(nc.gpsimd.tensor_tensor(b2_b[:, :], b2_b[:, :], gb2_b[:, :], ALU.add))
            for t in range(NT):
                pool.wait_ge(y_ready, t + 1)
                r = rows(t)
                link(nc.gpsimd.tensor_tensor(xr[0:r, t, :], xr[0:r, t, :], v[0:r, t, :], ALU.add))
                nc.gpsimd.tensor_tensor(xr[0:r, t, :], xr[0:r, t, :], b2_b[0:r, :], ALU.add).then_inc(xy_ready, 1)
            pool.wait_ge(xy_ready, NT)
            nc.gpsimd.iota(iota1[:, :], pattern=[[1, NX]], base=1, channel_multiplier=0,
                           allow_small_or_imprecise_dtypes=True).then_inc(consts, 1)
            nc.gpsimd.iota(iota_s[:, :], pattern=[[1, SLOTS]], base=0, channel_multiplier=0,
                           allow_small_or_imprecise_dtypes=True).then_inc(consts, 1)
            nc.gpsimd.iota(t3(tile_no, TOP), pattern=[[0, TOP], [1, NT]], base=0, channel_multiplier=0,
                           allow_small_or_imprecise_dtypes=True).then_inc(consts, 1)
            nc.gpsimd.iota(iota_c[:, :], pattern=[[1, P]], base=0, channel_multiplier=0,
                           allow_small_or_imprecise_dtypes=True).then_inc(consts, 1)
            pool.sem_inc(gu_split, 1)
            pool.sem_inc(d_split, DC)
            for c in range(GC):
                pool.wait_ge(gu_hi, c + 1)
                nc.gpsimd.tensor_tensor(w_sp[:, c, 1, :], raw_gu[c % 2], w_sp[:, c, 0, :].bitcast(F32), ALU.subtract)\
                    .then_inc(gu_split, 1)
            for h in range(DC):
                pool.wait_ge(d_hi, h + 1)
                nc.gpsimd.tensor_tensor(w_sp[:, GC + h, 1, :], raw_d[h], w_sp[:, GC + h, 0, :].bitcast(F32),
                                        ALU.subtract).then_inc(d_split, 1)
            pool.wait_ge(route_ready, 1)
            for i in range(2):
                pool.wait_ge(st_x2[i], 16 * (NT // 2))
            last = nc.gpsimd.value_load(last_i[0:1, 1:2], min_val=SLOTS_MIN - 1, max_val=SLOTS - 1)
            pool.sem_inc(xt_full, 1)
            with pool.Fori(0, last + 1) as s:
                pool.wait_ge(xt_full, s + 1)
                nc.gpsimd.tensor_copy(idx_s[:, :], idx_i[:, bass.ds(s, 1)]).then_inc(idx_ready, 1)
                pool.wait_ge(idx_ready, s + 1)
                pool.sem_inc(pool_passed, 1)
                nc.gpsimd.indirect_dma_start(xs, None, x2_d, bass.IndirectOffsetOnAxis(ap=idx_s[:, :], axis=0),
                                             bounds_check=N - 1).then_inc(gath, 16)
                pool.wait_ge(gath, (s + 1) * 16)
            pool.wait_ge(y_st, nc.gpsimd.snap((last + 3) * 16))
            pool.sem_inc(pool_passed, 1)
            for t in range(NT):
                r = rows(t)
                if t >= CB:
                    pool.wait_ge(o_ready, t - CB + 1)
                for k in range(TOP):
                    nc.gpsimd.indirect_dma_start(yg[0:r, t % CB, k, :], None, y_d,
                                                 bass.IndirectOffsetOnAxis(ap=pos_i[0:r, k, t:t + 1], axis=0),
                                                 bounds_check=SLOTS * P - 1).then_inc(cg[t % CB], 16)

        @block.scalar
        def _(act):
            n_sqrt = 0

            def sqrt(a, b):
                nonlocal n_sqrt
                n_sqrt += 1
                act.wait_ge(sq_in, n_sqrt)
                nc.scalar.activation(sd[:, a:b], ve[:, a:b], ACT.Sqrt).then_inc(sq_out, 1)

            def full(n):
                act.wait_ge(a_in, n + 1)
                return ps[:, n % 4, :]

            def linear(to, n0, cols, fn, bias):
                for b in range(KD):
                    for c, (a, m) in enumerate(cols):
                        bank = full(n0 + b * NC + c)
                        nc.scalar.activation(to[:, b, a:a + m], bank[:, 0:m], fn,
                                             bias=vT[:, bias + b:bias + b + 1]).then_inc(a_out, 1)
            nc.scalar.copy(vT[:, :], full(A_VEC)[:, 0:8 * KD]).then_inc(a_out, 1)
            for m in range(KM):
                nc.scalar.copy(wT[:, :, m * P:(m + 1) * P],
                               full(A_WT + m)[:, :].rearrange("p (k c) -> p k c", k=KD)).then_inc(a_out, 1)
            act.wait_ge(a_out, A_VEC + 1)

            def affine(to, n0, scale, bias):
                for b in range(KD):
                    for c, (a, m) in enumerate(COLS):
                        bank = full(n0 + b * NC + c)
                        nc.scalar.activation(to[:, b, a:a + m], bank[:, 0:m], ACT.Identity,
                                             scale=vT[:, scale + b:scale + b + 1],
                                             bias=vT[:, bias + b:bias + b + 1]).then_inc(a_out, 1)
            act.wait_ge(range_ready, 1)
            long_ranges = nc.scalar.alloc_register("long_ranges")
            nc.scalar.reg_mov(long_ranges, 0)
            for j in range(NT):
                nc.scalar.reg_add(long_ranges, long_ranges,
                                  nc.scalar.value_load(rng_i[j:j + 1, 3:4], min_val=0, max_val=ET >> LONG_SHIFT))
            for j in range(NT + 1):
                if j < NT:
                    act.wait_ge(c_full, j + 1)
                    if j:
                        act.wait_ge(ct_full, NC * j)
                    for c, (a, m) in enumerate(COLS):
                        nc.scalar.copy(c_stage[:, a:a + m], ps[:, 3 * (j % 2) + c, 0:m]).then_inc(c_out, 1)
                if j == 0:
                    sqrt(0, NT)
                    sqrt(0, NT)
                    for t in range(NT):
                        r = rows(t)
                        if t == 0:
                            act.wait_ge(nmr_ready, 1)
                        nc.scalar.activation(xn[0:r, t, :], xr[0:r, t, :], ACT.Identity, scale=rstd[0:r, t:t + 1],
                                             bias=nmr[0:r, t:t + 1]).then_inc(xn_ready, 1)
                    for t in range(NT):
                        act.wait_ge(xn_ready, t + 1)
                        nc.scalar.copy(xh[0:rows(t), t, :], xn[0:rows(t), t, :]).then_inc(xh_ready, 1)
                if j == 1:
                    act.wait_ge(nmr_ready, 2)
                    for t in range(NT):
                        r = rows(t)
                        act.wait_ge(xl_ready, t + 1)
                        nc.scalar.activation(xm[0:r, t, :], xn[0:r, t, :], ACT.Copy,
                                             scale=rstd2[0:r, t:t + 1]).then_inc(xm_ready, 1)
                if j < NT:
                    for g in range(NC):
                        n = NC * j + g
                        act.wait_ge(ct_full, n + 1)
                        bank = ps[:, 6 + n % 2, :].rearrange("p (k c) -> p k c", k=TPC)
                        r = rows(j)
                        whole = min(TPC, NT - 1 - TPC * g)

                        def turned(to):
                            nc.scalar.copy(to[:, TPC * g:TPC * g + whole, j * P:j * P + r], bank[:, 0:whole, 0:r])\
                                .then_inc(ct_out, 1)
                            if whole < TPC:
                                nc.scalar.copy(to[0:LAST, NT - 1, j * P:j * P + r], bank[0:LAST, whole, 0:r])\
                                    .then_inc(ct_out, 1)
                        with act.If_eq(long_ranges, 0):
                            turned(cT_r)
                        with act.If_ne(long_ranges, 0):
                            turned(cT)
            act.wait_ge(st_zero, 16 * (SLOTS - SLOTS_MIN))
            for b in range(KD):
                for c, (a, m) in enumerate(COLS):
                    nc.scalar.copy(zT[:, b, a:a + m], full(A_Z + b * NC + c)[:, 0:m]).then_inc(a_out, 1)
            affine(xmT, A_XMT, V_G1, V_BE1)
            linear(rT, A_R, COLS, ACT.Relu, V_GB1)
            linear(kT, A_KQ, COLS, ACT.Identity, V_BK)
            linear(qT, A_KQ + KD * NC, COLS, ACT.Identity, V_BQ)
            for i, (to, n0, d0) in enumerate(((kp, A_KP, D_XDK), (qp, A_QP, D_XDQ))):
                act.wait_ge(d_out, d0 + 1)
                for t in range(NT):
                    r = rows(t)
                    nc.scalar.activation(to[0:r, t, :], full(n0 + t)[0:r, 0:M], ACT.Exp,
                                         bias=xdn[0:r, i * NT + t:i * NT + t + 1]).then_inc(a_out, 1)
            for b in range(KM):
                for c, (a, m) in enumerate(COLS):
                    nc.scalar.copy(qpT[:, b, a:a + m], full(A_QPT + b * NC + c)[:, 0:m]).then_inc(a_out, 1)
            for b in range(KM):
                nc.scalar.copy(kptvT[:, b, :], full(A_KPTV + b)).then_inc(a_out, 1)
            for b in range(KD):
                for c, (a, m) in enumerate(COLS):
                    nc.scalar.copy(attT[:, b, a:a + m], full(A_ATT + b * NC + c)[:, 0:m]).then_inc(a_out, 1)
            for c in range(NC):
                sqrt(TPC * c, min(TPC * c + TPC, NT))
            affine(hT, A_H, V_G2, V_BE2)
            linear(gT, A_G, COLS, ACT.Gelu, V_B1)

            def gate_up_hi(i, c):
                act.wait_ge(gu_raw[c % 2], i * 32 + 16 * (c // 2 + 1))
                nc.scalar.copy(w_sp[:, c, 0, :], raw_gu[c % 2]).then_inc(gu_hi, 1)

            def down_hi(i, h):
                act.wait_ge(d_raw[h], i * 16 + 16)
                nc.scalar.copy(w_sp[:, GC + h, 0, :], raw_d[h]).then_inc(d_hi, 1)
            gate_up_hi(0, 0)
            gate_up_hi(0, 1)
            for t in range(NT + 1):
                if t == 3:
                    gate_up_hi(0, 2)
                if t < NT:
                    sqrt(t, t + 1)
                if t >= 1:
                    r = rows(t - 1)
                    nc.scalar.copy(x2T[:, (t - 1) % 2, :, 0:r],
                                   full(A_X2T + t - 1)[:, :].rearrange("p (k c) -> p k c", k=KD)[:, :, 0:r])\
                        .then_inc(a_out, 1)
            act.wait_ge(exp_in, 1)
            nc.scalar.activation(ex2[:, 1, :], ex2[:, 0, :], ACT.Exp).then_inc(exp_out, 1)

            act.wait_ge(d_in, D_LOG[NT - 1] + 1)
            for i in range(2):
                act.wait_ge(st_x2[i], 16 * (NT // 2))
            gate_up_hi(0, 3)
            for h in range(DC):
                down_hi(0, h)

            def xsT_out(s):
                act.wait_ge(xt_full, s + 2)
                if not (isinstance(s, int) and s == 0):
                    act.wait_ge(gu_full, s * GC)
                nc.scalar.copy(xT_sp[:, 0, :], ps[:, 7, :]).then_inc(xt_hi, 1)

            def slot(s, prev, nxt):
                if nxt:
                    changes = nc.scalar.value_load(change_i[0:1, bass.ds(s, 1)] if prev else change_i[0:1, 0:1],
                                                   min_val=0, max_val=1)
                    i = nc.scalar.snap(nc.scalar.value_load(
                        place_i[0:1, bass.ds(s, 1)] if prev else place_i[0:1, 0:1], min_val=0, max_val=NX - 1) + 1)
                    with act.If(changes):
                        for c in range(2):
                            act.wait_ge(gu_full, s * GC + (c + 1))
                            gate_up_hi(i, c)
                if prev:
                    aT_out(s)
                act.wait_ge(g_out, s + 1)
                nc.scalar.activation(sig_s, g_s, ACT.Sigmoid, scale=1.702).then_inc(sig_out, 1)
                if nxt:
                    xsT_out(s + 1)
                    with act.If(changes):
                        for c in range(2, GC):
                            gate_up_hi(i, c)
                if prev:
                    change_down(s)
                    store(s)

            def change_down(s):
                changed = nc.scalar.value_load(change_i[0:1, bass.ds(s - 1, 1)], min_val=0, max_val=1)
                i = nc.scalar.snap(nc.scalar.value_load(place_i[0:1, bass.ds(s, 1)], min_val=0, max_val=NX - 1))
                with act.If(changed):
                    act.wait_ge(dn_full, s)
                    for h in range(DC):
                        down_hi(i, h)

            def aT_out(n):
                for h in range(2):
                    act.wait_ge(at_full, 2 * n + h)
                    nc.scalar.copy(aT_sp[:, 0, h * BANK:(h + 1) * BANK], ps[:, 4 + h, :]).then_inc(at_hi, 1)

            def store(n):
                act.wait_ge(slot_done, n + 1)
                act.wait_ge(y_st, 16 * (n + 1))
                act.dma_start(y_d[bass.ds((n - 1) * P, P), :], ybuf[:, (n - 1) % 2, :]).then_inc(y_st, 16)
            act.sem_inc(y_st, 32)
            act.sem_inc(at_hi, 1)
            act.wait_ge(route_ready, 1)
            with act.If(nc.scalar.value_load(place_i[0:1, 0:1], min_val=0, max_val=1)):
                for c in range(GC):
                    gate_up_hi(1, c)
                for h in range(DC):
                    down_hi(1, h)
            xsT_out(0)
            slot(0, False, True)
            last = nc.scalar.value_load(last_i[0:1, 1:2], min_val=SLOTS_MIN - 1, max_val=SLOTS - 1)
            with act.Fori(1, last) as s:
                slot(s, True, True)
            slot(last, True, False)
            aT_out(last + 1)
            store(last + 1)

        @block.vector
        def _(dve):
            n_link = 0

            def link(ins):
                nonlocal n_link
                n_link += 1
                ins.then_inc(dch, 1)
                dve.wait_ge(dch, n_link)

            def full(n):
                dve.wait_ge(d_in, n + 1)
                return ps[:, 4 + n % 4, :]

            n_sqrt = 0

            def stats(t, rows_of):
                r = rows(t)
                link(nc.vector.bn_stats(st6[0:r, t, :], rows_of[0:r, t, :]))
                link(nc.vector.bn_aggr(mv[0:r, t, :], st6[0:r, t, :]))

            def rstds(a, b):
                nonlocal n_sqrt
                n_sqrt += 1
                nc.vector.tensor_scalar(ve[:, a:b], mv[:, a:b, 1], EPS, None, ALU.add).then_inc(sq_in, 1)
                dve.wait_ge(sq_out, n_sqrt)
                link(nc.vector.reciprocal(rstd[:, a:b], sd[:, a:b]))

            def normed(to, rows_of, t):
                r = rows(t)
                return nc.vector.tensor_scalar(to, rows_of[0:r, t, :], mv[0:r, t, 0:1], rstd[0:r, t:t + 1],
                                               ALU.subtract, ALU.mult)
            nc.vector.memset(e_int[:, 0, 1, :], 0).then_inc(pads, 1)
            nc.vector.memset(e_int[:, 1, 1, :], NOWHERE).then_inc(pads, 1)
            nc.vector.memset(mv[:, :, :], 1.0).then_inc(dch, 1)
            n_link += 1
            dve.wait_ge(ld_e, 6 * 16)
            link(nc.vector.tensor_copy(e_f[:, :, :, :], e_int[:, :, :, :]))
            for g in range(2):
                link(nc.vector.tensor_reduce(mm2[:, g:g + 1], e_f[:, 1, g, :], AX_X, ALU.min))
                link(nc.vector.tensor_reduce(mm2[:, 2 + g:3 + g], e_f[:, 1, g, :], AX_X, ALU.max))
            dve.wait_ge(consts, 1)
            for i in range(4):
                link(nc.vector.tensor_scalar(e_diag[:, i // 2, i % 2, :], ident[:, :], mm2[:, i:i + 1], None, ALU.mult))
            bank = full(D_EDGE)
            nc.vector.tensor_copy(srcT[:, :], bank[:, 0:2 * P])
            link(nc.vector.tensor_copy(dstT[:, :], bank[:, 2 * P:4 * P]))
            dve.wait_ge(consts, 5)
            link(nc.vector.tensor_scalar(lo_j[:, :], piota[:, :], float(P), None, ALU.mult))
            link(nc.vector.tensor_scalar(hi_j[:, :], piota[:, :], float(P), float(P), ALU.mult, ALU.add))
            bank = full(D_RANGE)
            link(nc.vector.tensor_scalar(erow[0:NT, 0, 0:ET], bank[0:NT, 2 * P:2 * P + ET], lo_j[0:NT, :], None, ALU.is_ge))
            link(nc.vector.scalar_tensor_tensor(out=erow[0:NT, 1, 0:ET], in0=bank[0:NT, 0:ET], scalar=hi_j[0:NT, :],
                                                in1=erow[0:NT, 0, 0:ET], op0=ALU.is_lt, op1=ALU.mult))
            link(nc.vector.scalar_tensor_tensor(out=erow[0:NT, 2, 0:ET], in0=erow[0:NT, 4, 0:ET], scalar=1.0,
                                                in1=erow[0:NT, 1, 0:ET], op0=ALU.add, op1=ALU.mult))
            link(nc.vector.tensor_scalar(erow[0:NT, 3, 0:ET], erow[0:NT, 4, 0:ET], -1.0, float(ET), ALU.mult, ALU.add))
            link(nc.vector.tensor_tensor(erow[0:NT, 3, 0:ET], erow[0:NT, 3, 0:ET], erow[0:NT, 1, 0:ET], ALU.mult))
            link(nc.vector.tensor_reduce(rng[0:NT, 0:1], erow[0:NT, 3, 0:ET], AX_X, ALU.max))
            link(nc.vector.tensor_reduce(rng[0:NT, 1:2], erow[0:NT, 2, 0:ET], AX_X, ALU.max))
            link(nc.vector.tensor_scalar(rng[0:NT, 2:3], rng[0:NT, 0:1], -1.0, float(ET), ALU.mult, ALU.add))
            link(nc.vector.tensor_scalar(rng[0:NT, 2:3], rng[0:NT, 2:3], float(ET - 1), None, ALU.min))
            link(nc.vector.scalar_tensor_tensor(out=rng[0:NT, 3:4], in0=rng[0:NT, 2:3], scalar=1.0,
                                                in1=rng[0:NT, 1:2], op0=ALU.add, op1=ALU.max))
            link(nc.vector.tensor_copy(rng_i[0:NT, 0:2], rng[0:NT, 2:4]))
            link(nc.vector.scalar_tensor_tensor(out=rng_i[0:NT, 2:3], in0=rng[0:NT, 3:4], scalar=256.0,
                                                in1=rng[0:NT, 2:3], op0=ALU.mult, op1=ALU.add))
            link(nc.vector.tensor_tensor(rng_i[0:NT, 3:4], rng_i[0:NT, 1:2], rng_i[0:NT, 0:1], ALU.subtract))
            link(nc.vector.tensor_scalar(rng_i[0:NT, 3:4], rng_i[0:NT, 3:4], LONG_SHIFT, None, ALU.arith_shift_right))
            link(nc.vector.scalar_tensor_tensor(out=rng_i[0:NT, 2:3], in0=rng_i[0:NT, 3:4], scalar=65536.0,
                                                in1=rng_i[0:NT, 2:3], op0=ALU.mult, op1=ALU.add))
            dve.sem_inc(range_ready, 1)
            dve.sem_inc(d_out, 2)
            ranges = [[nc.vector.snap(nc.vector.value_load(rng_i[j:j + 1, i:i + 1], min_val=i, max_val=ET - 1 + i))
                       for i in range(2)] for j in range(NT)]
            made = nc.vector.alloc_register("onehots_made")
            nc.vector.reg_mov(made, 0)
            for j in range(NT):
                with dve.Fori(*ranges[j], RING) as i:
                    k = nc.vector.snap(made, min_val=0, max_val=NT * (ET + RING))
                    for b in range(RING):
                        dve.wait_ge(oh_free, k + (b + 1))
                        nc.vector.tensor_scalar(ring[:, b, 0:N], iota16[:, 0:N], srcT[:, bass.ds(i + b, 1)], None,
                                                ALU.is_equal)
                        nc.vector.tensor_scalar(ring[:, b, NT * P:RW], iota16[:, j * P:(j + 1) * P],
                                                dstT[:, bass.ds(i + b, 1)], None, ALU.is_equal).then_inc(oh_ready, 1)
                    nc.vector.reg_add(made, made, RING)
                if j == 0:
                    dve.wait_ge(ld_x, 32)
                    for t in range(NT):
                        stats(t, xr)
                    rstds(0, NT)
                    nc.vector.scalar_tensor_tensor(out=nmr[:, :], in0=mv[:, :, 0], scalar=-1.0, in1=rstd[:, :],
                                                   op0=ALU.mult, op1=ALU.mult).then_inc(nmr_ready, 1)
                    n_sqrt += 1
                    link(nc.vector.tensor_tensor(ve[:, :], mv[:, :, 1], rstd[:, :], ALU.mult))
                    link(nc.vector.tensor_tensor(ve[:, :], ve[:, :], rstd[:, :], ALU.mult))
                    nc.vector.tensor_scalar(ve[:, :], ve[:, :], EPS, None, ALU.add).then_inc(sq_in, 1)
                if j == 1:
                    dve.wait_ge(sq_out, n_sqrt)
                    nc.vector.reciprocal(rstd2[:, :], sd[:, :]).then_inc(nmr_ready, 1)
            dve.wait_ge(a_out, A_KQ + KD * NC)

            def squares(xT):
                for b in range(KD):
                    ins = nc.vector.tensor_tensor(sq[:, b, :], xT[:, b, :], xT[:, b, :], ALU.mult)
                    link(ins)
                    if b:
                        ins = nc.vector.tensor_tensor(sq[:, 0, :], sq[:, 0, :], sq[:, b, :], ALU.add)
                        if b < KD - 1:
                            link(ins)
                ins.then_inc(sq_ready, 1)
            squares(kT)
            nc.vector.tensor_scalar(xdn[:, 0:NT], full(D_XDK)[:, 0:NT], -0.5, None, ALU.mult).then_inc(d_out, 1)
            dve.wait_ge(a_out, A_KQ + 2 * KD * NC)
            squares(qT)
            dve.wait_ge(ld_rows, 6 * 16)
            for t in range(NT):
                r = rows(t)
                nc.vector.tensor_tensor(v[0:r, t, :], full(D_V + t)[0:r, :], bv_b[0:r, :], ALU.add).then_inc(d_out, 1)
            nc.vector.tensor_scalar(xdn[:, NT:2 * NT], full(D_XDQ)[:, 0:NT], -0.5, None, ALU.mult).then_inc(d_out, 1)
            dve.wait_ge(a_out, A_KP + NT)
            for t in range(1, NT):
                r = rows(t)
                link(nc.vector.tensor_tensor(kpsum[0:r, :], kp[0:r, 0, :] if t == 1 else kpsum[0:r, :], kp[0:r, t, :],
                                             ALU.add))
            dve.sem_inc(ks_ready, 1)
            nc.vector.tensor_copy(ksum, full(D_KSUM)[:, 0:M]).then_inc(d_out, 1)
            dve.wait_ge(d_out, D_KSUM + 1)
            link(nc.vector.memset(den[:, :], 1.0))
            dve.wait_ge(a_out, A_QP + NT)
            for t in range(NT):
                r = rows(t)
                link(nc.vector.tensor_tensor_reduce(out=qk[0:r, :], in0=qp[0:r, t, :], in1=ksum[0:r, :], scale=1.0,
                                                    scalar=0.0, op0=ALU.mult, op1=ALU.add,
                                                    accum_out=den[0:r, t:t + 1]))
            link(nc.vector.tensor_scalar(den[:, :], den[:, :], float(M) * ATT_EPS, None, ALU.add))
            link(nc.vector.reciprocal(rden[:, :], den[:, :]))
            for t in range(NT):
                r = rows(t)
                link(nc.vector.scalar_tensor_tensor(out=v[0:r, t, :], in0=full(D_Y + t)[0:r, :], scalar=rden[0:r, t:t + 1],
                                                    in1=v[0:r, t, :], op0=ALU.mult, op1=ALU.add))
                dve.sem_inc(d_out, 1)
                nc.vector.tensor_tensor(v[0:r, t, :], v[0:r, t, :], bo_b[0:r, :], ALU.add).then_inc(y_ready, 1)
                dve.wait_ge(y_ready, t + 1)
                stats(t, v)
                if t % TPC == TPC - 1 or t == NT - 1:
                    a = t - t % TPC
                    rstds(a, t + 1)
                    for u in range(a, t + 1):
                        normed(yhat[0:rows(u), u, :], v, u).then_inc(yh_ready, 1)
            link(nc.vector.memset(logit[:, :, :], 0.0))
            for t in range(NT + 2):
                if t < NT:
                    r = rows(t)
                    bank = full(D_X1[t])
                    dve.wait_ge(xy_ready, t + 1)
                    nc.vector.tensor_tensor(xr[0:r, t, :], bank[0:r, :], xr[0:r, t, :], ALU.add).then_inc(d_out, 1)
                    dve.wait_ge(d_out, D_X1[t] + 1)
                    stats(t, xr)
                    rstds(t, t + 1)
                    if t >= 2:
                        dve.wait_ge(a_in, A_X2T + t - 1)
                        dve.wait_ge(st_x2[t % 2], 16 * (t // 2))
                    normed(x2[0:r, t % 2, :], xr, t).then_inc(xn2_ready, 1)
                if t >= 2:
                    r = rows(t - 2)
                    nc.vector.tensor_tensor(logit[0:r, t - 2, :], full(D_LOG[t - 2])[0:r, 0:NX], rb_b[0:r, :],
                                            ALU.add).then_inc(d_out, 1)
                    dve.wait_ge(d_out, D_LOG[t - 2] + 1)
                    if t == 2:
                        dve.wait_ge(xy_ready, NT)
                    link(nc.vector.max(mx8[:, t - 2, :], logit[:, t - 2, :]))
                    link(nc.vector.max_index(mi8[:, t - 2, :], mx8[:, t - 2, :], logit[:, t - 2, :]))
            dve.sem_inc(slot_done, 1)
            dve.sem_inc(at_out, 1)
            dve.sem_inc(gu_out, 1)
            dve.wait_ge(consts, 9)

            def across(ap, n):
                return ap.unsqueeze(len(ap.shape)).to_broadcast([*ap.shape, n])

            def down_by(ap, *n):
                for _ in n:
                    ap = ap.unsqueeze(1)
                return ap.to_broadcast([P, *n, ap.shape[-1]])
            nc.vector.tensor_tensor(ex2[:, 0, :], mx8[:, :, 1], mx8[:, :, 0], ALU.subtract).then_inc(exp_in, 1)
            nc.vector.tensor_scalar(lo_j[:, :], piota[:, :], float(LAST), None, ALU.is_lt)
            nc.vector.tensor_scalar(behind, piota[:, :], float(LAST), 64.0 * P, ALU.is_ge, ALU.mult)
            link(nc.vector.tensor_scalar(mif[:, :, :], mi8[:, :, :], 1.0, None, ALU.add))
            link(nc.vector.tensor_tensor(oh, down_by(iota1, TOP, NT),
                                         across(mif[:, :, 0:TOP].rearrange("p t k -> p k t"), NX), ALU.is_equal))
            link(nc.vector.tensor_scalar(oh[:, :, NT - 1, :], oh[:, :, NT - 1, :], lo_j[:, 0:1], None, ALU.mult))
            nc.vector.tensor_tensor(msk_b.rearrange("p (t e) -> p t e", t=NT), oh[:, 0, :, :], oh[:, 1, :, :],
                                    ALU.add).then_inc(msk_ready, 1)
            dve.wait_ge(exp_out, 1)
            link(nc.vector.tensor_scalar(den[:, :], ex2[:, 1, :], 1.0, None, ALU.add))
            link(nc.vector.reciprocal(wgt[:, 0, :], den[:, :]))
            nc.vector.tensor_tensor(wgt[:, 1, :], wgt[:, 0, :], ex2[:, 1, :], ALU.mult)
            bank = full(D_RANK)
            link(nc.vector.tensor_scalar(cnt_i, bank[:, NT * NX:(NT + 1) * NX], float(P - 1), None, ALU.add))
            link(nc.vector.tensor_scalar(cnt_i, cnt_i, 7, None, ALU.arith_shift_right))
            link(nc.vector.tensor_copy(cnt, cnt_i))
            link(nc.vector.tensor_tensor_scan(ends[:, 1, :], ones[:, 0:NX], cnt, 0.0, ALU.mult, ALU.add))
            link(nc.vector.tensor_tensor(base, ends[:, 1, :], cnt, ALU.subtract))
            link(nc.vector.tensor_scalar(base, base, float(P), None, ALU.mult))
            link(nc.vector.tensor_tensor(rank, t3(bank[:, 0:NT * NX], NT), down_by(base, NT), ALU.add))
            link(nc.vector.tensor_tensor(oh, oh, rank.unsqueeze(1).to_broadcast([P, TOP, NT, NX]), ALU.mult))
            link(nc.vector.tensor_reduce(posf, oh.rearrange("p k t e -> p (k t) e"), AX_X, ALU.add))
            link(nc.vector.tensor_scalar(t3(posf, TOP)[:, :, NT - 1], t3(posf, TOP)[:, :, NT - 1], behind, None, ALU.add))
            link(nc.vector.tensor_copy(pos_i.rearrange("p k t -> p (k t)"), posf))
            link(nc.vector.tensor_scalar(pa_i, pos_i.rearrange("p k t -> p (k t)"), 7, None, ALU.arith_shift_right))
            nc.vector.tensor_scalar(pb_i, pos_i.rearrange("p k t -> p (k t)"), P - 1, None, ALU.bitwise_and)\
                .then_inc(dch, 1)
            n_link += 1
            link(nc.vector.tensor_copy(pa_f, pa_i))
            link(nc.vector.tensor_copy(pb_f, pb_i))
            link(nc.vector.tensor_tensor(slot_1, down_by(iota_s, KT), across(pa_f, SLOTS), ALU.is_equal))
            nc.vector.tensor_tensor(slot_a[:, :, 0, :], slot_1, across(tile_no, SLOTS), ALU.mult).then_inc(slot_ready, 1)
            nc.vector.tensor_scalar(slot_a[:, :, 1, :], slot_1, piota[:, 0:1], None, ALU.mult).then_inc(slot_ready, 1)
            for k in range(TOP):
                nc.vector.tensor_tensor(slot_b[:, k * NT:(k + 1) * NT, :], down_by(iota_c, NT),
                                        across(pb_f[:, k * NT:(k + 1) * NT], P), ALU.is_equal).then_inc(slot_ready, 1)
            link(nc.vector.tensor_scalar(has, cnt, 1.0, None, ALU.min))
            link(nc.vector.memset(has[:, 0:1], 1.0))
            link(nc.vector.tensor_tensor_scan(ends[:, 0, :], ones[:, 0:NX], has, 0.0, ALU.mult, ALU.add))
            link(nc.vector.tensor_scalar(last_f, ends[:, :, NX - 1], -1.0, None, ALU.add))
            nc.vector.tensor_copy(last_i[:, :], last_f)
            link(nc.vector.tensor_tensor(cmp_s, across(iota_s, NX), down_by(ends[:, 1, :], SLOTS), ALU.is_ge))
            link(nc.vector.tensor_tensor(cmp_s, cmp_s, down_by(has, SLOTS), ALU.mult))
            link(nc.vector.tensor_reduce(place_f, cmp_s, AX_X, ALU.add))
            link(nc.vector.tensor_scalar(place_f, place_f, last_f[:, 0:1], None, ALU.min))
            nc.vector.tensor_copy(place_i[:, :], place_f)
            link(nc.vector.memset(change_i[:, :], 0))
            link(nc.vector.tensor_tensor(change_i[:, 0:SLOTS - 1], place_f[:, 1:SLOTS], place_f[:, 0:SLOTS - 1],
                                         ALU.subtract))
            link(nc.vector.scalar_tensor_tensor(out=num_end[:, 0, :], in0=iota1, scalar=-1.0, in1=has,
                                                op0=ALU.add, op1=ALU.mult))
            link(nc.vector.tensor_tensor(num_end[:, 1, :], ends[:, 1, :], has, ALU.mult))
            link(nc.vector.tensor_tensor(cmp_u, across(iota1, NX), down_by(ends[:, 0, :], NX), ALU.is_equal))
            for i in range(2):
                link(nc.vector.tensor_tensor(num_end_of[:, i, :, :], cmp_u, down_by(num_end[:, i, :], NX), ALU.mult))
            link(nc.vector.tensor_reduce(used_f, num_end_of, AX_X, ALU.add))
            link(nc.vector.memset(used_end_i[:, 0:1], 0))
            nc.vector.tensor_copy(used_i[:, :], used_f[:, 0, :])
            link(nc.vector.tensor_copy(used_end_i[:, 1:NX + 1], used_f[:, 1, :]))
            bank = full(D_SLOT)
            link(nc.vector.tensor_copy(row_f, bank[:, SLOTS:2 * SLOTS]))
            link(nc.vector.scalar_tensor_tensor(out=idx_i[:, :], in0=bank[:, 0:SLOTS], scalar=float(P),
                                                in1=row_f, op0=ALU.mult, op1=ALU.add))
            dve.sem_inc(route_ready, 1)

            gate = ps[:, 0:2, :].rearrange("p a b -> p (a b)")
            up = ps[:, 2:4, :].rearrange("p a b -> p (a b)")

            def place_of(s):
                return nc.vector.snap(nc.vector.value_load(place_i[0:1, bass.ds(s, 1)] if not isinstance(s, int) else
                                                           place_i[0:1, s:s + 1], min_val=0, max_val=NX - 1))

            def gate_up_lo(i, c):
                dve.wait_ge(gu_hi, i * GC + (c + 1))
                nc.vector.tensor_tensor(w_sp[:, c, 1, :], raw_gu[c % 2], w_sp[:, c, 0, :].bitcast(F32), ALU.subtract)\
                    .then_inc(gu_split, 1)

            def down_lo(i, h):
                dve.wait_ge(d_hi, i * DC + (h + 1))
                nc.vector.tensor_tensor(w_sp[:, GC + h, 1, :], raw_d[h], w_sp[:, GC + h, 0, :].bitcast(F32),
                                        ALU.subtract).then_inc(d_split, 1)

            def xsT_lo(n):
                dve.wait_ge(xt_hi, n)
                nc.vector.tensor_tensor(xT_sp[:, 1, :], ps[:, 7, :], xT_sp[:, 0, :].bitcast(F32), ALU.subtract)\
                    .then_inc(xt_out, 1)

            def aT_lo(n):
                for h in range(2):
                    dve.wait_ge(at_hi, 2 * n + h)
                    nc.vector.tensor_tensor(aT_sp[:, 1, h * BANK:(h + 1) * BANK], ps[:, 4 + h, :],
                                            aT_sp[:, 0, h * BANK:(h + 1) * BANK].bitcast(F32), ALU.subtract)\
                        .then_inc(at_out, 1)

            def activate(s, prev, nxt):
                place = place_of(s)
                if nxt:
                    changes = nc.vector.value_load(change_i[0:1, bass.ds(s, 1)] if prev else change_i[0:1, 0:1],
                                                   min_val=0, max_val=1)
                    with dve.If(changes):
                        for c in range(2):
                            dve.wait_ge(gu_full, s * GC + (c + 1))
                            gate_up_lo(place + 1, c)
                bias = nc.vector.snap((place % 2) * BIAS_STEP)
                dve.wait_ge(b_ld, place * 32 + 32)
                dve.wait_ge(gu_full, s * GC + 2)
                nc.vector.tensor_tensor(g_s, gate, wa[:, bass.ds(bias + BIAS0, I)], ALU.add).then_inc(g_out, 1)
                if prev:
                    aT_lo(s)
                dve.wait_ge(gu_full, s * GC + 4)
                if prev:
                    dve.wait_ge(a_ready, s)
                nc.vector.scalar_tensor_tensor(out=u_s, in0=up, scalar=1.0, in1=wa[:, bass.ds(bias + BIAS0 + I, I)],
                                               op0=ALU.add, op1=ALU.add).then_inc(gu_out, 1)
                if nxt:
                    xsT_lo(s + 2)
                dve.wait_ge(sig_out, s + 1)
                nc.vector.tensor_tensor(sig_s, g_s, sig_s, ALU.mult).then_inc(gu_out, 1)
                dve.wait_ge(gu_out, 2 * s + 3)
                if prev:
                    dve.wait_ge(at_full, 2 * s + 1)
                nc.vector.tensor_tensor(a_s, u_s, sig_s, ALU.mult).then_inc(a_ready, 1)
                if nxt:
                    with dve.If(changes):
                        for c in range(2, GC):
                            gate_up_lo(place + 1, c)

            def finish(n):
                h = nc.vector.snap(place_of(n - 1) % 2)
                dve.wait_ge(dn_full, n)
                dve.wait_ge(y_st, 16 * n)
                nc.vector.tensor_tensor(r1[:, bass.ds(((n - 1) % 2) * D, D)], ps[:, 6, :],
                                        bd_b[:, bass.ds(h * D, D)], ALU.add).then_inc(slot_done, 1)

            def change_down(s):
                changed = nc.vector.value_load(change_i[0:1, bass.ds(s - 1, 1)], min_val=0, max_val=1)
                i = place_of(s)
                with dve.If(changed):
                    for h in range(DC):
                        down_lo(i, h)
            with dve.If(nc.vector.value_load(place_i[0:1, 0:1], min_val=0, max_val=1)):
                for c in range(GC):
                    gate_up_lo(1, c)
                for h in range(DC):
                    down_lo(1, h)
            xsT_lo(1)
            last = nc.vector.value_load(last_i[0:1, 1:2], min_val=SLOTS_MIN - 1, max_val=SLOTS - 1)
            activate(0, False, True)
            with dve.Fori(1, last) as s:
                activate(s, True, True)
                finish(s)
                change_down(s)
            activate(last, True, False)
            finish(last)
            change_down(last)
            aT_lo(last + 1)
            finish(last + 1)

            for t in range(NT):
                r, c = rows(t), t % CB
                dve.wait_ge(cg[c], 32 * (t // CB + 1))
                if t >= CB:
                    dve.wait_ge(o_st[c], 16 * (t // CB))
                link(nc.vector.scalar_tensor_tensor(out=xr[0:r, t, :], in0=yg[0:r, c, 0, :], scalar=wgt[0:r, 0, t:t + 1],
                                                    in1=xr[0:r, t, :], op0=ALU.mult, op1=ALU.add))
                nc.vector.scalar_tensor_tensor(out=ob[0:r, c, :], in0=yg[0:r, c, 1, :], scalar=wgt[0:r, 1, t:t + 1],
                                               in1=xr[0:r, t, :], op0=ALU.mult, op1=ALU.add).then_inc(o_ready, 1)

        @block.tensor
        def _(pe):
            mm, tr = nc.tensor.matmul, nc.tensor.transpose

            def a_tile(n):
                if n >= 4:
                    pe.wait_ge(a_out, n - 3)
                return ps[:, n % 4, :]

            def d_tile(n):
                if n >= 4:
                    pe.wait_ge(d_out, n - 3)
                return ps[:, 4 + n % 4, :]

            def to_cols(n0, rows_of, ready, nb):
                for b in range(nb):
                    for c, (a, m) in enumerate(COLS):
                        bank = a_tile(n0 + b * NC + c)
                        for t in range(TPC * c, min(TPC * c + TPC, NT)):
                            ready(t)
                            r = rows(t)
                            q = tr(bank[:, (t - TPC * c) * P:(t - TPC * c) * P + r], rows_of[0:r, t, b * P:(b + 1) * P],
                                   ident[0:r, 0:r])
                        q.then_inc(a_in, 1)

            def layer(n0, wt, xT, nk, col0=0):
                for b in range(KD):
                    for c, (a, m) in enumerate(COLS):
                        bank = a_tile(n0 + b * NC + c)
                        for k in range(nk):
                            q = mm(bank[:, 0:m], wt[:, k, col0 + b * P:col0 + (b + 1) * P], xT[:, k, a:a + m],
                                   start=(k == 0), stop=(k == nk - 1))
                        q.then_inc(a_in, 1)
            pe.wait_ge(consts, 1)
            pe.wait_ge(dch, 2)
            bank = d_tile(D_EDGE)
            for i in range(4):
                q = tr(bank[:, i * P:(i + 1) * P], e_f[:, i // 2, i % 2, :], ident[:, :])
            q.then_inc(d_in, 1)
            pe.wait_ge(dch, 10)
            pe.wait_ge(consts, 2)
            bank = d_tile(D_RANGE)
            for i in range(4):
                q = mm(bank[0:NT, i * P:(i + 1) * P], ones[:, 0:NT], e_diag[:, i // 2, i % 2, :], start=True, stop=True)
            q.then_inc(d_in, 1)
            pe.wait_ge(ld_vec, 7 * 16)
            tr(a_tile(A_VEC)[:, 0:8 * KD], vrow[:, :], ident[0:8 * KD, 0:8 * KD]).then_inc(a_in, 1)
            pe.wait_ge(ld_w, 16)
            for m in range(KM):
                bank = a_tile(A_WT + m)
                for k in range(KD):
                    q = tr(bank[:, k * P:(k + 1) * P], w_raw[:, m, k * P:(k + 1) * P], ident[:, :])
                q.then_inc(a_in, 1)

            pe.wait_ge(consts, 5)
            pe.wait_ge(range_ready, 1)
            pe.wait_ge(a_out, A_Z)
            pe.wait_ge(d_out, D_RANGE + 1)
            pe.sem_inc(oh_free, RING)

            def range_of(j):
                word = nc.tensor.snap(nc.tensor.value_load(rng_i[j:j + 1, 2:3], min_val=256,
                                                           max_val=((ET >> LONG_SHIFT) + 1 << 16) - 1))
                nc.tensor.reg_add(long_ranges, long_ranges, nc.tensor.snap(word >> 16))
                return (nc.tensor.snap(word % 256, min_val=0, max_val=ET - 1),
                        nc.tensor.snap((word >> 8) % 256, min_val=1, max_val=ET))
            long_ranges = nc.tensor.alloc_register("long_ranges")
            nc.tensor.reg_mov(long_ranges, 0)
            ahead = range_of(0)
            used = nc.tensor.alloc_register("onehots_used")
            nc.tensor.reg_mov(used, 0)

            def turn_counts(j):
                for g in range(NC):
                    n = NC * j + g
                    pe.wait_ge(c_out, NC * j + g + 1)
                    if n >= 2:
                        before = n - 2
                        pe.wait_ge(ct_out, (NC + 1) * (before // NC) + (before % NC + 1 if before % NC < NC - 1 else NC + 1))
                    bank = ps[:, 6 + n % 2, :]
                    for i in range(TPC * g, min(TPC * g + TPC, NT)):
                        r = rows(i)
                        q = tr(bank[0:r, (i - TPC * g) * P:(i - TPC * g + 1) * P], c_stage[:, i * P:i * P + r], ident[:, :])
                    q.then_inc(ct_full, 1)
            for j in range(NT):
                if j >= 2:
                    pe.wait_ge(c_out, NC * (j - 1))
                banks = [ps[:, 3 * (j % 2) + c, 0:m] for c, (a, m) in enumerate(COLS)]
                for c, (a, m) in enumerate(COLS):
                    o = (NT - 1 - j) * P + a
                    mm(banks[c], ident_b[:, :], e_id[:, o:o + m], start=True, stop=False, skip_group_check=True)
                edge_range, ahead = ahead, range_of(j + 1) if j < NT - 1 else None
                with pe.Fori(*edge_range, RING) as i:
                    k = nc.tensor.snap(used, min_val=0, max_val=NT * (ET + RING))
                    for b in range(RING):
                        pe.wait_ge(oh_ready, k + (b + 1))
                        for c, (a, m) in enumerate(COLS):
                            q = mm(banks[c], ring[:, b, NT * P:RW], ring[:, b, a:a + m],
                                   start=False, stop=True, skip_group_check=True)
                        q.then_inc(oh_free, 1)
                    nc.tensor.reg_add(used, used, RING)
                pe.wait_ge(oh_free, nc.tensor.snap(used, min_val=1, max_val=NT * (ET + RING)) + RING)
                pe.sem_inc(c_full, 1)
                if j >= 1:
                    turn_counts(j - 1)
            turn_counts(NT - 1)

            pe.wait_ge(ct_out, (NC + 1) * NT)
            pe.wait_ge(xl_ready, NT)

            def neighbours(first, second, counts):
                for b in range(KD):
                    for c, (a, m) in enumerate(COLS):
                        bank = a_tile(A_Z + b * NC + c)
                        for i in range(NT):
                            r = rows(i)
                            for part in (first, second):
                                q = mm(bank[:, 0:m], part[0:r, i, b * P:(b + 1) * P], counts[0:r, i, a:a + m],
                                       start=(i == 0 and part is first), stop=(i == NT - 1 and part is second))
                        q.then_inc(a_in, 1)
            with pe.If_eq(long_ranges, 0):
                neighbours(xh, xl, cT_r)
            with pe.If_ne(long_ranges, 0):
                neighbours(xh.bitcast(F32), xl.bitcast(F32), cT)
            to_cols(A_XMT, xm, lambda t: pe.wait_ge(xm_ready, t + 1), KD)
            pe.wait_ge(a_out, A_Z + KD * NC)
            pe.wait_ge(ld_gw1, 16)
            layer(A_R, gw1_s, zT, KD)
            pe.wait_ge(ld_kqv, 16)
            layer(A_KQ, kqv_s, xmT, KD)
            layer(A_KQ + KD * NC, kqv_s, xmT, KD, D)

            def squares(n, count):
                pe.wait_ge(sq_ready, count)
                bank = d_tile(n)
                for t in range(NT):
                    r = rows(t)
                    q = mm(bank[0:r, t:t + 1], sq[:, 0, t * P:t * P + r], ones[:, 0:1], start=True, stop=True)
                q.then_inc(d_in, 1)
            squares(D_XDK, 1)
            for t in range(NT):
                r = rows(t)
                bank = d_tile(D_V + t)
                for k in range(KD):
                    q = mm(bank[0:r, :], xmT[:, k, t * P:t * P + r], kqv_s[:, k, 2 * D:3 * D],
                           start=(k == 0), stop=(k == KD - 1))
                q.then_inc(d_in, 1)
            squares(D_XDQ, 2)
            for n0, xT in ((A_KP, kT), (A_QP, qT)):
                for t in range(NT):
                    r = rows(t)
                    bank = a_tile(n0 + t)
                    for k in range(KD):
                        q = mm(bank[0:r, 0:M], xT[:, k, t * P:t * P + r], wT[:, k, :], start=(k == 0), stop=(k == KD - 1))
                    q.then_inc(a_in, 1)
            to_cols(A_QPT, qp, lambda t: pe.wait_ge(a_out, A_QP + t + 1), KM)
            pe.wait_ge(ks_ready, 1)
            mm(d_tile(D_KSUM)[:, 0:M], ones[:, :], kpsum, start=True, stop=True).then_inc(d_in, 1)
            pe.wait_ge(d_out, D_V + NT)
            for b in range(KM):
                bank = a_tile(A_KPTV + b)
                for t in range(NT):
                    r = rows(t)
                    q = mm(bank, kp[0:r, t, b * P:(b + 1) * P], v[0:r, t, :], start=(t == 0), stop=(t == NT - 1))
                q.then_inc(a_in, 1)
            pe.wait_ge(a_out, A_QPT + KM * NC)
            pe.wait_ge(a_out, A_KPTV + KM)
            layer(A_ATT, kptvT, qpT, KM)
            pe.wait_ge(ld_ow1w2, 3 * 16)
            pe.wait_ge(a_out, A_ATT + KD * NC)
            for t in range(NT):
                r = rows(t)
                bank = d_tile(D_Y + t)
                for k in range(KD):
                    q = mm(bank[0:r, :], attT[:, k, t * P:t * P + r], wo_s[:, k, :], start=(k == 0), stop=(k == KD - 1))
                q.then_inc(d_in, 1)
            to_cols(A_H, yhat, lambda t: pe.wait_ge(yh_ready, t + 1), KD)
            pe.wait_ge(a_out, A_H + KD * NC)
            layer(A_G, w1_s, hT, KD)
            pe.wait_ge(a_out, A_G + KD * NC)
            pe.wait_ge(ld_gw2, 16)
            for t in range(NT + 2):
                if t < NT:
                    r = rows(t)
                    bank = d_tile(D_X1[t])
                    for k in range(KD):
                        mm(bank[0:r, :], gT[:, k, t * P:t * P + r], w2_s[:, k, :], start=(k == 0), stop=False)
                    for k in range(KD):
                        q = mm(bank[0:r, :], rT[:, k, t * P:t * P + r], gw2_s[:, k, :], start=False, stop=(k == KD - 1))
                    q.then_inc(d_in, 1)
                if 1 <= t <= NT:
                    u = t - 1
                    r = rows(u)
                    pe.wait_ge(xn2_ready, u + 1)
                    bank = a_tile(A_X2T + u)
                    for k in range(KD):
                        q = tr(bank[:, k * P:k * P + r], x2[0:r, u % 2, k * P:(k + 1) * P], ident[0:r, 0:r])
                    q.then_inc(a_in, 1)
                if t >= 2:
                    u = t - 2
                    r = rows(u)
                    pe.wait_ge(a_out, A_X2T + u + 1)
                    bank = d_tile(D_LOG[u])
                    for k in range(KD):
                        q = mm(bank[0:r, 0:NX], x2T[:, u % 2, k, 0:r], rw_s[:, k, :], start=(k == 0), stop=(k == KD - 1))
                    q.then_inc(d_in, 1)
            pe.wait_ge(msk_ready, 1)
            bank = d_tile(D_RANK)
            for i in range(NT):
                mm(bank[:, i * NX:NT * NX], ones_b[:, :] if i else tri_b[:, :], msk_b[:, 0:(NT - i) * NX],
                   start=(i == 0), stop=False, skip_group_check=True)
            for i in range(NT):
                q = mm(bank[:, NT * NX:(NT + 1) * NX], ones_b[:, :], msk_b[:, i * NX:(i + 1) * NX],
                       start=(i == 0), stop=(i == NT - 1), skip_group_check=True)
            q.then_inc(d_in, 1)
            bank = d_tile(D_SLOT)
            for n in range(KT):
                if n % NT == 0:
                    pe.wait_ge(slot_ready, 3 + n // NT)
                q = mm(bank[:, 0:2 * SLOTS], slot_b[:, n, :], slot_a[:, n, :, :].rearrange("p w s -> p (w s)"),
                       start=(n == 0), stop=(n == KT - 1))
            q.then_inc(d_in, 1)

            pe.wait_ge(route_ready, 1)

            def place_of(s):
                return nc.tensor.snap(nc.tensor.value_load(place_i[0:1, bass.ds(s, 1)] if not isinstance(s, int) else
                                                           place_i[0:1, s:s + 1], min_val=0, max_val=NX - 1))

            def turn_xs(n):
                pe.wait_ge(gath, 16 * n)
                for k in range(KD):
                    q = tr(ps[:, 7, k * P:(k + 1) * P], xs[:, k * P:(k + 1) * P], ident[:, :])
                q.then_inc(xt_full, 1)

            def split_product(bank, rows_sp, at, c, first, last):
                for k in range(KD):
                    for n, (a, b) in enumerate(((0, 0), (0, 1), (1, 0))):
                        q = mm(bank, rows_sp[:, a, at + k * P:at + (k + 1) * P],
                               w_sp[:, c, b, k * BANK:(k + 1) * BANK],
                               start=(first and k == 0 and n == 0), stop=(last and k == KD - 1 and n == 2))
                return q

            def gate_up(s, place, chunks, first=False):
                for c in chunks:
                    if c == 0:
                        pe.wait_ge(xt_out, s + 1)
                    if c % 2 == 0 and not first:
                        pe.wait_ge(*((g_out, s) if c == 0 else (gu_out, 2 * s)))
                    pe.wait_ge(gu_split, place * GC + (c + 2))
                    split_product(ps[:, c, :], xT_sp, 0, c, True, True).then_inc(gu_full, 1)

            def turn_act(n):
                pe.wait_ge(a_ready, n)
                for h in range(2):
                    for k in range(4):
                        i = 4 * h + k
                        q = tr(ps[:, 4 + h, k * P:(k + 1) * P], a_s[:, i * P:(i + 1) * P], ident[:, :])
                    q.then_inc(at_full, 1)

            def down(n):
                place = place_of(n - 1)
                pe.wait_ge(slot_done, n)
                for h in range(DC):
                    pe.wait_ge(d_split, place * DC + (DC + h + 1))
                    pe.wait_ge(at_out, 2 * n + h)
                    q = split_product(ps[:, 6, :], aT_sp, h * BANK, GC + h, h == 0, h == DC - 1)
                q.then_inc(dn_full, 1)
            pe.sem_inc(at_full, 1)
            turn_xs(1)
            gate_up(0, place_of(0), range(GC), True)
            turn_xs(2)
            last = nc.tensor.value_load(last_i[0:1, 1:2], min_val=SLOTS_MIN - 1, max_val=SLOTS - 1)
            with pe.Fori(1, last) as s:
                place = place_of(s)
                gate_up(s, place, range(GC - 1))
                turn_act(s)
                turn_xs(s + 2)
                gate_up(s, place, [GC - 1])
                down(s)
            gate_up(last, place_of(last), range(GC))
            turn_act(last)
            down(last)
            turn_act(last + 1)
            down(last + 1)


_INS = ['x', 'src', 'dst', 'L0_gnn_W1', 'L0_gnn_b1', 'L0_gnn_W2', 'L0_gnn_b2', 'L0_mix_w', 'L0_mix_Wkqv',
        'L0_mix_bkqv', 'L0_mix_Wo', 'L0_mix_bo', 'L0_mix_W1', 'L0_mix_b1', 'L0_mix_W2', 'L0_mix_b2', 'L0_mix_g1',
        'L0_mix_be1', 'L0_mix_g2', 'L0_mix_be2', 'L0_ffn_router_w', 'L0_ffn_router_b', 'L0_ffn_gate_up_proj',
        'L0_ffn_gate_up_proj_bias', 'L0_ffn_down_proj', 'L0_ffn_down_proj_bias']
_OUTS = [((1250, 512), 'float32')]


def kernel(**inputs):
    import numpy as _np
    import concourse.bacc as _bacc
    from concourse import mybir as _mybir
    from concourse.bass_utils import run_bass_kernel_spmd as _run

    nc = _bacc.Bacc("TRN2", target_bir_lowering=False, num_devices=1)
    arrays, args = {}, []
    for name in _INS:
        a = _np.ascontiguousarray(inputs[name])
        arrays[f"in_{name}_dram"] = a
        args.append(nc.dram_tensor(f"in_{name}_dram", a.shape, _mybir.dt.from_np(a.dtype), kind="ExternalInput").ap())
    for i, (shape, dtype) in enumerate(_OUTS):
        dt = _mybir.dt.from_np(_np.dtype(dtype))
        args.append(nc.dram_tensor(f"out_{i}_dram", shape, dt, kind="ExternalOutput").ap())
    bass_gps_gnn_performer_moe(nc, *args)
    r = _run(nc, [arrays], core_ids=[0])
    got = tuple(r.results[0][f"out_{i}_dram"] for i in range(len(_OUTS)))
    return got[0]
```

```python
from contextlib import ExitStack

import concourse.bass as bass
from concourse import mybir

ALU = mybir.AluOpType
ACT = mybir.ActivationFunctionType
AX_X = mybir.AxisListType.X
F32 = mybir.dt.float32
F32R = mybir.dt.float32r
BF16 = mybir.dt.bfloat16
I32 = mybir.dt.int32
U32 = mybir.dt.uint32
I16 = mybir.dt.int16
P = 128
BANK = 512
EPS = 1e-5
ATT_EPS = 1e-8


def bass_gps_gnn_performer_moe(nc, x, src, dst, gw1, gb1, gw2, gb2, w, wkqv, bkqv, wo, bo, w1, b1, w2, b2,
                               g1, be1, g2, be2, rw, rb, wgu, bgu, wd, bd, out):
    N, D = x.shape
    E = src.shape[0]
    M = w.shape[0]
    NX = rw.shape[1]
    I = wd.shape[1]
    TOP = 2
    NT = -(-N // P)
    KD = D // P
    KM = M // P
    KI = I // P
    LAST = N - (NT - 1) * P
    ET = -(-E // P)
    EFULL = E // P
    EREST = E - EFULL * P
    LONG_SHIFT = 5
    assert (P << LONG_SHIFT) <= 1 << 12
    NOWHERE = 2047
    SLOTS = (TOP * N + NX * (P - 1)) // P
    SLOTS_MIN = -(-TOP * N // P)
    RING = 6
    assert D == BANK and EREST and ET + RING - 1 <= 2 * P and M % P == 0

    def rows(t):
        return P if t < NT - 1 else LAST

    COLS = [(a, min(BANK, N - a)) for a in range(0, N, BANK)]
    NC = len(COLS)
    TPC = BANK // P

    a_n = 0

    def a_stage(n):
        nonlocal a_n
        a_n += n
        return a_n - n
    A_VEC = a_stage(1)
    A_WT = a_stage(KM)
    A_Z = a_stage(KD * NC)
    A_XMT = a_stage(KD * NC)
    A_KQ = a_stage(2 * KD * NC)
    A_KP = a_stage(NT)
    A_QP = a_stage(NT)
    A_QPT = a_stage(KM * NC)
    A_R = a_stage(KD * NC)
    A_KPTV = a_stage(KM)
    A_ATT = a_stage(KD * NC)
    A_H = a_stage(KD * NC)
    A_G = a_stage(KD * NC)
    A_X2T = a_stage(NT)
    A_END = a_n
    D_EDGE, D_RANGE, D_XDK, D_V = 0, 1, 2, 3
    D_XDQ = D_V + NT
    D_KSUM = D_XDQ + 1
    D_Y = D_KSUM + 1
    d_last = D_Y + NT
    D_X1, D_LOG = {}, {}
    for t in range(NT + 2):
        if t < NT:
            D_X1[t] = d_last
            d_last += 1
        if t >= 2:
            D_LOG[t - 2] = d_last
            d_last += 1
    D_RANK = d_last
    D_SLOT = D_RANK + 1

    with ExitStack() as ctx:
        def sb(name, shape, dt=F32):
            return ctx.enter_context(nc.sbuf_tensor(name, shape, dt))

        def sem(name):
            return ctx.enter_context(nc.semaphore(name))

        xr = sb("x_rows", [P, NT, D])
        r1_at = nc.sbuf_base
        r1 = sb("r1", [P, NT * D])
        HALF = 2 * KD * N + NT * M
        assert NT * N <= HALF
        XL = -(-NT * N // 8) * 8
        B2, B4 = HALF, max(HALF + KD * N, XL + NT * D)
        B5 = B4 + 2 * NT * M
        arena_at = nc.sbuf_base
        arena = sb("arena", [P, B5 + NT * D])
        CW = KD * BANK
        GC, DC = 2 * I // BANK, KI // KD
        assert D == BANK and KD * BANK == CW and 2 * (GC + DC) * CW + 2 * I + 2 * D <= B5 + NT * D
        w_sp = nc.alloc_sbuf_tensor_at("weights_split", [P, GC + DC, 2, CW], F32R, offset=arena_at)
        aT_sp = nc.alloc_sbuf_tensor_at("act_split", [P, 2, I], F32R, offset=arena_at + 8 * (GC + DC) * CW)
        xT_sp = nc.alloc_sbuf_tensor_at("rows_split", [P, 2, D], F32R, offset=arena_at + 8 * (GC + DC) * CW + 8 * I)
        wa_at = nc.sbuf_base
        wa = sb("weights", [P, 5 * KD * D + KD * M + 3 * D + 4 * P])

        def t3(ap, n):
            return ap.rearrange("p (a b) -> p a b", a=n)

        v = t3(r1[:, :], NT)
        cT = t3(arena[:, 0:NT * N], NT)
        cT_r = nc.alloc_sbuf_tensor_at("countsT_short", [P, NT, N], F32R, offset=arena_at)
        xh = nc.alloc_sbuf_tensor_at("xn_leading", [P, NT, D], F32R, offset=r1_at)
        xl = nc.alloc_sbuf_tensor_at("xn_rest", [P, NT, D], F32R, offset=arena_at + 4 * XL)
        f_sp = nc.alloc_sbuf_tensor_at("features_split", [P, 2, KD, N], F32R, offset=arena_at)
        kT = t3(arena[:, B2:B2 + KD * N], KD)
        qT = t3(arena[:, B5:B5 + KD * N], KD)
        kp = t3(arena[:, 2 * KD * N:HALF], NT)
        attT = t3(arena[:, 0:KD * N], KD)
        kptvT = t3(arena[:, KD * N:KD * N + KM * D], KM)
        yhat = t3(arena[:, B5:B5 + NT * D], NT)
        o = KM * D
        e_int = arena[:, o:o + 4 * P].bitcast(I32).rearrange("p (a g c) -> p a g c", a=2, g=2)
        o += 4 * P
        e_f = arena[:, o:o + 4 * P].rearrange("p (a g c) -> p a g c", a=2, g=2)
        o += 4 * P
        e_diag = arena[:, o:o + 4 * P].rearrange("p (a g c) -> p a g c", a=2, g=2)
        f_whole = t3(arena[:, B2:B2 + KD * N], KD)
        zero = arena[:, B2:B2 + D]
        gT = f_whole
        zT = t3(arena[:, B4:B4 + KD * N], KD)
        rT = zT
        sq_k, sq_q = (t3(arena[:, o:o + 2 * N], 2) for o in (2 * KD * N, B2 + NT * M))
        RW = NT * P + P
        ring = t3(wa[:, 2 * KD * D:2 * KD * D + RING * RW // 2].bitcast(BF16), RING)
        c_stage = arena[:, B4:B4 + N]
        w_raw = t3(wa[:, 5 * KD * D - KM * D:5 * KD * D], KM)
        assert RING * RW // 2 + KM * D <= 3 * KD * D
        qp = t3(arena[:, B2:B2 + NT * M], NT)
        qpT = t3(arena[:, B2 + NT * M:B2 + NT * M + KM * N], KM)
        assert B2 + NT * M + 2 * N <= B4 and KM <= 2
        x2 = t3(arena[:, B5:B5 + 2 * D], 2)
        x2T = arena[:, B5 + 2 * D:B5 + 4 * D].rearrange("p (b k c) -> p b k c", b=2, k=KD)
        xn = t3(arena[:, B5:B5 + NT * D], NT)
        xm = xn
        WSZ = KD * D
        gw1_s = t3(wa[:, 0:WSZ], KD)
        ksum, kpsum, qk = (wa[:, i * M:(i + 1) * M] for i in range(3))
        gw2_s = t3(wa[:, WSZ:2 * WSZ], KD)
        EW = N + (NT - 1) * P
        e_id = wa[:, WSZ:WSZ + EW // 2].bitcast(BF16)
        o = WSZ + EW // 2 + 1
        iota16 = wa[:, o:o + NT * P // 2].bitcast(I16)
        assert o + NT * P // 2 <= 2 * WSZ
        kqv_s = t3(wa[:, 2 * WSZ:5 * WSZ], KD)
        wv_sp = nc.alloc_sbuf_tensor_at("wv_split", [P, KD, 3 * D], F32R, offset=wa_at + 8 * WSZ)
        slices = [nc.alloc_sbuf_tensor_at(f"weight_slices{i}", [P, 2, 2, KD, P], F32R, offset=at)
                  for i, at in enumerate((wa_at + 4 * WSZ, arena_at + 8 * KD * N))]
        assert 4 * KD * P <= min(WSZ, NT * M)
        wo_s, w1_s, w2_s = (t3(wa[:, (2 + i) * WSZ:(3 + i) * WSZ], KD) for i in range(3))
        wT = t3(wa[:, 5 * WSZ:5 * WSZ + KD * M], KD)
        raw_gu, raw_d = ([wa[:, i * WSZ:(i + 1) * WSZ] for i in at] for at in ((0, 2), (3, 1)))
        BIAS0 = 4 * WSZ
        BIAS_STEP = WSZ + KD * M
        bd_b = wa[:, 5 * WSZ:5 * WSZ + 2 * D]
        assert CW == WSZ and 2 * I <= WSZ and 2 * D <= KD * M and BIAS0 + BIAS_STEP + 2 * I <= wa.shape[1]
        g_s, u_s, sig_s, a_s = (r1[:, 2 * D + i * I:2 * D + (i + 1) * I] for i in range(4))
        assert 2 * D + 4 * I <= NT * D
        ybuf = t3(r1[:, 0:2 * D], 2)

        ident = sb("ident", [P, P])
        ident_b = sb("ident_b", [P, P], BF16)
        ones = sb("ones", [P, P])
        ones_b = sb("ones_b", [P, P], BF16)
        tri_b = sb("tri_b", [P, P], BF16)
        vrow = sb("vrow", [8 * KD, P])
        vT = sb("vT", [P, 8 * KD])
        V_G1, V_BE1, V_G2, V_BE2, V_GB1, V_B1, V_BK, V_BQ = (KD * i for i in range(8))
        o = 5 * WSZ + KD * M
        bv_b, bo_b, b2_b = (wa[:, o + i * D:o + (i + 1) * D] for i in range(3))
        o += 3 * D
        srcT, dstT = wa[:, o:o + 2 * P], wa[:, o + 2 * P:o + 4 * P]
        gb2_b = sb("gb2_b", [P, D])
        xs = gb2_b[:, :]
        rb_b = sb("rb_b", [P, NX])
        rw_s = sb("rw_s", [P, KD, NX])
        x_sum = sb("x_sum", [P, NT])
        x_sq = sb("x_sq", [P, NT])
        nmean = sb("nmean", [P, NT])
        st6 = sb("st6", [P, NT, 6])
        mv = sb("mv", [P, NT, 2])
        ve = sb("ve", [P, NT])
        sd = sb("sd", [P, NT])
        rstd = sb("rstd", [P, NT])
        rstd2 = sb("rstd2", [P, NT])
        nmr = sb("nmr", [P, NT])
        mm2 = sb("minmax", [P, 4])
        xdn = sb("xdn", [P, 2 * NT])
        den = sb("den", [P, NT])
        rden = sb("rden", [P, NT])
        piota = sb("piota", [P, 1])
        lo_j = sb("lo_j", [P, 1])
        hi_j = sb("hi_j", [P, 1])
        rng = sb("rng", [P, 4])
        rng_i = sb("rng_i", [P, 4], I32)
        place_i = sb("place_i", [P, SLOTS], I32)
        used_i = sb("used_i", [P, NX + 1], I32)
        used_end_i = sb("used_end_i", [P, NX + 1], I32)
        last_i = sb("last_i", [P, 2], I32)
        change_i = sb("change_i", [P, SLOTS], I32)
        pos_i = sb("pos_i", [P, TOP, NT], I32)
        idx_i = sb("idx_i", [P, SLOTS], I32)
        idx_s = sb("idx_s", [P, 1], I32)
        wgt = sb("wgt", [P, TOP, NT])
        wgt2 = sb("wgt2", [P, TOP, NT])
        logit = sb("logit", [P, NT, NX])
        erow = t3(arena[:, B5:B5 + 5 * 2 * P], 5)
        o = 2 * D

        def r1_take(n):
            nonlocal o
            o += n
            assert o <= NT * D
            return r1[:, o - n:o]
        mx8 = t3(r1_take(NT * NX), NT)
        mi8 = t3(r1_take(NT * NX).bitcast(U32), NT)
        mif = t3(r1_take(NT * NX), NT)
        KT = TOP * NT
        oh = r1_take(KT * NX).rearrange("p (k t e) -> p k t e", k=TOP, t=NT)
        msk_b = r1_take(NT * NX // 2).bitcast(BF16)
        rank = t3(r1_take(NT * NX), NT)
        cnt_i = r1_take(NX).bitcast(I32)
        cnt = r1_take(NX)
        has = r1_take(NX)
        ends = t3(r1_take(2 * NX), 2)
        base = r1_take(NX)
        ex2 = t3(r1_take(2 * NT), 2)
        posf = r1_take(KT)
        pa_i, pb_i = (r1_take(KT).bitcast(I32) for _ in range(2))
        pa_f, pb_f = (r1_take(KT) for _ in range(2))
        behind = r1_take(1)
        tile_no = r1_take(KT)
        iota1 = r1_take(NX)
        iota_s = r1_take(SLOTS)
        iota_c = r1_take(P)
        cmp_s = t3(r1_take(SLOTS * NX), SLOTS)
        cmp_u = t3(r1_take(NX * NX), NX)
        num_end = t3(r1_take(2 * NX), 2)
        num_end_of = r1_take(2 * NX * NX).rearrange("p (w i e) -> p w i e", w=2, i=NX)
        used_f = t3(r1_take(2 * NX), 2)
        place_f = r1_take(SLOTS)
        last_f = r1_take(2)
        row_f = r1_take(SLOTS)
        low, w_of = (t3(r1_take(2 * NT), 2) for _ in range(2))
        slot_b = r1_take(KT * P // 2).bitcast(BF16).rearrange("p (n c) -> p n c", n=KT)
        slot_1 = r1_take(KT * SLOTS // 2).bitcast(BF16).rearrange("p (n s) -> p n s", n=KT)
        slot_a = r1_take(KT * SLOTS).bitcast(BF16).rearrange("p (n w s) -> p n w s", n=KT, w=2)
        CB = 4
        yg = arena[:, 0:CB * TOP * D].rearrange("p (b k c) -> p b k c", b=CB, k=TOP)
        LOWER = [raw_gu[i // (CW // D)][:, i % (CW // D) * D:(i % (CW // D) + 1) * D] for i in range(2 * CW // D)][:NT]
        EARLY = len(LOWER)
        ob = t3(arena[:, CB * TOP * D:CB * (TOP + 1) * D], CB)

        ps = ctx.enter_context(nc.psum_tensor("ps", [P, 8, BANK], F32))

        x2_d = nc.dram_tensor("x2_scratch", (N, D), F32, kind="Internal").ap()
        y_d = nc.dram_tensor("y_scratch", (SLOTS * P, D), F32, kind="Internal").ap()

        ld_x, ld_e, ld_w, ld_vec, ld_rows = (sem(f"ld_{n}") for n in ("x", "edges", "w", "vec", "rows"))
        ld_gw1, ld_gw2, ld_kqv, ld_ow1w2 = (sem(f"ld_{n}") for n in ("gw1", "gw2", "kqv", "wow1w2"))
        consts = sem("consts_ready")
        pads = sem("edge_pads")
        dch = sem("dve_chain")
        pch = sem("pool_chain")
        sq_in, sq_out = sem("sqrt_in"), sem("sqrt_out")
        a_in, a_out = sem("act_tile_full"), sem("act_tile_out")
        d_in, d_out = sem("dve_tile_full"), sem("dve_tile_out")
        range_ready = sem("edge_ranges_ready")
        oh_ready, oh_free = sem("onehots_ready"), sem("onehots_free")
        c_full, c_out = sem("counts_full"), sem("counts_out")
        ct_full, ct_out = sem("countsT_full"), sem("countsT_out")
        sq_ready, ks_ready = sem("squares_ready"), sem("keys_sum_ready")
        nmr_ready, xn_ready = sem("nmr_ready"), sem("xn_ready")
        x_summed, x_mean, x_squared = (sem(n) for n in ("x_summed", "x_mean_ready", "x_squares_summed"))
        xh_ready, xl_ready = sem("xn_leading_ready"), sem("xn_rest_ready")
        sl_hi, sl_ready = sem("slice_leading"), sem("slice_ready")
        wv_hi, wv_ready = sem("wv_leading"), sem("wv_ready")
        f_mid, f_hi, f_even, f_odd = (sem(n) for n in (
            "features_unsplit", "features_leading", "features_even_ready", "features_odd_ready"))
        xm_ready, yh_ready = sem("xm_ready"), sem("yhat_ready")
        xy_ready = sem("x_plus_y_ready")
        xn2_ready = sem("xn2_ready")
        st_x2 = [sem(f"x2_stored{i}") for i in range(2)]
        y_ready = sem("y_rows_ready")
        msk_ready, slot_ready, route_ready, exp_in, exp_out = (sem(n) for n in (
            "mask_ready", "slot_onehots_ready", "route_ready", "gate_exp_in", "gate_exp_out"))
        zero_ready, st_zero = sem("zeros_ready"), sem("zeros_stored")
        gu_raw = [sem(f"gate_up_chunk_loaded{i}") for i in range(2)]
        d_raw = [sem(f"down_chunk_loaded{i}") for i in range(DC)]
        b_ld = sem("biases_loaded")
        gu_hi, gu_split, d_hi, d_split = (sem(n) for n in (
            "gate_up_leading", "gate_up_split", "down_leading", "down_split"))
        xt_hi, at_hi = sem("xsT_leading"), sem("actT_leading")
        idx_ready, pool_passed, sp_passed = sem("slot_index_ready"), sem("pool_passed"), sem("sp_passed")
        gath, xt_full, xt_out = sem("rows_gathered"), sem("xsT_full"), sem("xsT_out")
        gu_full, g_out, gu_out = sem("gate_up_full"), sem("gate_out"), sem("gate_up_out")
        sig_out, a_ready = sem("sigmoid_out"), sem("act_ready")
        at_full, at_out, dn_full, slot_done, y_st = (sem(n) for n in (
            "actT_full", "actT_out", "down_full", "slots_done", "y_stored"))
        cg = [sem(f"pair_gathered{i}") for i in range(CB)]
        slots_known, pos_sorted, lower_in = sem("slots_known"), sem("positions_sorted"), sem("lower_rows_gathered")
        o_ready = sem("out_ready")
        o_st = [sem(f"out_stored{i}") for i in range(CB)]

        block = ctx.enter_context(nc.Block())

        SLICES = [(wt, col0 + b * P, n0 + b * NC)
                  for wt, col0, n0 in ((kqv_s, 0, A_KQ), (kqv_s, D, A_KQ + KD * NC), (gw1_s, 0, A_R), (w1_s, 0, A_G))
                  for b in range(KD)]
        S_K, S_Q, S_R, S_G = (i * KD for i in range(4))

        def slice_of(n):
            return slices[n // S_G][:, n % 2]

        def whole_slice(n):
            wt, col, n0 = SLICES[n]
            return wt[:, :, col:col + P]

        def tiled(ap):
            return ap.rearrange("(k p) n -> p k n", p=P)

        def one_row(ap):
            return ap.rearrange("(a n) -> a n", a=1)

        @block.sync
        def _(sp):
            sp.wait_ge(pads, 2)
            for i, e in enumerate((src, dst)):
                sp.dma_start(e_int[:, i, 0, :], e[0:P * P].rearrange("(c k) -> c k", k=P)).then_inc(ld_e, 16)
                sp.dma_start(e_int[0:EFULL - P, i, 1, :],
                             e[P * P:EFULL * P].rearrange("(c k) -> c k", k=P)).then_inc(ld_e, 16)
                sp.dma_start(e_int[EFULL - P:EFULL - P + 1, i, 1, 0:EREST],
                             one_row(e[EFULL * P:E])).then_inc(ld_e, 16)
            sp.dma_start(xr[:, 0:NT - 1, :], tiled(x[0:(NT - 1) * P, :])).then_inc(ld_x, 16)
            sp.dma_start(xr[0:LAST, NT - 1, :], x[(NT - 1) * P:N, :]).then_inc(ld_x, 16)
            sp.dma_start(w_raw, tiled(w)).then_inc(ld_w, 16)
            for at, vec in ((V_G1, g1), (V_BE1, be1), (V_G2, g2), (V_BE2, be2), (V_GB1, gb1), (V_B1, b1),
                            (V_BK, bkqv[0:2 * D])):
                n = vec.shape[0] // P
                sp.dma_start(vrow[at:at + n, :], vec.rearrange("(k p) -> k p", p=P)).then_inc(ld_vec, 16)
            sp.dma_start(gw1_s, tiled(gw1)).then_inc(ld_gw1, 16)
            for to, row in ((bv_b, bkqv[2 * D:3 * D]), (bo_b, bo), (b2_b, b2), (gb2_b, gb2), (rb_b, rb)):
                sp.dma_start(to[:, :], row.partition_broadcast(P)).then_inc(ld_rows, 16)
            sp.dma_start(rw_s[:, :, :], tiled(rw)).then_inc(ld_rows, 16)
            sp.wait_ge(zero_ready, 1)
            for s in range(SLOTS):
                sp.dma_start(y_d[s * P:(s + 1) * P, :], zero).then_inc(st_zero, 16)
            sp.wait_ge(a_in, A_WT + KM)
            sp.dma_start(kqv_s, tiled(wkqv)).then_inc(ld_kqv, 16)
            sp.wait_ge(d_in, D_V + NT)
            for to, f in ((wo_s, wo), (w1_s, w1), (w2_s, w2)):
                sp.dma_start(to, tiled(f)).then_inc(ld_ow1w2, 16)
            sp.wait_ge(a_in, A_R + KD * NC)
            sp.dma_start(gw2_s, tiled(gw2)).then_inc(ld_gw2, 16)

            def load_gate_up(e, c):
                w_e = wgu[bass.ds(e, 1), :, c * BANK:(c + 1) * BANK] if not isinstance(e, int) else \
                    wgu[e:e + 1, :, c * BANK:(c + 1) * BANK]
                sp.dma_start(t3(raw_gu[c % 2], KD), w_e.rearrange("a (k p) n -> p (a k) n", p=P))\
                    .then_inc(gu_raw[c % 2], 16)

            def load_down(e, h):
                w_e = wd[bass.ds(e, 1), h * CW // KD:(h + 1) * CW // KD, :] if not isinstance(e, int) else \
                    wd[e:e + 1, h * CW // KD:(h + 1) * CW // KD, :]
                sp.dma_start(t3(raw_d[h], KD), w_e.rearrange("a (k p) n -> p (a k) n", p=P)).then_inc(d_raw[h], 16)
            sp.wait_ge(d_out, D_Y + 1)
            load_gate_up(0, 0)
            sp.wait_ge(d_in, D_Y + NT)
            load_gate_up(0, 1)
            sp.wait_ge(a_in, A_G + KD * NC)
            load_down(0, 0)
            for t in range(NT):
                if t in (1, 3):
                    c = 2 + t // 2
                    sp.wait_ge(gu_split, c)
                    load_gate_up(0, c)
                sp.wait_ge(xn2_ready, t + 1)
                sp.dma_start(x2_d[t * P:t * P + rows(t), :], x2[0:rows(t), t % 2, :]).then_inc(st_x2[t % 2], 16)
            for i in range(2):
                sp.wait_ge(st_x2[i], 16 * (NT // 2))
            sp.wait_ge(d_in, D_X1[NT - 1] + 1)
            load_down(0, 1)
            sp.dma_start(wa[:, BIAS0:BIAS0 + 2 * I], bgu[0].partition_broadcast(P)).then_inc(b_ld, 16)
            sp.dma_start(bd_b[:, 0:D], bd[0].partition_broadcast(P)).then_inc(b_ld, 16)
            sp.wait_ge(route_ready, 1)
            sp.wait_ge(gu_split, GC + 1)
            sp.wait_ge(d_split, 2 * DC)
            used_last = sp.value_load(last_i[0:1, 0:1], min_val=1, max_val=NX - 1)

            def chunks(i, cs):
                e = sp.snap(sp.value_load(used_i[0:1, i:i + 1] if isinstance(i, int) else used_i[0:1, bass.ds(i, 1)],
                                          min_val=0, max_val=NX - 1))
                for c in cs:
                    sp.wait_ge(gu_split, i * GC + c)
                    sp.sem_inc(sp_passed, 1)
                    load_gate_up(e, c)
                return e
            sp.wait_ge(gath, 16)
            chunks(1, (0, 1))
            with sp.Fori(1, used_last + 1) as i:
                end2 = sp.snap(sp.value_load(used_end_i[0:1, bass.ds(i - 1, 1)], min_val=0, max_val=SLOTS))
                half = sp.snap(i % 2)
                e = chunks(i, range(2, GC))
                sp.wait_ge(slot_done, end2 + 1)
                sp.sem_inc(sp_passed, 1)
                sp.wait_ge(b_ld, i * 32)
                sp.sem_inc(sp_passed, 1)
                sp.dma_start(wa[:, bass.ds(half * BIAS_STEP + BIAS0, 2 * I)],
                             bgu[bass.ds(e, 1), :].rearrange("a n -> (a n)").partition_broadcast(P)).then_inc(b_ld, 16)
                sp.dma_start(bd_b[:, bass.ds(half * D, D)],
                             bd[bass.ds(e, 1), :].rearrange("a n -> (a n)").partition_broadcast(P)).then_inc(b_ld, 16)
                with sp.If(sp.snap(used_last - i)):
                    chunks(i + 1, (0, 1))
                for h in range(DC):
                    sp.wait_ge(d_split, i * DC + (h + 1))
                    sp.sem_inc(sp_passed, 1)
                    load_down(e, h)
            for t in range(NT):
                sp.wait_ge(o_ready, t + 1)
                sp.dma_start(out[t * P:t * P + rows(t), :], ob[0:rows(t), t % CB, :]).then_inc(o_st[t % CB], 16)
            for i in range(CB):
                sp.wait_ge(o_st[i], 16 * len(range(i, NT, CB)))

        @block.gpsimd
        def _(pool):
            n_link = 0

            def link(ins):
                nonlocal n_link
                n_link += 1
                ins.then_inc(pch, 1)
                pool.wait_ge(pch, n_link)
            link(nc.gpsimd.memset(ident[:, :], 0.0))
            nc.gpsimd.affine_select(out=ident[:, :], in_=ident[:, :], compare_op=ALU.not_equal, fill=1.0, base=0,
                                    pattern=[[-1, P]], channel_multiplier=1).then_inc(consts, 1)
            link(nc.gpsimd.memset(ones[:, :], 1.0))
            nc.gpsimd.memset(zero, 0.0).then_inc(zero_ready, 1)
            link(nc.gpsimd.memset(ident_b[:, :], 0.0))
            link(nc.gpsimd.affine_select(out=ident_b[:, :], in_=ident_b[:, :], compare_op=ALU.not_equal, fill=1.0,
                                         base=0, pattern=[[-1, P]], channel_multiplier=1))
            link(nc.gpsimd.iota(piota[:, :], pattern=[[0, 1]], base=0, channel_multiplier=1,
                                allow_small_or_imprecise_dtypes=True))
            nc.gpsimd.iota(iota16[:, :], pattern=[[1, NT * P]], base=0, channel_multiplier=0,
                           allow_small_or_imprecise_dtypes=True).then_inc(consts, 1)
            nc.gpsimd.iota(erow[:, 4, 0:ET], pattern=[[1, ET]], base=0, channel_multiplier=0,
                           allow_small_or_imprecise_dtypes=True).then_inc(consts, 1)
            link(nc.gpsimd.memset(e_id[:, :], 0.0))
            nc.gpsimd.affine_select(out=e_id[:, (NT - 1) * P:NT * P], in_=e_id[:, (NT - 1) * P:NT * P],
                                    compare_op=ALU.not_equal, fill=1.0, base=0, pattern=[[-1, P]],
                                    channel_multiplier=1).then_inc(consts, 1)
            link(nc.gpsimd.memset(ones_b[:, :], 1.0))
            nc.gpsimd.affine_select(out=tri_b[:, :], in_=ones_b[:, :], compare_op=ALU.is_gt, fill=0.0, base=0,
                                    pattern=[[1, P]], channel_multiplier=-1).then_inc(consts, 1)
            pool.wait_ge(st_zero, 16 * SLOTS)
            for t in range(NT):
                r = rows(t)
                pool.wait_ge(xh_ready, t + 1)
                nc.gpsimd.tensor_tensor(xl[0:r, t, :], xn[0:r, t, :], xh[0:r, t, :].bitcast(F32), ALU.subtract)\
                    .then_inc(xl_ready, 1)

            def slice_rest(*ns):
                for n in ns:
                    pool.wait_ge(sl_hi, n + 1)
                    nc.gpsimd.tensor_tensor(slice_of(n)[:, 1], whole_slice(n), slice_of(n)[:, 0].bitcast(F32),
                                            ALU.subtract).then_inc(sl_ready, 1)

            def features_rest(n0):
                for c, (a, m) in enumerate(COLS):
                    for b in range(0, KD, 2):
                        pool.wait_ge(f_hi, n0 + c * KD + b + 1)
                        nc.gpsimd.tensor_tensor(f_sp[:, 1, b, a:a + m], f_whole[:, b, a:a + m],
                                                f_sp[:, 0, b, a:a + m].bitcast(F32), ALU.subtract).then_inc(f_even, 1)
            slice_rest(0, 1)
            features_rest(0)
            slice_rest(*range(2, S_R + 2))
            for k in range(KD):
                pool.wait_ge(wv_hi, k + 1)
                nc.gpsimd.tensor_tensor(wv_sp[:, k, D:2 * D], kqv_s[:, k, 2 * D:3 * D], wv_sp[:, k, 0:D].bitcast(F32),
                                        ALU.subtract).then_inc(wv_ready, 1)
            for b in range(0, KD, 2):
                pool.wait_ge(f_hi, KD * NC + b + 1)
                nc.gpsimd.tensor_tensor(f_sp[:, 1, b, :], zT[:, b, :], f_sp[:, 0, b, :].bitcast(F32), ALU.subtract)\
                    .then_inc(f_even, 1)
            slice_rest(S_R + 2, S_R + 3)
            pool.wait_ge(ld_rows, 6 * 16)
            link(nc.gpsimd.tensor_tensor(b2_b[:, :], b2_b[:, :], gb2_b[:, :], ALU.add))
            slice_rest(S_G, S_G + 1)
            for t in range(NT):
                pool.wait_ge(y_ready, t + 1)
                r = rows(t)
                link(nc.gpsimd.tensor_tensor(xr[0:r, t, :], xr[0:r, t, :], v[0:r, t, :], ALU.add))
                nc.gpsimd.tensor_tensor(xr[0:r, t, :], xr[0:r, t, :], b2_b[0:r, :], ALU.add).then_inc(xy_ready, 1)
            features_rest(KD * NC + KD)
            slice_rest(S_G + 2, S_G + 3)
            pool.wait_ge(xy_ready, NT)
            nc.gpsimd.iota(iota1[:, :], pattern=[[1, NX]], base=1, channel_multiplier=0,
                           allow_small_or_imprecise_dtypes=True).then_inc(consts, 1)
            nc.gpsimd.iota(iota_s[:, :], pattern=[[1, SLOTS]], base=0, channel_multiplier=0,
                           allow_small_or_imprecise_dtypes=True).then_inc(consts, 1)
            nc.gpsimd.iota(t3(tile_no, TOP), pattern=[[0, TOP], [1, NT]], base=0, channel_multiplier=0,
                           allow_small_or_imprecise_dtypes=True).then_inc(consts, 1)
            nc.gpsimd.iota(iota_c[:, :], pattern=[[1, P]], base=0, channel_multiplier=0,
                           allow_small_or_imprecise_dtypes=True).then_inc(consts, 1)
            pool.sem_inc(gu_split, 1)
            pool.sem_inc(d_split, DC)
            for c in range(GC):
                pool.wait_ge(gu_hi, c + 1)
                nc.gpsimd.tensor_tensor(w_sp[:, c, 1, :], raw_gu[c % 2], w_sp[:, c, 0, :].bitcast(F32), ALU.subtract)\
                    .then_inc(gu_split, 1)
            for h in range(DC - 1):
                pool.wait_ge(d_hi, h + 1)
                nc.gpsimd.tensor_tensor(w_sp[:, GC + h, 1, :], raw_d[h], w_sp[:, GC + h, 0, :].bitcast(F32),
                                        ALU.subtract).then_inc(d_split, 1)
            pool.wait_ge(slots_known, 1)
            for i in range(2):
                pool.wait_ge(st_x2[i], 16 * (NT // 2))
            last = nc.gpsimd.value_load(last_i[0:1, 1:2], min_val=SLOTS_MIN - 1, max_val=SLOTS - 1)
            pool.sem_inc(xt_full, 1)
            with pool.Fori(0, last + 1) as s:
                pool.wait_ge(xt_full, s + 1)
                nc.gpsimd.tensor_copy(idx_s[:, :], idx_i[:, bass.ds(s, 1)]).then_inc(idx_ready, 1)
                pool.wait_ge(idx_ready, s + 1)
                pool.sem_inc(pool_passed, 1)
                nc.gpsimd.indirect_dma_start(xs, None, x2_d, bass.IndirectOffsetOnAxis(ap=idx_s[:, :], axis=0),
                                             bounds_check=N - 1).then_inc(gath, 16)
                pool.wait_ge(gath, (s + 1) * 16)
            used_last = nc.gpsimd.value_load(last_i[0:1, 0:1], min_val=1, max_val=NX - 1)
            end_before = nc.gpsimd.value_load(used_end_i[0:1, bass.ds(used_last, 1)], min_val=0, max_val=SLOTS)
            pool.wait_ge(pos_sorted, TOP)
            pool.wait_ge(gu_split, nc.gpsimd.snap(used_last * GC + GC + 1))
            pool.sem_inc(pool_passed, 1)
            pool.wait_ge(y_st, nc.gpsimd.snap((end_before + 2) * 16))
            pool.sem_inc(pool_passed, 1)

            def gather(t, k, to, done):
                r = rows(t)
                nc.gpsimd.indirect_dma_start(to[0:r, :], None, y_d,
                                             bass.IndirectOffsetOnAxis(ap=pos_i[0:r, k, t:t + 1], axis=0),
                                             bounds_check=SLOTS * P - 1).then_inc(done, 16)
            for t in range(EARLY):
                gather(t, 0, LOWER[t], lower_in)
            pool.wait_ge(y_st, nc.gpsimd.snap((last + 3) * 16))
            pool.sem_inc(pool_passed, 1)
            for t in range(NT):
                if t >= CB:
                    pool.wait_ge(o_ready, t - CB + 1)
                for k in range(1 if t < EARLY else 0, TOP):
                    gather(t, k, yg[:, t % CB, k, :], cg[t % CB])

        @block.scalar
        def _(act):
            n_sqrt = 0

            def sqrt(a, b):
                nonlocal n_sqrt
                n_sqrt += 1
                act.wait_ge(sq_in, n_sqrt)
                nc.scalar.activation(sd[:, a:b], ve[:, a:b], ACT.Sqrt).then_inc(sq_out, 1)

            def full(n):
                act.wait_ge(a_in, n + 1)
                return ps[:, n % 4, :]

            def slice_hi(n):
                if n in (S_K, S_R, S_G):
                    act.wait_ge(*{S_K: (ld_kqv, 16), S_R: (ld_gw1, 16), S_G: (ld_ow1w2, 3 * 16)}[n])
                if n == S_G:
                    act.wait_ge(ks_ready, 1)
                if n % S_G >= 2:
                    act.wait_ge(a_in, SLICES[n - 2][2] + NC)
                nc.scalar.copy(slice_of(n)[:, 0], whole_slice(n)).then_inc(sl_hi, 1)

            def features_hi(n0):
                for c, (a, m) in enumerate(COLS):
                    for b in range(KD):
                        act.wait_ge(f_mid, n0 + c * KD + b + 1)
                        nc.scalar.copy(f_sp[:, 0, b, a:a + m], f_whole[:, b, a:a + m]).then_inc(f_hi, 1)

            def linear(to, n0, cols, fn, bias, n_slice, n_last):
                for b in range(KD):
                    if b and n_slice + b + 1 <= n_last:
                        slice_hi(n_slice + b + 1)
                    for c, (a, m) in enumerate(cols):
                        bank = full(n0 + b * NC + c)
                        nc.scalar.activation(to[:, b, a:a + m], bank[:, 0:m], fn,
                                             bias=vT[:, bias + b:bias + b + 1]).then_inc(a_out, 1)

            act.wait_ge(pads, 4)
            act.wait_ge(ld_x, 32)
            for t in range(NT):
                r = rows(t)
                nc.scalar.activation(v[0:r, t, :], xr[0:r, t, :], ACT.Copy,
                                     accum_out=x_sum[0:r, t:t + 1]).then_inc(x_summed, 1)
            act.wait_ge(x_summed, NT)
            nc.scalar.activation(nmean[:, :], x_sum[:, :], ACT.Copy, scale=-1.0 / D).then_inc(x_mean, 1)
            act.wait_ge(x_mean, 1)
            act.wait_ge(range_ready, 1)
            for t in range(NT):
                r = rows(t)
                nc.scalar.activation(xn[0:r, t, :], xr[0:r, t, :], ACT.Square, bias=nmean[0:r, t:t + 1],
                                     accum_out=x_sq[0:r, t:t + 1]).then_inc(x_squared, 1)
            long_ranges = nc.scalar.alloc_register("long_ranges")
            nc.scalar.reg_mov(long_ranges, 0)
            for j in range(NT):
                nc.scalar.reg_add(long_ranges, long_ranges,
                                  nc.scalar.value_load(rng_i[j:j + 1, 3:4], min_val=0, max_val=ET >> LONG_SHIFT))
            for j in range(NT + 1):
                if j < NT:
                    act.wait_ge(c_full, j + 1)
                    if j:
                        act.wait_ge(ct_full, NC * j)
                    for c, (a, m) in enumerate(COLS):
                        nc.scalar.copy(c_stage[:, a:a + m], ps[:, 3 * (j % 2) + c, 0:m]).then_inc(c_out, 1)
                if j == 0:
                    sqrt(0, NT)
                    sqrt(0, NT)
                    for t in range(NT):
                        r = rows(t)
                        if t == 0:
                            act.wait_ge(nmr_ready, 1)
                        nc.scalar.activation(xn[0:r, t, :], xr[0:r, t, :], ACT.Identity, scale=rstd[0:r, t:t + 1],
                                             bias=nmr[0:r, t:t + 1]).then_inc(xn_ready, 1)
                    for t in range(NT):
                        act.wait_ge(xn_ready, t + 1)
                        nc.scalar.copy(xh[0:rows(t), t, :], xn[0:rows(t), t, :]).then_inc(xh_ready, 1)
                if j == 1:
                    act.wait_ge(nmr_ready, 2)
                    for t in range(NT):
                        r = rows(t)
                        act.wait_ge(xl_ready, t + 1)
                        nc.scalar.activation(xm[0:r, t, :], xn[0:r, t, :], ACT.Copy,
                                             scale=rstd2[0:r, t:t + 1]).then_inc(xm_ready, 1)
                if j < NT:
                    for g in range(NC):
                        n = NC * j + g
                        act.wait_ge(ct_full, n + 1)
                        bank = ps[:, 6 + n % 2, :].rearrange("p (k c) -> p k c", k=TPC)
                        r = rows(j)
                        whole = min(TPC, NT - 1 - TPC * g)

                        def turned(to):
                            nc.scalar.copy(to[:, TPC * g:TPC * g + whole, j * P:j * P + r], bank[:, 0:whole, 0:r])\
                                .then_inc(ct_out, 1)
                            if whole < TPC:
                                nc.scalar.copy(to[0:LAST, NT - 1, j * P:j * P + r], bank[0:LAST, whole, 0:r])\
                                    .then_inc(ct_out, 1)
                        with act.If_eq(long_ranges, 0):
                            turned(cT_r)
                        with act.If_ne(long_ranges, 0):
                            turned(cT)
            nc.scalar.copy(vT[:, :], full(A_VEC)[:, 0:8 * KD]).then_inc(a_out, 1)
            for m in range(KM):
                nc.scalar.copy(wT[:, :, m * P:(m + 1) * P],
                               full(A_WT + m)[:, :].rearrange("p (k c) -> p k c", k=KD)).then_inc(a_out, 1)
            act.wait_ge(a_out, A_VEC + 1)
            act.wait_ge(st_zero, 16 * SLOTS)
            for b in range(KD):
                for c, (a, m) in enumerate(COLS):
                    nc.scalar.copy(zT[:, b, a:a + m], full(A_Z + b * NC + c)[:, 0:m]).then_inc(a_out, 1)
            slice_hi(0)
            slice_hi(1)
            features_hi(0)
            linear(kT, A_KQ, COLS, ACT.Identity, V_BK, S_K, S_Q)
            slice_hi(S_Q + 1)
            linear(qT, A_KQ + KD * NC, COLS, ACT.Identity, V_BQ, S_Q, S_R)
            slice_hi(S_R + 1)
            act.wait_ge(sl_ready, S_R)
            for k in range(KD):
                nc.scalar.copy(wv_sp[:, k, 0:D], kqv_s[:, k, 2 * D:3 * D]).then_inc(wv_hi, 1)
            for i, (to, n0, d0) in enumerate(((kp, A_KP, D_XDK), (qp, A_QP, D_XDQ))):
                if i:
                    act.wait_ge(d_in, D_V + NT)
                    for b in range(KD):
                        nc.scalar.copy(f_sp[:, 0, b, :], zT[:, b, :]).then_inc(f_hi, 1)
                act.wait_ge(d_out, d0 + 1)
                for t in range(NT):
                    r = rows(t)
                    nc.scalar.activation(to[0:r, t, :], full(n0 + t)[0:r, 0:M], ACT.Exp,
                                         bias=xdn[0:r, i * NT + t:i * NT + t + 1]).then_inc(a_out, 1)
            for b in range(KM):
                for c, (a, m) in enumerate(COLS):
                    nc.scalar.copy(qpT[:, b, a:a + m], full(A_QPT + b * NC + c)[:, 0:m]).then_inc(a_out, 1)
            linear(rT, A_R, COLS, ACT.Relu, V_GB1, S_R, S_R + KD - 1)
            for b in range(KM):
                nc.scalar.copy(kptvT[:, b, :], full(A_KPTV + b)).then_inc(a_out, 1)
            slice_hi(S_G)
            slice_hi(S_G + 1)
            for b in range(KD):
                for c, (a, m) in enumerate(COLS):
                    nc.scalar.copy(attT[:, b, a:a + m], full(A_ATT + b * NC + c)[:, 0:m]).then_inc(a_out, 1)
            for c in range(NC):
                sqrt(TPC * c, min(TPC * c + TPC, NT))
            features_hi(KD * NC)
            linear(gT, A_G, COLS, ACT.Gelu, V_B1, S_G, S_G + KD - 1)

            def gate_up_hi(i, c):
                act.wait_ge(gu_raw[c % 2], i * 32 + 16 * (c // 2 + 1))
                nc.scalar.copy(w_sp[:, c, 0, :], raw_gu[c % 2]).then_inc(gu_hi, 1)

            def down_hi(i, h):
                act.wait_ge(d_raw[h], i * 16 + 16)
                nc.scalar.copy(w_sp[:, GC + h, 0, :], raw_d[h]).then_inc(d_hi, 1)
            gate_up_hi(0, 0)
            gate_up_hi(0, 1)
            for t in range(NT + 1):
                if t == 3:
                    gate_up_hi(0, 2)
                if t < NT:
                    sqrt(t, t + 1)
                if t >= 1:
                    r = rows(t - 1)
                    nc.scalar.copy(x2T[:, (t - 1) % 2, :, 0:r],
                                   full(A_X2T + t - 1)[:, :].rearrange("p (k c) -> p k c", k=KD)[:, :, 0:r])\
                        .then_inc(a_out, 1)
            act.wait_ge(exp_in, 1)
            nc.scalar.activation(ex2[:, 1, :], ex2[:, 0, :], ACT.Exp).then_inc(exp_out, 1)

            act.wait_ge(d_in, D_LOG[NT - 1] + 1)
            for i in range(2):
                act.wait_ge(st_x2[i], 16 * (NT // 2))
            gate_up_hi(0, 3)
            for h in range(DC):
                down_hi(0, h)

            def xsT_out(s):
                act.wait_ge(xt_full, s + 2)
                if not (isinstance(s, int) and s == 0):
                    act.wait_ge(gu_full, s * GC)
                nc.scalar.copy(xT_sp[:, 0, :], ps[:, 7, :]).then_inc(xt_hi, 1)

            def slot(s, prev, nxt):
                if nxt:
                    changes = nc.scalar.value_load(change_i[0:1, bass.ds(s, 1)] if prev else change_i[0:1, 0:1],
                                                   min_val=0, max_val=1)
                    i = nc.scalar.snap(nc.scalar.value_load(
                        place_i[0:1, bass.ds(s, 1)] if prev else place_i[0:1, 0:1], min_val=0, max_val=NX - 1) + 1)
                    with act.If(changes):
                        for c in range(2):
                            act.wait_ge(gu_full, s * GC + (c + 1))
                            gate_up_hi(i, c)
                if prev:
                    aT_out(s)
                act.wait_ge(g_out, s + 1)
                nc.scalar.activation(sig_s, g_s, ACT.Sigmoid, scale=1.702).then_inc(sig_out, 1)
                if nxt:
                    xsT_out(s + 1)
                    with act.If(changes):
                        for c in range(2, GC):
                            gate_up_hi(i, c)
                if prev:
                    change_down(s)
                    store(s)

            def change_down(s):
                changed = nc.scalar.value_load(change_i[0:1, bass.ds(s - 1, 1)], min_val=0, max_val=1)
                i = nc.scalar.snap(nc.scalar.value_load(place_i[0:1, bass.ds(s, 1)], min_val=0, max_val=NX - 1))
                with act.If(changed):
                    act.wait_ge(dn_full, s)
                    for h in range(DC):
                        down_hi(i, h)

            def aT_out(n):
                for h in range(2):
                    act.wait_ge(at_full, 2 * n + h)
                    nc.scalar.copy(aT_sp[:, 0, h * BANK:(h + 1) * BANK], ps[:, 4 + h, :]).then_inc(at_hi, 1)

            def store(n):
                act.wait_ge(slot_done, n + 1)
                act.wait_ge(y_st, 16 * (n + 1))
                act.dma_start(y_d[bass.ds((n - 1) * P, P), :], ybuf[:, (n - 1) % 2, :]).then_inc(y_st, 16)
            act.sem_inc(y_st, 32)
            act.sem_inc(at_hi, 1)
            act.wait_ge(route_ready, 1)
            with act.If(nc.scalar.value_load(place_i[0:1, 0:1], min_val=0, max_val=1)):
                for c in range(GC):
                    gate_up_hi(1, c)
                for h in range(DC):
                    down_hi(1, h)
            xsT_out(0)
            slot(0, False, True)
            last = nc.scalar.value_load(last_i[0:1, 1:2], min_val=SLOTS_MIN - 1, max_val=SLOTS - 1)
            with act.Fori(1, last) as s:
                slot(s, True, True)
            slot(last, True, False)
            aT_out(last + 1)
            store(last + 1)

        @block.vector
        def _(dve):
            n_link = 0

            def link(ins):
                nonlocal n_link
                n_link += 1
                ins.then_inc(dch, 1)
                dve.wait_ge(dch, n_link)

            def full(n):
                dve.wait_ge(d_in, n + 1)
                return ps[:, 4 + n % 4, :]

            n_sqrt = 0

            def stats(t, rows_of):
                r = rows(t)
                link(nc.vector.bn_stats(st6[0:r, t, :], rows_of[0:r, t, :]))
                link(nc.vector.bn_aggr(mv[0:r, t, :], st6[0:r, t, :]))

            def rstds(a, b):
                nonlocal n_sqrt
                n_sqrt += 1
                nc.vector.tensor_scalar(ve[:, a:b], mv[:, a:b, 1], EPS, None, ALU.add).then_inc(sq_in, 1)
                dve.wait_ge(sq_out, n_sqrt)
                link(nc.vector.reciprocal(rstd[:, a:b], sd[:, a:b]))

            def normed(to, rows_of, t):
                r = rows(t)
                return nc.vector.tensor_scalar(to, rows_of[0:r, t, :], mv[0:r, t, 0:1], rstd[0:r, t:t + 1],
                                               ALU.subtract, ALU.mult)
            nc.vector.memset(e_int[:, 0, 1, :], 0).then_inc(pads, 1)
            nc.vector.memset(e_int[:, 1, 1, :], NOWHERE).then_inc(pads, 1)
            nc.vector.memset(x_sum[:, :], 1.0).then_inc(pads, 1)
            nc.vector.memset(x_sq[:, :], 1.0).then_inc(pads, 1)
            nc.vector.memset(mv[:, :, :], 1.0).then_inc(dch, 1)
            n_link += 1
            dve.wait_ge(consts, 2)
            link(nc.vector.tensor_scalar(lo_j[:, :], piota[:, :], float(P), None, ALU.mult))
            link(nc.vector.tensor_scalar(hi_j[:, :], piota[:, :], float(P), float(P), ALU.mult, ALU.add))
            dve.wait_ge(ld_e, 6 * 16)
            link(nc.vector.tensor_copy(e_f[:, :, :, :], e_int[:, :, :, :]))
            for g in range(2):
                link(nc.vector.tensor_reduce(mm2[:, g:g + 1], e_f[:, 1, g, :], AX_X, ALU.min))
                link(nc.vector.tensor_reduce(mm2[:, 2 + g:3 + g], e_f[:, 1, g, :], AX_X, ALU.max))
            dve.wait_ge(consts, 1)
            for i in range(4):
                link(nc.vector.tensor_scalar(e_diag[:, i // 2, i % 2, :], ident[:, :], mm2[:, i:i + 1], None, ALU.mult))
            dve.wait_ge(consts, 3)
            bank = full(D_RANGE)
            link(nc.vector.tensor_scalar(erow[0:NT, 0, 0:ET], bank[0:NT, 2 * P:2 * P + ET], lo_j[0:NT, :], None, ALU.is_ge))
            link(nc.vector.scalar_tensor_tensor(out=erow[0:NT, 1, 0:ET], in0=bank[0:NT, 0:ET], scalar=hi_j[0:NT, :],
                                                in1=erow[0:NT, 0, 0:ET], op0=ALU.is_lt, op1=ALU.mult))
            link(nc.vector.scalar_tensor_tensor(out=erow[0:NT, 2, 0:ET], in0=erow[0:NT, 4, 0:ET], scalar=1.0,
                                                in1=erow[0:NT, 1, 0:ET], op0=ALU.add, op1=ALU.mult))
            link(nc.vector.tensor_scalar(erow[0:NT, 3, 0:ET], erow[0:NT, 4, 0:ET], -1.0, float(ET), ALU.mult, ALU.add))
            link(nc.vector.tensor_tensor(erow[0:NT, 3, 0:ET], erow[0:NT, 3, 0:ET], erow[0:NT, 1, 0:ET], ALU.mult))
            link(nc.vector.tensor_reduce(rng[0:NT, 0:1], erow[0:NT, 3, 0:ET], AX_X, ALU.max))
            link(nc.vector.tensor_reduce(rng[0:NT, 1:2], erow[0:NT, 2, 0:ET], AX_X, ALU.max))
            link(nc.vector.tensor_scalar(rng[0:NT, 2:3], rng[0:NT, 0:1], -1.0, float(ET), ALU.mult, ALU.add))
            link(nc.vector.tensor_scalar(rng[0:NT, 2:3], rng[0:NT, 2:3], float(ET - 1), None, ALU.min))
            link(nc.vector.scalar_tensor_tensor(out=rng[0:NT, 3:4], in0=rng[0:NT, 2:3], scalar=1.0,
                                                in1=rng[0:NT, 1:2], op0=ALU.add, op1=ALU.max))
            link(nc.vector.tensor_copy(rng_i[0:NT, 0:2], rng[0:NT, 2:4]))
            link(nc.vector.scalar_tensor_tensor(out=rng_i[0:NT, 2:3], in0=rng[0:NT, 3:4], scalar=256.0,
                                                in1=rng[0:NT, 2:3], op0=ALU.mult, op1=ALU.add))
            link(nc.vector.tensor_tensor(rng_i[0:NT, 3:4], rng_i[0:NT, 1:2], rng_i[0:NT, 0:1], ALU.subtract))
            link(nc.vector.tensor_scalar(rng_i[0:NT, 3:4], rng_i[0:NT, 3:4], LONG_SHIFT, None, ALU.arith_shift_right))
            link(nc.vector.scalar_tensor_tensor(out=rng_i[0:NT, 2:3], in0=rng_i[0:NT, 3:4], scalar=65536.0,
                                                in1=rng_i[0:NT, 2:3], op0=ALU.mult, op1=ALU.add))
            dve.sem_inc(range_ready, 1)
            bank = full(D_EDGE)
            nc.vector.tensor_copy(srcT[:, :], bank[:, 0:2 * P])
            link(nc.vector.tensor_copy(dstT[:, :], bank[:, 2 * P:4 * P]))
            dve.sem_inc(d_out, 2)

            def range_of(j):
                return [nc.vector.value_load(rng_i[j:j + 1, i:i + 1], min_val=i, max_val=ET - 1 + i) for i in range(2)]
            made = nc.vector.alloc_register("onehots_made")
            nc.vector.reg_mov(made, 0)
            for j in range(NT):
                with dve.Fori(*range_of(j), RING) as i:
                    k = nc.vector.snap(made, min_val=0, max_val=NT * (ET + RING))
                    for b in range(RING):
                        dve.wait_ge(oh_free, k + (b + 1))
                        nc.vector.tensor_scalar(ring[:, b, 0:N], iota16[:, 0:N], srcT[:, bass.ds(i + b, 1)], None,
                                                ALU.is_equal)
                        nc.vector.tensor_scalar(ring[:, b, NT * P:RW], iota16[:, j * P:(j + 1) * P],
                                                dstT[:, bass.ds(i + b, 1)], None, ALU.is_equal).then_inc(oh_ready, 1)
                    nc.vector.reg_add(made, made, RING)
                if j == 0:
                    dve.wait_ge(x_squared, NT)
                    link(nc.vector.tensor_scalar(mv[:, :, 1], x_sq[:, :], 1.0 / D, None, ALU.mult))
                    rstds(0, NT)
                    nc.vector.tensor_tensor(nmr[:, :], nmean[:, :], rstd[:, :], ALU.mult).then_inc(nmr_ready, 1)
                    n_sqrt += 1
                    link(nc.vector.tensor_tensor(ve[:, :], mv[:, :, 1], rstd[:, :], ALU.mult))
                    link(nc.vector.tensor_tensor(ve[:, :], ve[:, :], rstd[:, :], ALU.mult))
                    nc.vector.tensor_scalar(ve[:, :], ve[:, :], EPS, None, ALU.add).then_inc(sq_in, 1)
                if j == 1:
                    dve.wait_ge(sq_out, n_sqrt)
                    nc.vector.reciprocal(rstd2[:, :], sd[:, :]).then_inc(nmr_ready, 1)

            def features(n0, n_hi, scale, bias):
                for c, (a, m) in enumerate(COLS):
                    for b in range(KD):
                        i = c * KD + b
                        dve.wait_ge(a_in, n0 + i + 1)
                        nc.vector.tensor_scalar(f_whole[:, b, a:a + m], ps[:, (n0 + i) % 4, 0:m],
                                                vT[:, scale + b:scale + b + 1], vT[:, bias + b:bias + b + 1],
                                                ALU.mult, ALU.add).then_inc(f_mid, 1)
                    for b in range(1, KD, 2):
                        dve.wait_ge(f_hi, n_hi + c * KD + b + 1)
                        nc.vector.tensor_tensor(f_sp[:, 1, b, a:a + m], f_whole[:, b, a:a + m],
                                                f_sp[:, 0, b, a:a + m].bitcast(F32), ALU.subtract).then_inc(f_odd, 1)
            dve.wait_ge(a_out, A_XMT)
            features(A_XMT, 0, V_G1, V_BE1)
            dve.wait_ge(a_out, A_KQ + KD * NC)

            def squares(xT, sq):
                for b in range(KD):
                    ins = nc.vector.tensor_tensor(sq[:, min(b, 1), :], xT[:, b, :], xT[:, b, :], ALU.mult)
                    link(ins)
                    if b:
                        ins = nc.vector.tensor_tensor(sq[:, 0, :], sq[:, 0, :], sq[:, 1, :], ALU.add)
                        link(ins)
                dve.sem_inc(sq_ready, 1)
            squares(kT, sq_k)
            nc.vector.tensor_scalar(xdn[:, 0:NT], full(D_XDK)[:, 0:NT], -0.5, None, ALU.mult).then_inc(d_out, 1)
            dve.wait_ge(a_out, A_KQ + 2 * KD * NC)
            dve.wait_ge(a_in, A_KP + NT)
            squares(qT, sq_q)
            dve.wait_ge(ld_rows, 6 * 16)
            for t in range(NT):
                r = rows(t)
                nc.vector.tensor_tensor(v[0:r, t, :], full(D_V + t)[0:r, :], bv_b[0:r, :], ALU.add).then_inc(d_out, 1)
            nc.vector.tensor_scalar(xdn[:, NT:2 * NT], full(D_XDQ)[:, 0:NT], -0.5, None, ALU.mult).then_inc(d_out, 1)
            for b in range(1, KD, 2):
                dve.wait_ge(f_hi, KD * NC + b + 1)
                nc.vector.tensor_tensor(f_sp[:, 1, b, :], zT[:, b, :], f_sp[:, 0, b, :].bitcast(F32), ALU.subtract)\
                    .then_inc(f_odd, 1)
            dve.wait_ge(a_out, A_R + KD * NC)
            for t in range(1, NT):
                r = rows(t)
                link(nc.vector.tensor_tensor(kpsum[0:r, :], kp[0:r, 0, :] if t == 1 else kpsum[0:r, :], kp[0:r, t, :],
                                             ALU.add))
            dve.sem_inc(ks_ready, 1)
            nc.vector.tensor_copy(ksum, full(D_KSUM)[:, 0:M]).then_inc(d_out, 1)
            dve.wait_ge(d_out, D_KSUM + 1)
            link(nc.vector.memset(den[:, :], 1.0))
            dve.wait_ge(a_out, A_QP + NT)
            for t in range(NT):
                r = rows(t)
                link(nc.vector.tensor_tensor_reduce(out=qk[0:r, :], in0=qp[0:r, t, :], in1=ksum[0:r, :], scale=1.0,
                                                    scalar=0.0, op0=ALU.mult, op1=ALU.add,
                                                    accum_out=den[0:r, t:t + 1]))
            link(nc.vector.tensor_scalar(den[:, :], den[:, :], float(M) * ATT_EPS, None, ALU.add))
            link(nc.vector.reciprocal(rden[:, :], den[:, :]))
            for t in range(NT):
                r = rows(t)
                link(nc.vector.scalar_tensor_tensor(out=v[0:r, t, :], in0=full(D_Y + t)[0:r, :], scalar=rden[0:r, t:t + 1],
                                                    in1=v[0:r, t, :], op0=ALU.mult, op1=ALU.add))
                dve.sem_inc(d_out, 1)
                nc.vector.tensor_tensor(v[0:r, t, :], v[0:r, t, :], bo_b[0:r, :], ALU.add).then_inc(y_ready, 1)
                dve.wait_ge(y_ready, t + 1)
                stats(t, v)
                if t % TPC == TPC - 1 or t == NT - 1:
                    a = t - t % TPC
                    rstds(a, t + 1)
                    for u in range(a, t + 1):
                        normed(yhat[0:rows(u), u, :], v, u).then_inc(yh_ready, 1)
            features(A_H, KD * NC + KD, V_G2, V_BE2)
            link(nc.vector.memset(logit[:, :, :], 0.0))
            for t in range(NT + 2):
                if t < NT:
                    r = rows(t)
                    bank = full(D_X1[t])
                    dve.wait_ge(xy_ready, t + 1)
                    nc.vector.tensor_tensor(xr[0:r, t, :], bank[0:r, :], xr[0:r, t, :], ALU.add).then_inc(d_out, 1)
                    dve.wait_ge(d_out, D_X1[t] + 1)
                    stats(t, xr)
                    rstds(t, t + 1)
                    if t >= 2:
                        dve.wait_ge(a_in, A_X2T + t - 1)
                        dve.wait_ge(st_x2[t % 2], 16 * (t // 2))
                    normed(x2[0:r, t % 2, :], xr, t).then_inc(xn2_ready, 1)
                if t >= 2:
                    r = rows(t - 2)
                    nc.vector.tensor_tensor(logit[0:r, t - 2, :], full(D_LOG[t - 2])[0:r, 0:NX], rb_b[0:r, :],
                                            ALU.add).then_inc(d_out, 1)
                    dve.wait_ge(d_out, D_LOG[t - 2] + 1)
                    if t == 2:
                        dve.wait_ge(xy_ready, NT)
                    link(nc.vector.max(mx8[:, t - 2, :], logit[:, t - 2, :]))
                    link(nc.vector.max_index(mi8[:, t - 2, :], mx8[:, t - 2, :], logit[:, t - 2, :]))
            dve.sem_inc(slot_done, 1)
            dve.sem_inc(at_out, 1)
            dve.sem_inc(gu_out, 1)
            dve.wait_ge(consts, 9)

            def across(ap, n):
                return ap.unsqueeze(len(ap.shape)).to_broadcast([*ap.shape, n])

            def down_by(ap, *n):
                for _ in n:
                    ap = ap.unsqueeze(1)
                return ap.to_broadcast([P, *n, ap.shape[-1]])
            nc.vector.tensor_tensor(ex2[:, 0, :], mx8[:, :, 1], mx8[:, :, 0], ALU.subtract).then_inc(exp_in, 1)
            nc.vector.tensor_scalar(lo_j[:, :], piota[:, :], float(LAST), None, ALU.is_lt)
            nc.vector.tensor_scalar(behind, piota[:, :], float(LAST), 64.0 * P, ALU.is_ge, ALU.mult)
            link(nc.vector.tensor_scalar(mif[:, :, :], mi8[:, :, :], 1.0, None, ALU.add))
            link(nc.vector.tensor_tensor(oh, down_by(iota1, TOP, NT),
                                         across(mif[:, :, 0:TOP].rearrange("p t k -> p k t"), NX), ALU.is_equal))
            link(nc.vector.tensor_scalar(oh[:, :, NT - 1, :], oh[:, :, NT - 1, :], lo_j[:, 0:1], None, ALU.mult))
            nc.vector.tensor_tensor(msk_b.rearrange("p (t e) -> p t e", t=NT), oh[:, 0, :, :], oh[:, 1, :, :],
                                    ALU.add).then_inc(msk_ready, 1)
            dve.wait_ge(exp_out, 1)
            link(nc.vector.tensor_scalar(den[:, :], ex2[:, 1, :], 1.0, None, ALU.add))
            link(nc.vector.reciprocal(wgt[:, 0, :], den[:, :]))
            nc.vector.tensor_tensor(wgt[:, 1, :], wgt[:, 0, :], ex2[:, 1, :], ALU.mult)
            bank = full(D_RANK)
            link(nc.vector.tensor_scalar(cnt_i, bank[:, NT * NX:(NT + 1) * NX], float(P - 1), None, ALU.add))
            link(nc.vector.tensor_scalar(cnt_i, cnt_i, 7, None, ALU.arith_shift_right))
            link(nc.vector.tensor_copy(cnt, cnt_i))
            link(nc.vector.tensor_tensor_scan(ends[:, 1, :], ones[:, 0:NX], cnt, 0.0, ALU.mult, ALU.add))
            link(nc.vector.tensor_tensor(base, ends[:, 1, :], cnt, ALU.subtract))
            link(nc.vector.tensor_scalar(base, base, float(P), None, ALU.mult))
            link(nc.vector.tensor_tensor(rank, t3(bank[:, 0:NT * NX], NT), down_by(base, NT), ALU.add))
            link(nc.vector.tensor_tensor(oh, oh, rank.unsqueeze(1).to_broadcast([P, TOP, NT, NX]), ALU.mult))
            link(nc.vector.tensor_reduce(posf, oh.rearrange("p k t e -> p (k t) e"), AX_X, ALU.add))
            link(nc.vector.tensor_scalar(t3(posf, TOP)[:, :, NT - 1], t3(posf, TOP)[:, :, NT - 1], behind, None, ALU.add))
            link(nc.vector.tensor_copy(pos_i.rearrange("p k t -> p (k t)"), posf))
            link(nc.vector.tensor_scalar(pa_i, pos_i.rearrange("p k t -> p (k t)"), 7, None, ALU.arith_shift_right))
            nc.vector.tensor_scalar(pb_i, pos_i.rearrange("p k t -> p (k t)"), P - 1, None, ALU.bitwise_and)\
                .then_inc(dch, 1)
            n_link += 1
            link(nc.vector.tensor_copy(pa_f, pa_i))
            link(nc.vector.tensor_copy(pb_f, pb_i))
            link(nc.vector.tensor_tensor(slot_1, down_by(iota_s, KT), across(pa_f, SLOTS), ALU.is_equal))
            nc.vector.tensor_tensor(slot_a[:, :, 0, :], slot_1, across(tile_no, SLOTS), ALU.mult).then_inc(slot_ready, 1)
            nc.vector.tensor_scalar(slot_a[:, :, 1, :], slot_1, piota[:, 0:1], None, ALU.mult).then_inc(slot_ready, 1)
            for k in range(TOP):
                nc.vector.tensor_tensor(slot_b[:, k * NT:(k + 1) * NT, :], down_by(iota_c, NT),
                                        across(pb_f[:, k * NT:(k + 1) * NT], P), ALU.is_equal).then_inc(slot_ready, 1)
            link(nc.vector.tensor_scalar(has, cnt, 1.0, None, ALU.min))
            link(nc.vector.memset(has[:, 0:1], 1.0))
            link(nc.vector.tensor_tensor_scan(ends[:, 0, :], ones[:, 0:NX], has, 0.0, ALU.mult, ALU.add))
            link(nc.vector.tensor_scalar(last_f, ends[:, :, NX - 1], -1.0, None, ALU.add))
            nc.vector.tensor_copy(last_i[:, :], last_f)
            bank = full(D_SLOT)
            link(nc.vector.tensor_copy(row_f, bank[:, SLOTS:2 * SLOTS]))
            link(nc.vector.scalar_tensor_tensor(out=idx_i[:, :], in0=bank[:, 0:SLOTS], scalar=float(P),
                                                in1=row_f, op0=ALU.mult, op1=ALU.add))
            dve.sem_inc(slots_known, 1)
            link(nc.vector.tensor_tensor(cmp_s, across(iota_s, NX), down_by(ends[:, 1, :], SLOTS), ALU.is_ge))
            link(nc.vector.tensor_tensor(cmp_s, cmp_s, down_by(has, SLOTS), ALU.mult))
            link(nc.vector.tensor_reduce(place_f, cmp_s, AX_X, ALU.add))
            link(nc.vector.tensor_scalar(place_f, place_f, last_f[:, 0:1], None, ALU.min))
            nc.vector.tensor_copy(place_i[:, :], place_f)
            link(nc.vector.memset(change_i[:, :], 0))
            link(nc.vector.tensor_tensor(change_i[:, 0:SLOTS - 1], place_f[:, 1:SLOTS], place_f[:, 0:SLOTS - 1],
                                         ALU.subtract))
            link(nc.vector.scalar_tensor_tensor(out=num_end[:, 0, :], in0=iota1, scalar=-1.0, in1=has,
                                                op0=ALU.add, op1=ALU.mult))
            link(nc.vector.tensor_tensor(num_end[:, 1, :], ends[:, 1, :], has, ALU.mult))
            link(nc.vector.tensor_tensor(cmp_u, across(iota1, NX), down_by(ends[:, 0, :], NX), ALU.is_equal))
            for i in range(2):
                link(nc.vector.tensor_tensor(num_end_of[:, i, :, :], cmp_u, down_by(num_end[:, i, :], NX), ALU.mult))
            link(nc.vector.tensor_reduce(used_f, num_end_of, AX_X, ALU.add))
            link(nc.vector.memset(used_end_i[:, 0:1], 0))
            link(nc.vector.memset(used_i[:, NX:NX + 1], 0))
            nc.vector.tensor_copy(used_i[:, 0:NX], used_f[:, 0, :])
            link(nc.vector.tensor_copy(used_end_i[:, 1:NX + 1], used_f[:, 1, :]))
            dve.sem_inc(route_ready, 1)
            link(nc.vector.tensor_tensor(low[:, 0, :], posf[:, 0:NT], posf[:, NT:KT], ALU.is_lt))
            link(nc.vector.tensor_scalar(low[:, 1, :], low[:, 0, :], -1.0, 1.0, ALU.mult, ALU.add))
            for k, op in enumerate((ALU.min, ALU.max)):
                nc.vector.tensor_tensor(pos_i[:, k, :], posf[:, 0:NT], posf[:, NT:KT], op).then_inc(pos_sorted, 1)
                link(nc.vector.tensor_tensor(w_of[:, 0, :], wgt[:, 0, :], low[:, k, :], ALU.mult))
                link(nc.vector.tensor_tensor(w_of[:, 1, :], wgt[:, 1, :], low[:, 1 - k, :], ALU.mult))
                link(nc.vector.tensor_tensor(wgt2[:, k, :], w_of[:, 0, :], w_of[:, 1, :], ALU.add))

            gate = ps[:, 0:2, :].rearrange("p a b -> p (a b)")
            up = ps[:, 2:4, :].rearrange("p a b -> p (a b)")

            def place_of(s):
                return nc.vector.snap(nc.vector.value_load(place_i[0:1, bass.ds(s, 1)] if not isinstance(s, int) else
                                                           place_i[0:1, s:s + 1], min_val=0, max_val=NX - 1))

            def gate_up_lo(i, c):
                dve.wait_ge(gu_hi, i * GC + (c + 1))
                nc.vector.tensor_tensor(w_sp[:, c, 1, :], raw_gu[c % 2], w_sp[:, c, 0, :].bitcast(F32), ALU.subtract)\
                    .then_inc(gu_split, 1)

            def down_lo(i, h):
                dve.wait_ge(d_hi, i * DC + (h + 1))
                nc.vector.tensor_tensor(w_sp[:, GC + h, 1, :], raw_d[h], w_sp[:, GC + h, 0, :].bitcast(F32),
                                        ALU.subtract).then_inc(d_split, 1)

            def xsT_lo(n):
                dve.wait_ge(xt_hi, n)
                nc.vector.tensor_tensor(xT_sp[:, 1, :], ps[:, 7, :], xT_sp[:, 0, :].bitcast(F32), ALU.subtract)\
                    .then_inc(xt_out, 1)

            def aT_lo(n):
                for h in range(2):
                    dve.wait_ge(at_hi, 2 * n + h)
                    nc.vector.tensor_tensor(aT_sp[:, 1, h * BANK:(h + 1) * BANK], ps[:, 4 + h, :],
                                            aT_sp[:, 0, h * BANK:(h + 1) * BANK].bitcast(F32), ALU.subtract)\
                        .then_inc(at_out, 1)

            def activate(s, prev, nxt):
                place = place_of(s)
                if nxt:
                    changes = nc.vector.value_load(change_i[0:1, bass.ds(s, 1)] if prev else change_i[0:1, 0:1],
                                                   min_val=0, max_val=1)
                    with dve.If(changes):
                        for c in range(2):
                            dve.wait_ge(gu_full, s * GC + (c + 1))
                            gate_up_lo(place + 1, c)
                bias = nc.vector.snap((place % 2) * BIAS_STEP)
                dve.wait_ge(b_ld, place * 32 + 32)
                dve.wait_ge(gu_full, s * GC + 2)
                nc.vector.tensor_tensor(g_s, gate, wa[:, bass.ds(bias + BIAS0, I)], ALU.add).then_inc(g_out, 1)
                if prev:
                    aT_lo(s)
                dve.wait_ge(gu_full, s * GC + 4)
                if prev:
                    dve.wait_ge(a_ready, s)
                nc.vector.scalar_tensor_tensor(out=u_s, in0=up, scalar=1.0, in1=wa[:, bass.ds(bias + BIAS0 + I, I)],
                                               op0=ALU.add, op1=ALU.add).then_inc(gu_out, 1)
                if nxt:
                    xsT_lo(s + 2)
                dve.wait_ge(sig_out, s + 1)
                nc.vector.tensor_tensor(sig_s, g_s, sig_s, ALU.mult).then_inc(gu_out, 1)
                dve.wait_ge(gu_out, 2 * s + 3)
                if prev:
                    dve.wait_ge(at_full, 2 * s + 1)
                nc.vector.tensor_tensor(a_s, u_s, sig_s, ALU.mult).then_inc(a_ready, 1)
                if nxt:
                    with dve.If(changes):
                        for c in range(2, GC):
                            gate_up_lo(place + 1, c)

            def finish(n):
                h = nc.vector.snap(place_of(n - 1) % 2)
                dve.wait_ge(dn_full, n)
                dve.wait_ge(y_st, 16 * n)
                nc.vector.tensor_tensor(r1[:, bass.ds(((n - 1) % 2) * D, D)], ps[:, 6, :],
                                        bd_b[:, bass.ds(h * D, D)], ALU.add).then_inc(slot_done, 1)

            def change_down(s):
                changed = nc.vector.value_load(change_i[0:1, bass.ds(s - 1, 1)], min_val=0, max_val=1)
                i = place_of(s)
                with dve.If(changed):
                    for h in range(DC):
                        down_lo(i, h)
            dve.wait_ge(d_split, 2 * DC - 1)
            down_lo(0, DC - 1)
            with dve.If(nc.vector.value_load(place_i[0:1, 0:1], min_val=0, max_val=1)):
                for c in range(GC):
                    gate_up_lo(1, c)
                for h in range(DC):
                    down_lo(1, h)
            xsT_lo(1)
            last = nc.vector.value_load(last_i[0:1, 1:2], min_val=SLOTS_MIN - 1, max_val=SLOTS - 1)
            activate(0, False, True)
            with dve.Fori(1, last) as s:
                activate(s, True, True)
                finish(s)
                change_down(s)
            activate(last, True, False)
            finish(last)
            change_down(last)
            aT_lo(last + 1)
            dve.wait_ge(lower_in, 16 * EARLY)
            for t in range(EARLY):
                r = rows(t)
                link(nc.vector.scalar_tensor_tensor(out=xr[0:r, t, :], in0=LOWER[t][0:r, :], scalar=wgt2[0:r, 0, t:t + 1],
                                                    in1=xr[0:r, t, :], op0=ALU.mult, op1=ALU.add))
            finish(last + 1)
            for t in range(NT):
                r, c = rows(t), t % CB
                dve.wait_ge(cg[c], 16 * sum(1 if u < EARLY else TOP for u in range(c, t + 1, CB)))
                if t >= CB:
                    dve.wait_ge(o_st[c], 16 * (t // CB))
                if t >= EARLY:
                    link(nc.vector.scalar_tensor_tensor(out=xr[0:r, t, :], in0=yg[0:r, c, 0, :],
                                                        scalar=wgt2[0:r, 0, t:t + 1], in1=xr[0:r, t, :],
                                                        op0=ALU.mult, op1=ALU.add))
                nc.vector.scalar_tensor_tensor(out=ob[0:r, c, :], in0=yg[0:r, c, 1, :], scalar=wgt2[0:r, 1, t:t + 1],
                                               in1=xr[0:r, t, :], op0=ALU.mult, op1=ALU.add).then_inc(o_ready, 1)

        @block.tensor
        def _(pe):
            mm, tr = nc.tensor.matmul, nc.tensor.transpose

            def a_tile(n):
                if n >= 4:
                    pe.wait_ge(a_out, n - 3)
                return ps[:, n % 4, :]

            def d_tile(n):
                if n >= 4:
                    pe.wait_ge(d_out, n - 3)
                return ps[:, 4 + n % 4, :]

            def to_cols(n0, rows_of, ready, nb):
                for b in range(nb):
                    for c, (a, m) in enumerate(COLS):
                        bank = a_tile(n0 + b * NC + c)
                        for t in range(TPC * c, min(TPC * c + TPC, NT)):
                            ready(t)
                            r = rows(t)
                            q = tr(bank[:, (t - TPC * c) * P:(t - TPC * c) * P + r], rows_of[0:r, t, b * P:(b + 1) * P],
                                   ident[0:r, 0:r])
                        q.then_inc(a_in, 1)

            def layer(n0, wt, xT, nk):
                for b in range(KD):
                    for c, (a, m) in enumerate(COLS):
                        bank = a_tile(n0 + b * NC + c)
                        for k in range(nk):
                            q = mm(bank[:, 0:m], wt[:, k, b * P:(b + 1) * P], xT[:, k, a:a + m],
                                   start=(k == 0), stop=(k == nk - 1))
                        q.then_inc(a_in, 1)

            PARTS = ((0, 0), (0, 1), (1, 0))

            def split_layer(n0, n_slice, ready, by_c=False):
                for b in range(KD):
                    pe.wait_ge(sl_ready, n_slice + b + 1)
                    wt = slice_of(n_slice + b)
                    for c, (a, m) in enumerate(COLS):
                        bank = a_tile(n0 + b * NC + c)
                        if b == 0:
                            for f in (f_even, f_odd):
                                pe.wait_ge(f, (ready + (c * KD if by_c else 0) + KD) // 2)
                        for k in range(KD):
                            for i, (u, w) in enumerate(PARTS):
                                q = mm(bank[:, 0:m], wt[:, u, k, :], f_sp[:, w, k, a:a + m],
                                       start=(k == 0 and i == 0), stop=(k == KD - 1 and i == 2))
                        q.then_inc(a_in, 1)

            def to_features(n0, n, rows_of, ready):
                for c, (a, m) in enumerate(COLS):
                    for b in range(KD):
                        i = c * KD + b
                        if i >= 4:
                            pe.wait_ge(f_mid, n + i - 3)
                        else:
                            pe.wait_ge(a_out, n0 + i - 3)
                        bank = ps[:, (n0 + i) % 4, :]
                        for t in range(TPC * c, min(TPC * c + TPC, NT)):
                            ready(t)
                            r = rows(t)
                            q = tr(bank[:, (t - TPC * c) * P:(t - TPC * c) * P + r], rows_of[0:r, t, b * P:(b + 1) * P],
                                   ident[0:r, 0:r])
                        q.then_inc(a_in, 1)
                pe.wait_ge(f_mid, n + KD * NC)
                pe.sem_inc(a_out, KD * NC)
            pe.wait_ge(consts, 1)
            pe.wait_ge(dch, 4)
            bank = d_tile(D_EDGE)
            for i in range(4):
                q = tr(bank[:, i * P:(i + 1) * P], e_f[:, i // 2, i % 2, :], ident[:, :])
            q.then_inc(d_in, 1)
            pe.wait_ge(dch, 12)
            pe.wait_ge(consts, 2)
            bank = d_tile(D_RANGE)
            for i in range(4):
                q = mm(bank[0:NT, i * P:(i + 1) * P], ones[:, 0:NT], e_diag[:, i // 2, i % 2, :], start=True, stop=True)
            q.then_inc(d_in, 1)
            pe.wait_ge(consts, 5)
            pe.wait_ge(range_ready, 1)
            pe.wait_ge(d_out, D_RANGE + 1)
            pe.sem_inc(oh_free, RING)

            def range_of(j):
                word = nc.tensor.snap(nc.tensor.value_load(rng_i[j:j + 1, 2:3], min_val=256,
                                                           max_val=((ET >> LONG_SHIFT) + 1 << 16) - 1))
                nc.tensor.reg_add(long_ranges, long_ranges, nc.tensor.snap(word >> 16))
                return (nc.tensor.snap(word % 256, min_val=0, max_val=ET - 1),
                        nc.tensor.snap((word >> 8) % 256, min_val=1, max_val=ET))
            long_ranges = nc.tensor.alloc_register("long_ranges")
            nc.tensor.reg_mov(long_ranges, 0)
            ahead = range_of(0)
            used = nc.tensor.alloc_register("onehots_used")
            nc.tensor.reg_mov(used, 0)

            def turn_counts(j):
                for g in range(NC):
                    n = NC * j + g
                    pe.wait_ge(c_out, NC * j + g + 1)
                    if n >= 2:
                        before = n - 2
                        pe.wait_ge(ct_out, (NC + 1) * (before // NC) + (before % NC + 1 if before % NC < NC - 1 else NC + 1))
                    bank = ps[:, 6 + n % 2, :]
                    for i in range(TPC * g, min(TPC * g + TPC, NT)):
                        r = rows(i)
                        q = tr(bank[0:r, (i - TPC * g) * P:(i - TPC * g + 1) * P], c_stage[:, i * P:i * P + r], ident[:, :])
                    q.then_inc(ct_full, 1)
            for j in range(NT):
                if j >= 2:
                    pe.wait_ge(c_out, NC * (j - 1))
                banks = [ps[:, 3 * (j % 2) + c, 0:m] for c, (a, m) in enumerate(COLS)]
                for c, (a, m) in enumerate(COLS):
                    o = (NT - 1 - j) * P + a
                    mm(banks[c], ident_b[:, :], e_id[:, o:o + m], start=True, stop=False, skip_group_check=True)
                edge_range, ahead = ahead, range_of(j + 1) if j < NT - 1 else None
                with pe.Fori(*edge_range, RING) as i:
                    k = nc.tensor.snap(used, min_val=0, max_val=NT * (ET + RING))
                    for b in range(RING):
                        pe.wait_ge(oh_ready, k + (b + 1))
                        for c, (a, m) in enumerate(COLS):
                            q = mm(banks[c], ring[:, b, NT * P:RW], ring[:, b, a:a + m],
                                   start=False, stop=True, skip_group_check=True)
                        q.then_inc(oh_free, 1)
                    nc.tensor.reg_add(used, used, RING)
                pe.wait_ge(oh_free, nc.tensor.snap(used, min_val=1, max_val=NT * (ET + RING)) + RING)
                pe.sem_inc(c_full, 1)
                if j >= 1:
                    turn_counts(j - 1)
            turn_counts(NT - 1)

            pe.wait_ge(ct_out, (NC + 1) * NT)
            pe.wait_ge(ld_vec, 7 * 16)
            tr(a_tile(A_VEC)[:, 0:8 * KD], vrow[:, :], ident[0:8 * KD, 0:8 * KD]).then_inc(a_in, 1)
            pe.wait_ge(ld_w, 16)
            for m in range(KM):
                bank = a_tile(A_WT + m)
                for k in range(KD):
                    q = tr(bank[:, k * P:(k + 1) * P], w_raw[:, m, k * P:(k + 1) * P], ident[:, :])
                q.then_inc(a_in, 1)
            pe.wait_ge(xl_ready, NT)

            def neighbours(first, second, counts):
                for b in range(KD):
                    for c, (a, m) in enumerate(COLS):
                        bank = a_tile(A_Z + b * NC + c)
                        for i in range(NT):
                            r = rows(i)
                            for part in (first, second):
                                q = mm(bank[:, 0:m], part[0:r, i, b * P:(b + 1) * P], counts[0:r, i, a:a + m],
                                       start=(i == 0 and part is first), stop=(i == NT - 1 and part is second))
                        q.then_inc(a_in, 1)
            with pe.If_eq(long_ranges, 0):
                neighbours(xh, xl, cT_r)
            with pe.If_ne(long_ranges, 0):
                neighbours(xh.bitcast(F32), xl.bitcast(F32), cT)
            to_features(A_XMT, 0, xm, lambda t: pe.wait_ge(xm_ready, t + 1))
            split_layer(A_KQ, S_K, 0, True)
            split_layer(A_KQ + KD * NC, S_Q, KD * (NC - 1))

            def squares(n, count, sq):
                pe.wait_ge(sq_ready, count)
                bank = d_tile(n)
                for t in range(NT):
                    r = rows(t)
                    q = mm(bank[0:r, t:t + 1], sq[:, 0, t * P:t * P + r], ones[:, 0:1], start=True, stop=True)
                q.then_inc(d_in, 1)

            def random_features(n0, xT):
                for t in range(NT):
                    r = rows(t)
                    bank = a_tile(n0 + t)
                    for k in range(KD):
                        q = mm(bank[0:r, 0:M], xT[:, k, t * P:t * P + r], wT[:, k, :], start=(k == 0), stop=(k == KD - 1))
                    q.then_inc(a_in, 1)
            squares(D_XDK, 1, sq_k)
            random_features(A_KP, kT)
            pe.wait_ge(wv_ready, KD)
            for t in range(NT):
                r = rows(t)
                bank = d_tile(D_V + t)
                for k in range(KD):
                    for i, (u, w) in enumerate(PARTS):
                        q = mm(bank[0:r, :], f_sp[:, u, k, t * P:t * P + r], wv_sp[:, k, w * D:(w + 1) * D],
                               start=(k == 0 and i == 0), stop=(k == KD - 1 and i == 2))
                q.then_inc(d_in, 1)
            squares(D_XDQ, 2, sq_q)
            random_features(A_QP, qT)
            to_cols(A_QPT, qp, lambda t: pe.wait_ge(a_out, A_QP + t + 1), KM)
            split_layer(A_R, S_R, KD * NC)
            pe.wait_ge(d_out, D_V + NT)
            for b in range(KM):
                bank = a_tile(A_KPTV + b)
                for t in range(NT):
                    r = rows(t)
                    q = mm(bank, kp[0:r, t, b * P:(b + 1) * P], v[0:r, t, :], start=(t == 0), stop=(t == NT - 1))
                q.then_inc(a_in, 1)
            pe.wait_ge(ks_ready, 1)
            mm(d_tile(D_KSUM)[:, 0:M], ones[:, :], kpsum, start=True, stop=True).then_inc(d_in, 1)
            pe.wait_ge(a_out, A_KPTV + KM)
            layer(A_ATT, kptvT, qpT, KM)
            pe.wait_ge(ld_ow1w2, 3 * 16)
            pe.wait_ge(a_out, A_ATT + KD * NC)
            for t in range(NT):
                r = rows(t)
                bank = d_tile(D_Y + t)
                for k in range(KD):
                    q = mm(bank[0:r, :], attT[:, k, t * P:t * P + r], wo_s[:, k, :], start=(k == 0), stop=(k == KD - 1))
                q.then_inc(d_in, 1)
            to_features(A_H, KD * NC, yhat, lambda t: pe.wait_ge(yh_ready, t + 1))
            split_layer(A_G, S_G, KD * NC + KD, True)
            pe.wait_ge(a_out, A_G + KD * NC)
            pe.wait_ge(ld_gw2, 16)
            for t in range(NT + 2):
                if t < NT:
                    r = rows(t)
                    bank = d_tile(D_X1[t])
                    for k in range(KD):
                        mm(bank[0:r, :], gT[:, k, t * P:t * P + r], w2_s[:, k, :], start=(k == 0), stop=False)
                    for k in range(KD):
                        q = mm(bank[0:r, :], rT[:, k, t * P:t * P + r], gw2_s[:, k, :], start=False, stop=(k == KD - 1))
                    q.then_inc(d_in, 1)
                if 1 <= t <= NT:
                    u = t - 1
                    r = rows(u)
                    pe.wait_ge(xn2_ready, u + 1)
                    bank = a_tile(A_X2T + u)
                    for k in range(KD):
                        q = tr(bank[:, k * P:k * P + r], x2[0:r, u % 2, k * P:(k + 1) * P], ident[0:r, 0:r])
                    q.then_inc(a_in, 1)
                if t >= 2:
                    u = t - 2
                    r = rows(u)
                    pe.wait_ge(a_out, A_X2T + u + 1)
                    bank = d_tile(D_LOG[u])
                    for k in range(KD):
                        q = mm(bank[0:r, 0:NX], x2T[:, u % 2, k, 0:r], rw_s[:, k, :], start=(k == 0), stop=(k == KD - 1))
                    q.then_inc(d_in, 1)
            pe.wait_ge(msk_ready, 1)
            bank = d_tile(D_RANK)
            for i in range(NT):
                mm(bank[:, i * NX:NT * NX], ones_b[:, :] if i else tri_b[:, :], msk_b[:, 0:(NT - i) * NX],
                   start=(i == 0), stop=False, skip_group_check=True)
            for i in range(NT):
                q = mm(bank[:, NT * NX:(NT + 1) * NX], ones_b[:, :], msk_b[:, i * NX:(i + 1) * NX],
                       start=(i == 0), stop=(i == NT - 1), skip_group_check=True)
            q.then_inc(d_in, 1)
            bank = d_tile(D_SLOT)
            for n in range(KT):
                if n % NT == 0:
                    pe.wait_ge(slot_ready, 3 + n // NT)
                q = mm(bank[:, 0:2 * SLOTS], slot_b[:, n, :], slot_a[:, n, :, :].rearrange("p w s -> p (w s)"),
                       start=(n == 0), stop=(n == KT - 1))
            q.then_inc(d_in, 1)

            pe.wait_ge(route_ready, 1)

            def place_of(s):
                return nc.tensor.snap(nc.tensor.value_load(place_i[0:1, bass.ds(s, 1)] if not isinstance(s, int) else
                                                           place_i[0:1, s:s + 1], min_val=0, max_val=NX - 1))

            def turn_xs(n):
                pe.wait_ge(gath, 16 * n)
                for k in range(KD):
                    q = tr(ps[:, 7, k * P:(k + 1) * P], xs[:, k * P:(k + 1) * P], ident[:, :])
                q.then_inc(xt_full, 1)

            def split_product(bank, rows_sp, at, c, first, last):
                for k in range(KD):
                    for n, (a, b) in enumerate(((0, 0), (0, 1), (1, 0))):
                        q = mm(bank, rows_sp[:, a, at + k * P:at + (k + 1) * P],
                               w_sp[:, c, b, k * BANK:(k + 1) * BANK],
                               start=(first and k == 0 and n == 0), stop=(last and k == KD - 1 and n == 2))
                return q

            def gate_up(s, place, chunks, first=False):
                for c in chunks:
                    if c == 0:
                        pe.wait_ge(xt_out, s + 1)
                    if c % 2 == 0 and not first:
                        pe.wait_ge(*((g_out, s) if c == 0 else (gu_out, 2 * s)))
                    pe.wait_ge(gu_split, place * GC + (c + 2))
                    split_product(ps[:, c, :], xT_sp, 0, c, True, True).then_inc(gu_full, 1)

            def turn_act(n):
                pe.wait_ge(a_ready, n)
                for h in range(2):
                    for k in range(4):
                        i = 4 * h + k
                        q = tr(ps[:, 4 + h, k * P:(k + 1) * P], a_s[:, i * P:(i + 1) * P], ident[:, :])
                    q.then_inc(at_full, 1)

            def down(n):
                place = place_of(n - 1)
                pe.wait_ge(slot_done, n)
                for h in range(DC):
                    pe.wait_ge(d_split, place * DC + (DC + h + 1))
                    pe.wait_ge(at_out, 2 * n + h)
                    q = split_product(ps[:, 6, :], aT_sp, h * BANK, GC + h, h == 0, h == DC - 1)
                q.then_inc(dn_full, 1)
            pe.sem_inc(at_full, 1)
            turn_xs(1)
            gate_up(0, place_of(0), range(GC), True)
            turn_xs(2)
            last = nc.tensor.value_load(last_i[0:1, 1:2], min_val=SLOTS_MIN - 1, max_val=SLOTS - 1)
            with pe.Fori(1, last) as s:
                place = place_of(s)
                gate_up(s, place, range(GC - 1))
                turn_act(s)
                turn_xs(s + 2)
                gate_up(s, place, [GC - 1])
                down(s)
            gate_up(last, place_of(last), range(GC))
            turn_act(last)
            down(last)
            turn_act(last + 1)
            down(last + 1)


_INS = ['x', 'src', 'dst', 'L0_gnn_W1', 'L0_gnn_b1', 'L0_gnn_W2', 'L0_gnn_b2', 'L0_mix_w', 'L0_mix_Wkqv',
        'L0_mix_bkqv', 'L0_mix_Wo', 'L0_mix_bo', 'L0_mix_W1', 'L0_mix_b1', 'L0_mix_W2', 'L0_mix_b2', 'L0_mix_g1',
        'L0_mix_be1', 'L0_mix_g2', 'L0_mix_be2', 'L0_ffn_router_w', 'L0_ffn_router_b', 'L0_ffn_gate_up_proj',
        'L0_ffn_gate_up_proj_bias', 'L0_ffn_down_proj', 'L0_ffn_down_proj_bias']
_OUTS = [((1250, 512), 'float32')]


def kernel(**inputs):
    import numpy as _np
    import concourse.bacc as _bacc
    from concourse import mybir as _mybir
    from concourse.bass_utils import run_bass_kernel_spmd as _run

    nc = _bacc.Bacc("TRN2", target_bir_lowering=False, num_devices=1)
    arrays, args = {}, []
    for name in _INS:
        a = _np.ascontiguousarray(inputs[name])
        arrays[f"in_{name}_dram"] = a
        args.append(nc.dram_tensor(f"in_{name}_dram", a.shape, _mybir.dt.from_np(a.dtype), kind="ExternalInput").ap())
    for i, (shape, dtype) in enumerate(_OUTS):
        dt = _mybir.dt.from_np(_np.dtype(dtype))
        args.append(nc.dram_tensor(f"out_{i}_dram", shape, dt, kind="ExternalOutput").ap())
    bass_gps_gnn_performer_moe(nc, *args)
    r = _run(nc, [arrays], core_ids=[0])
    got = tuple(r.results[0][f"out_{i}_dram"] for i in range(len(_OUTS)))
    return got[0]
```
